# Optimizing a Trainium2 kernel written in Bass

```python
import numpy as np
import jax
import jax.numpy as jnp

def _softmax(x, axis=-1):
    return jax.nn.softmax(x, axis=axis)

def _gelu(x):
    return jax.nn.gelu(x, approximate=True)

def _silu(x):
    return jax.nn.silu(x)

def _sigmoid(x):
    return jax.nn.sigmoid(x)

def _layernorm(x, axis=-1, eps=1e-05):
    m = jnp.mean(x, axis=axis, keepdims=True)
    v = jnp.var(x, axis=axis, keepdims=True)
    return (x - m) / jnp.sqrt(v + eps)

def _scatter_add(tgt, idx, src, axis=0):
    return tgt.at[idx].add(src)

def _segment_sum(src, seg, n):
    return jax.ops.segment_sum(src, seg, n)
kernel_name = 'mk_decoder_preln_d2_seqx_r8_ae4f0e'

def setup_inputs(seed: int=0):
    np.random.seed(seed)
    _w = jnp.asarray

    def _rec_inputs():
        import jax
        import jax.numpy as jnp
        _rk = jax.random.key(seed)
        x = -0.0002928 + 1 * jax.random.normal(jax.random.fold_in(_rk, 1), (8, 256, 128), jnp.float32)
        _lenS = 256 - jax.random.randint(jax.random.fold_in(_rk, 7), (8,), 0, max(1, 256 // 4) + 1, jnp.int32)
        _lenS2 = 256 - jax.random.randint(jax.random.fold_in(_rk, 8), (8,), 0, max(1, 256 // 4) + 1, jnp.int32)
        _ctx_1024P = jax.random.normal(jax.random.fold_in(_rk, 11), (8, 16, 128), jnp.float32)
        _ctx_1024c = jax.random.dirichlet(jax.random.fold_in(_rk, 511), 0.3 * jnp.ones((16,), jnp.float32), (8, 256))
        _ctx_1024t = jnp.einsum('bsk,bkd->bsd', _ctx_1024c, _ctx_1024P)
        _ctx_1024t = _ctx_1024t * jax.lax.rsqrt(jnp.mean(jnp.square(_ctx_1024t)) + 1e-12) * 0.953939
        ctx_1024 = -1.39393e-06 + 0.999914 * (_ctx_1024t + 0.3 * jax.random.normal(jax.random.fold_in(_rk, 611), (8, 256, 128), jnp.float32))
        return (x, ctx_1024)
    x, ctx_1024 = _rec_inputs()

    def _L0_attn_setup():
        import jax, jax.numpy as jnp
        import numpy as np
        import math
        D_MODEL = 128
        N_HEADS = 16
        D_HEAD = D_MODEL // N_HEADS
        MAX_SEQ_LEN = 256
        BASE = 10000.0

        def _rope_tables(L):
            pos = jnp.arange(L, dtype=jnp.float32)[:, None]
            freqs = jnp.exp(-math.log(BASE) * jnp.arange(0, D_HEAD, 2, dtype=jnp.float32) / D_HEAD)
            angles = pos * freqs
            return (jnp.sin(angles), jnp.cos(angles))

        def _apply_rope(x, sin, cos):
            s = sin[None, :, None, :]
            c = cos[None, :, None, :]
            x_even, x_odd = (x[..., ::2], x[..., 1::2])
            rot_even = x_even * c - x_odd * s
            rot_odd = x_even * s + x_odd * c
            return jnp.stack([rot_even, rot_odd], axis=-1).reshape(x.shape)
        key = jax.random.key(seed)
        k0, k1, k2, k3, k4 = jax.random.split(key, 5)
        B, L = (2, 256)
        scale = 1.0 / math.sqrt(D_MODEL)
        return {'x': jax.random.normal(k0, (B, L, D_MODEL), dtype=jnp.float32), 'W_q': jax.random.normal(k1, (D_MODEL, D_MODEL), dtype=jnp.float32) * scale, 'W_k': jax.random.normal(k2, (D_MODEL, D_MODEL), dtype=jnp.float32) * scale, 'W_v': jax.random.normal(k3, (D_MODEL, D_MODEL), dtype=jnp.float32) * scale, 'W_o': jax.random.normal(k4, (D_MODEL, D_MODEL), dtype=jnp.float32) * scale}
    _L0_attn_all = _L0_attn_setup()
    _L0_attn_in = {k: v for k, v in _L0_attn_all.items() if k in ('W_q', 'W_k', 'W_v', 'W_o')}
    del _L0_attn_all

    def _L0_xattn_setup():
        import jax, jax.numpy as jnp
        import numpy as np
        D_MODEL = 128
        NHEAD = 16
        NUM_KV = 4
        D_K = D_MODEL // NHEAD
        GROUP = NHEAD // NUM_KV
        ROPE_BASE = 10000.0

        def _rope(x, seq_len):
            half = D_K // 2
            inv_freq = 1.0 / ROPE_BASE ** (jnp.arange(0, D_K, 2, dtype=jnp.float32) / D_K)
            t = jnp.arange(seq_len, dtype=jnp.float32)
            freqs = jnp.outer(t, inv_freq)
            emb = jnp.concatenate([freqs, freqs], axis=-1)
            cos, sin = (jnp.cos(emb), jnp.sin(emb))
            x1, x2 = (x[..., :half], x[..., half:])
            rot = jnp.concatenate([-x2, x1], axis=-1)
            return x * cos + rot * sin
        key = jax.random.key(seed)
        ks = jax.random.split(key, 12)
        B, S = (2, 256)
        s_in = 1.0 / np.sqrt(D_MODEL)
        inp = {'query': jax.random.normal(ks[0], (B, S, D_MODEL), jnp.float32), 'key': jax.random.normal(ks[1], (B, S, D_MODEL), jnp.float32), 'value': jax.random.normal(ks[2], (B, S, D_MODEL), jnp.float32), 'Wq': jax.random.normal(ks[3], (D_MODEL, D_MODEL), jnp.float32) * s_in, 'bq': jnp.zeros((D_MODEL,), jnp.float32), 'Wk': jax.random.normal(ks[4], (NUM_KV * D_K, D_MODEL), jnp.float32) * s_in, 'bk': jnp.zeros((NUM_KV * D_K,), jnp.float32), 'Wv': jax.random.normal(ks[5], (NUM_KV * D_K, D_MODEL), jnp.float32) * s_in, 'bv': jnp.zeros((NUM_KV * D_K,), jnp.float32), 'Wo': jax.random.normal(ks[6], (D_MODEL, D_MODEL), jnp.float32) * s_in, 'bo': jnp.zeros((D_MODEL,), jnp.float32)}
        return inp
    _L0_xattn_all = _L0_xattn_setup()
    _L0_xattn_in = {k: v for k, v in _L0_xattn_all.items() if k in ('Wq', 'bq', 'Wk', 'bk', 'Wv', 'bv', 'Wo', 'bo')}
    del _L0_xattn_all

    def _L0_ffn_setup():
        import jax, jax.numpy as jnp
        import numpy as np
        DIM = 128
        DEPTH = 7
        PAR = 8
        N_NODES = 2 ** (DEPTH + 1) - 1
        WIDTH = PAR * N_NODES
        key = jax.random.key(seed)
        k1, k2, k3, k4 = jax.random.split(key, 4)
        init_k = float(np.sqrt(1.0 / DIM))
        init_k2 = float(np.sqrt(1.0 / ((DEPTH + 1) * PAR)))
        oldx = jax.random.normal(k1, (4, 256, DIM), dtype=jnp.float32)
        W_in = jax.random.uniform(k2, (WIDTH, DIM), jnp.float32, -init_k, init_k)
        b_in = jax.random.uniform(k3, (WIDTH,), jnp.float32, -init_k, init_k)
        W_out = jax.random.uniform(k4, (DIM, WIDTH), jnp.float32, -init_k2, init_k2)
        return {'oldx': oldx, 'W_in': W_in, 'b_in': b_in, 'W_out': W_out}
    _L0_ffn_all = _L0_ffn_setup()
    _L0_ffn_in = {k: v for k, v in _L0_ffn_all.items() if k in ('W_in', 'b_in', 'W_out')}
    del _L0_ffn_all

    def _L1_attn_setup():
        import jax, jax.numpy as jnp
        import numpy as np
        B, T, D = (2, 256, 128)
        H = 16
        DH = D // H
        TOPK = 32
        key = jax.random.key(seed)
        ks = jax.random.split(key, 5)
        s = 1.0 / np.sqrt(D).astype(np.float32)
        x = jax.random.normal(ks[0], (B, T, D), dtype=jnp.float32)
        Wq = jax.random.normal(ks[1], (D, D), dtype=jnp.float32) * s
        Wk = jax.random.normal(ks[2], (D, D), dtype=jnp.float32) * s
        Wv = jax.random.normal(ks[3], (D, D), dtype=jnp.float32) * s
        Wo = jax.random.normal(ks[4], (D, D), dtype=jnp.float32) * s
        z = jnp.zeros((D,), dtype=jnp.float32)
        return {'x': x, 'Wq': Wq, 'bq': z, 'Wk': Wk, 'bk': z, 'Wv': Wv, 'bv': z, 'Wo': Wo, 'bo': z}
    _L1_attn_all = _L1_attn_setup()
    _L1_attn_in = {k: v for k, v in _L1_attn_all.items() if k in ('Wq', 'bq', 'Wk', 'bk', 'Wv', 'bv', 'Wo', 'bo')}
    del _L1_attn_all

    def _L1_xattn_setup():
        import jax, jax.numpy as jnp
        import numpy as np
        import math
        B, S, D = (8, 256, 128)
        key = jax.random.key(seed)
        ks = jax.random.split(key, 8)
        s_in = 1.0 / math.sqrt(D)
        s_ent = 1.0 / math.sqrt(2 * D)
        return {'x': jax.random.normal(ks[0], (B, S, D), dtype=jnp.float32), 'context': jax.random.normal(ks[1], (B, S, D), dtype=jnp.float32), 'Wq': jax.random.normal(ks[2], (D, D), dtype=jnp.float32) * s_in, 'bq': jnp.zeros((D,), jnp.float32), 'Wk': jax.random.normal(ks[3], (D, D), dtype=jnp.float32) * s_in, 'bk': jnp.zeros((D,), jnp.float32), 'Wv': jax.random.normal(ks[4], (D, D), dtype=jnp.float32) * s_in, 'bv': jnp.zeros((D,), jnp.float32), 'We': jax.random.normal(ks[5], (D, 2 * D), dtype=jnp.float32) * s_ent, 'be': jnp.zeros((D,), jnp.float32)}
    _L1_xattn_all = _L1_xattn_setup()
    _L1_xattn_in = {k: v for k, v in _L1_xattn_all.items() if k in ('Wq', 'bq', 'Wk', 'bk', 'Wv', 'bv', 'We', 'be')}
    del _L1_xattn_all

    def _L1_ffn_setup():
        import jax, jax.numpy as jnp
        import numpy as np
        H, HP, NH_M, NH_D = (128, 64, 8, 8)
        B, T = (2, 256)
        SPARSITY = 8
        N_ROT = 32
        BASE = 10000.0

        def _rope(x, pos, n_rot, base):
            half = n_rot // 2
            inv = base ** (-jnp.arange(half, dtype=x.dtype) / half)
            ang = pos[..., None] * inv
            cos, sin = (jnp.cos(ang), jnp.sin(ang))
            x1, x2 = (x[..., :half], x[..., half:n_rot])
            rot = jnp.concatenate([x1 * cos - x2 * sin, x1 * sin + x2 * cos], axis=-1)
            return jnp.concatenate([rot, x[..., n_rot:]], axis=-1)

        def _mosa_branch(X, router_w, wqkv, wo):
            b, t, _ = X.shape
            k = t // SPARSITY
            scores = jnp.einsum('bth,hn->bnt', X, router_w)
            _, idx = jax.lax.top_k(scores, k)
            idx = jnp.sort(idx, axis=-1)
            gates = jax.nn.sigmoid(jnp.take_along_axis(scores, idx, axis=-1))
            Xg = jnp.take_along_axis(X[:, None], idx[..., None], axis=2)
            qkv = jnp.einsum('bnkh,hnd->bnkd', Xg, wqkv)
            Q, K, V = jnp.split(qkv, 3, axis=-1)
            pos = idx.astype(X.dtype)
            Q = _rope(Q, pos, N_ROT, BASE)
            K = _rope(K, pos, N_ROT, BASE)
            att = jnp.einsum('bnqd,bnkd->bnqk', Q, K) / jnp.sqrt(jnp.asarray(HP, X.dtype))
            causal = idx[..., :, None] >= idx[..., None, :]
            att = jnp.where(causal, att, -jnp.inf)
            AV = jnp.einsum('bnqk,bnkd->bnqd', jax.nn.softmax(att, axis=-1), V)
            AV = AV * gates[..., None]
            out = jnp.zeros((b, NH_M, t, HP), X.dtype)
            bi = jnp.arange(b)[:, None, None]
            hi = jnp.arange(NH_M)[None, :, None]
            out = out.at[bi, hi, idx].set(AV)
            out = out.transpose(0, 2, 1, 3).reshape(b, t, NH_M * HP)
            return out @ wo

        def _dense_branch(X, wqkv, wo):
            b, t, _ = X.shape
            qkv = jnp.einsum('bth,hnd->bntd', X, wqkv)
            Q, K, V = jnp.split(qkv, 3, axis=-1)
            pos = jnp.arange(t, dtype=X.dtype)
            Q = _rope(Q, pos, N_ROT, BASE)
            K = _rope(K, pos, N_ROT, BASE)
            att = jnp.einsum('bnqd,bnkd->bnqk', Q, K) / jnp.sqrt(jnp.asarray(HP, X.dtype))
            causal = jnp.tril(jnp.ones((t, t), bool))
            att = jnp.where(causal, att, -jnp.inf)
            AV = jnp.einsum('bnqk,bnkd->bnqd', jax.nn.softmax(att, axis=-1), V)
            return AV.transpose(0, 2, 1, 3).reshape(b, t, NH_D * HP) @ wo
        key = jax.random.key(seed)
        ks = jax.random.split(key, 6)
        s = 0.02
        return {'X': jax.random.normal(ks[0], (B, T, H), jnp.float32), 'mosa_router_w': jax.random.normal(ks[1], (H, NH_M), jnp.float32) * s, 'mosa_wqkv': jax.random.normal(ks[2], (H, NH_M, 3 * HP), jnp.float32) * s, 'mosa_wo': jax.random.normal(ks[3], (NH_M * HP, H), jnp.float32) * s, 'dense_wqkv': jax.random.normal(ks[4], (H, NH_D, 3 * HP), jnp.float32) * s, 'dense_wo': jax.random.normal(ks[5], (NH_D * HP, H), jnp.float32) * s}
    _L1_ffn_all = _L1_ffn_setup()
    _L1_ffn_in = {k: v for k, v in _L1_ffn_all.items() if k in ('mosa_router_w', 'mosa_wqkv', 'mosa_wo', 'dense_wqkv', 'dense_wo')}
    del _L1_ffn_all
    return {'x': x, 'ctx_1024': ctx_1024, 'L0_attn_W_q': _L0_attn_in['W_q'], 'L0_attn_W_k': _L0_attn_in['W_k'], 'L0_attn_W_v': _L0_attn_in['W_v'], 'L0_attn_W_o': _L0_attn_in['W_o'], 'L0_xattn_Wq': _L0_xattn_in['Wq'], 'L0_xattn_bq': _L0_xattn_in['bq'], 'L0_xattn_Wk': _L0_xattn_in['Wk'], 'L0_xattn_bk': _L0_xattn_in['bk'], 'L0_xattn_Wv': _L0_xattn_in['Wv'], 'L0_xattn_bv': _L0_xattn_in['bv'], 'L0_xattn_Wo': _L0_xattn_in['Wo'], 'L0_xattn_bo': _L0_xattn_in['bo'], 'L0_ffn_W_in': _L0_ffn_in['W_in'], 'L0_ffn_b_in': _L0_ffn_in['b_in'], 'L0_ffn_W_out': _L0_ffn_in['W_out'], 'L1_attn_Wq': _L1_attn_in['Wq'], 'L1_attn_bq': _L1_attn_in['bq'], 'L1_attn_Wk': _L1_attn_in['Wk'], 'L1_attn_bk': _L1_attn_in['bk'], 'L1_attn_Wv': _L1_attn_in['Wv'], 'L1_attn_bv': _L1_attn_in['bv'], 'L1_attn_Wo': _L1_attn_in['Wo'], 'L1_attn_bo': _L1_attn_in['bo'], 'L1_xattn_Wq': _L1_xattn_in['Wq'], 'L1_xattn_bq': _L1_xattn_in['bq'], 'L1_xattn_Wk': _L1_xattn_in['Wk'], 'L1_xattn_bk': _L1_xattn_in['bk'], 'L1_xattn_Wv': _L1_xattn_in['Wv'], 'L1_xattn_bv': _L1_xattn_in['bv'], 'L1_xattn_We': _L1_xattn_in['We'], 'L1_xattn_be': _L1_xattn_in['be'], 'L1_ffn_mosa_router_w': _L1_ffn_in['mosa_router_w'], 'L1_ffn_mosa_wqkv': _L1_ffn_in['mosa_wqkv'], 'L1_ffn_mosa_wo': _L1_ffn_in['mosa_wo'], 'L1_ffn_dense_wqkv': _L1_ffn_in['dense_wqkv'], 'L1_ffn_dense_wo': _L1_ffn_in['dense_wo']}

def reference(x, ctx_1024, L0_attn_W_q, L0_attn_W_k, L0_attn_W_v, L0_attn_W_o, L0_xattn_Wq, L0_xattn_bq, L0_xattn_Wk, L0_xattn_bk, L0_xattn_Wv, L0_xattn_bv, L0_xattn_Wo, L0_xattn_bo, L0_ffn_W_in, L0_ffn_b_in, L0_ffn_W_out, L1_attn_Wq, L1_attn_bq, L1_attn_Wk, L1_attn_bk, L1_attn_Wv, L1_attn_bv, L1_attn_Wo, L1_attn_bo, L1_xattn_Wq, L1_xattn_bq, L1_xattn_Wk, L1_xattn_bk, L1_xattn_Wv, L1_xattn_bv, L1_xattn_We, L1_xattn_be, L1_ffn_mosa_router_w, L1_ffn_mosa_wqkv, L1_ffn_mosa_wo, L1_ffn_dense_wqkv, L1_ffn_dense_wo):
    import jax
    import jax.numpy as jnp

    def _L0_attn_ref(x, W_q, W_k, W_v, W_o):
        import jax, jax.numpy as jnp
        import numpy as np
        import math
        D_MODEL = 128
        N_HEADS = 16
        D_HEAD = D_MODEL // N_HEADS
        MAX_SEQ_LEN = 256
        BASE = 10000.0

        def _rope_tables(L):
            pos = jnp.arange(L, dtype=jnp.float32)[:, None]
            freqs = jnp.exp(-math.log(BASE) * jnp.arange(0, D_HEAD, 2, dtype=jnp.float32) / D_HEAD)
            angles = pos * freqs
            return (jnp.sin(angles), jnp.cos(angles))

        def _apply_rope(x, sin, cos):
            s = sin[None, :, None, :]
            c = cos[None, :, None, :]
            x_even, x_odd = (x[..., ::2], x[..., 1::2])
            rot_even = x_even * c - x_odd * s
            rot_odd = x_even * s + x_odd * c
            return jnp.stack([rot_even, rot_odd], axis=-1).reshape(x.shape)
        B, L, _ = x.shape
        sin, cos = _rope_tables(L)
        q = (x @ W_q.T).reshape(B, L, N_HEADS, D_HEAD)
        k = (x @ W_k.T).reshape(B, L, N_HEADS, D_HEAD)
        v = (x @ W_v.T).reshape(B, L, N_HEADS, D_HEAD)
        q = _apply_rope(q, sin, cos)
        k = _apply_rope(k, sin, cos)
        scores = jnp.einsum('blhd,bshd->bhls', q, k) / math.sqrt(D_HEAD)
        weights = jax.nn.softmax(scores, axis=-1)
        out = jnp.einsum('bhls,bshd->blhd', weights, v).reshape(B, L, D_MODEL)
        return out @ W_o.T

    def _L0_xattn_ref(query, key, value, Wq, bq, Wk, bk, Wv, bv, Wo, bo):
        import jax, jax.numpy as jnp
        import numpy as np
        D_MODEL = 128
        NHEAD = 16
        NUM_KV = 4
        D_K = D_MODEL // NHEAD
        GROUP = NHEAD // NUM_KV
        ROPE_BASE = 10000.0

        def _rope(x, seq_len):
            half = D_K // 2
            inv_freq = 1.0 / ROPE_BASE ** (jnp.arange(0, D_K, 2, dtype=jnp.float32) / D_K)
            t = jnp.arange(seq_len, dtype=jnp.float32)
            freqs = jnp.outer(t, inv_freq)
            emb = jnp.concatenate([freqs, freqs], axis=-1)
            cos, sin = (jnp.cos(emb), jnp.sin(emb))
            x1, x2 = (x[..., :half], x[..., half:])
            rot = jnp.concatenate([-x2, x1], axis=-1)
            return x * cos + rot * sin
        B, S, _ = query.shape
        T = key.shape[1]
        Q = (query @ Wq.T + bq).reshape(B, S, NHEAD, D_K).transpose(0, 2, 1, 3)
        K = (key @ Wk.T + bk).reshape(B, T, NUM_KV, D_K).transpose(0, 2, 1, 3)
        V = (value @ Wv.T + bv).reshape(B, T, NUM_KV, D_K).transpose(0, 2, 1, 3)
        Q = _rope(Q, S)
        K = _rope(K, T)
        Kr = jnp.repeat(K, GROUP, axis=1)
        Vr = jnp.repeat(V, GROUP, axis=1)
        scale = 1.0 / np.sqrt(D_K)
        scores = jnp.einsum('bhsd,bhtd->bhst', Q, Kr) * scale
        attn = jax.nn.softmax(scores, axis=-1)
        context = jnp.einsum('bhst,bhtd->bhsd', attn, Vr)
        context = context.transpose(0, 2, 1, 3).reshape(B, S, D_MODEL)
        return context @ Wo.T + bo

    def _L0_ffn_ref(oldx, W_in, b_in, W_out):
        import jax, jax.numpy as jnp
        import numpy as np
        DIM = 128
        DEPTH = 7
        PAR = 8
        N_NODES = 2 ** (DEPTH + 1) - 1
        WIDTH = PAR * N_NODES
        x = oldx.reshape(-1, DIM)
        B = x.shape[0]
        logits = x @ W_in.T + b_in
        decisions = (logits > 0).astype(jnp.int32).reshape(B, PAR, N_NODES)
        acts = jax.nn.silu(logits).reshape(B, PAR, N_NODES)
        current = jnp.zeros((B, PAR), dtype=jnp.int32)
        dmap = jax.nn.one_hot(current, N_NODES, dtype=acts.dtype)
        for d in range(DEPTH):
            cur_platform = 2 ** d - 1
            next_platform = 2 ** (d + 1) - 1
            moves = jnp.take_along_axis(decisions, current[..., None], axis=2)[..., 0]
            current = (current - cur_platform) * 2 + moves + next_platform
            dmap = dmap + jax.nn.one_hot(current, N_NODES, dtype=acts.dtype)
        masked = acts * jax.lax.stop_gradient(dmap)
        out = masked.reshape(B, WIDTH) @ W_out.T
        return out.reshape(oldx.shape)

    def _L1_attn_ref(x, Wq, bq, Wk, bk, Wv, bv, Wo, bo):
        import jax, jax.numpy as jnp
        import numpy as np
        B, T, D = (2, 256, 128)
        H = 16
        DH = D // H
        TOPK = 32
        b, t, d = x.shape
        h, dh, topk = (H, DH, TOPK)
        q = (x @ Wq.T + bq).reshape(b, t, h, dh).transpose(0, 2, 1, 3)
        k = (x @ Wk.T + bk).reshape(b, t, h, dh).transpose(0, 2, 1, 3)
        v = (x @ Wv.T + bv).reshape(b, t, h, dh).transpose(0, 2, 1, 3)
        scale = np.float32(1.0 / np.sqrt(dh))
        scores = jnp.einsum('bhqd,bhkd->bhqk', q, k) * scale
        topv, topi = jax.lax.top_k(scores, topk)
        neg = jnp.full((b * h * t, t), -jnp.inf, dtype=scores.dtype)
        rows = jnp.arange(b * h * t)[:, None]
        sparse = neg.at[rows, topi.reshape(-1, topk)].set(topv.reshape(-1, topk))
        sparse = sparse.reshape(b, h, t, t)
        attn = jax.nn.softmax(sparse, axis=-1)
        out = jnp.einsum('bhqk,bhkd->bhqd', attn, v)
        out = out.transpose(0, 2, 1, 3).reshape(b, t, d)
        return out @ Wo.T + bo

    def _L1_xattn_ref(x, context, Wq, bq, Wk, bk, Wv, bv, We, be):
        import jax, jax.numpy as jnp
        import numpy as np
        import math
        B, S, D = (8, 256, 128)
        q = jnp.einsum('bsd,ed->bse', x, Wq) + bq
        k = jnp.einsum('bsd,ed->bse', context, Wk) + bk
        v = jnp.einsum('bsd,ed->bse', context, Wv) + bv
        entangled = jnp.tanh(jnp.einsum('bsd,ed->bse', jnp.concatenate([q, k], axis=-1), We) + be)
        scale = 1.0 / math.sqrt(x.shape[-1])
        scores = jnp.einsum('bqd,bkd->bqk', entangled, v) * scale
        attn = jax.nn.softmax(scores, axis=-1)
        return jnp.einsum('bqk,bkd->bqd', attn, v)

    def _L1_ffn_ref(X, mosa_router_w, mosa_wqkv, mosa_wo, dense_wqkv, dense_wo):
        import jax, jax.numpy as jnp
        import numpy as np
        H, HP, NH_M, NH_D = (128, 64, 8, 8)
        B, T = (2, 256)
        SPARSITY = 8
        N_ROT = 32
        BASE = 10000.0

        def _rope(x, pos, n_rot, base):
            half = n_rot // 2
            inv = base ** (-jnp.arange(half, dtype=x.dtype) / half)
            ang = pos[..., None] * inv
            cos, sin = (jnp.cos(ang), jnp.sin(ang))
            x1, x2 = (x[..., :half], x[..., half:n_rot])
            rot = jnp.concatenate([x1 * cos - x2 * sin, x1 * sin + x2 * cos], axis=-1)
            return jnp.concatenate([rot, x[..., n_rot:]], axis=-1)

        def _mosa_branch(X, router_w, wqkv, wo):
            b, t, _ = X.shape
            k = t // SPARSITY
            scores = jnp.einsum('bth,hn->bnt', X, router_w)
            _, idx = jax.lax.top_k(scores, k)
            idx = jnp.sort(idx, axis=-1)
            gates = jax.nn.sigmoid(jnp.take_along_axis(scores, idx, axis=-1))
            Xg = jnp.take_along_axis(X[:, None], idx[..., None], axis=2)
            qkv = jnp.einsum('bnkh,hnd->bnkd', Xg, wqkv)
            Q, K, V = jnp.split(qkv, 3, axis=-1)
            pos = idx.astype(X.dtype)
            Q = _rope(Q, pos, N_ROT, BASE)
            K = _rope(K, pos, N_ROT, BASE)
            att = jnp.einsum('bnqd,bnkd->bnqk', Q, K) / jnp.sqrt(jnp.asarray(HP, X.dtype))
            causal = idx[..., :, None] >= idx[..., None, :]
            att = jnp.where(causal, att, -jnp.inf)
            AV = jnp.einsum('bnqk,bnkd->bnqd', jax.nn.softmax(att, axis=-1), V)
            AV = AV * gates[..., None]
            out = jnp.zeros((b, NH_M, t, HP), X.dtype)
            bi = jnp.arange(b)[:, None, None]
            hi = jnp.arange(NH_M)[None, :, None]
            out = out.at[bi, hi, idx].set(AV)
            out = out.transpose(0, 2, 1, 3).reshape(b, t, NH_M * HP)
            return out @ wo

        def _dense_branch(X, wqkv, wo):
            b, t, _ = X.shape
            qkv = jnp.einsum('bth,hnd->bntd', X, wqkv)
            Q, K, V = jnp.split(qkv, 3, axis=-1)
            pos = jnp.arange(t, dtype=X.dtype)
            Q = _rope(Q, pos, N_ROT, BASE)
            K = _rope(K, pos, N_ROT, BASE)
            att = jnp.einsum('bnqd,bnkd->bnqk', Q, K) / jnp.sqrt(jnp.asarray(HP, X.dtype))
            causal = jnp.tril(jnp.ones((t, t), bool))
            att = jnp.where(causal, att, -jnp.inf)
            AV = jnp.einsum('bnqk,bnkd->bnqd', jax.nn.softmax(att, axis=-1), V)
            return AV.transpose(0, 2, 1, 3).reshape(b, t, NH_D * HP) @ wo
        return _mosa_branch(X, mosa_router_w, mosa_wqkv, mosa_wo) + _dense_branch(X, dense_wqkv, dense_wo)
    x = x + _L0_attn_ref(_layernorm(x, axis=-1), L0_attn_W_q, L0_attn_W_k, L0_attn_W_v, L0_attn_W_o)
    x = x + _L0_xattn_ref(_layernorm(x, axis=-1), ctx_1024, ctx_1024, L0_xattn_Wq, L0_xattn_bq, L0_xattn_Wk, L0_xattn_bk, L0_xattn_Wv, L0_xattn_bv, L0_xattn_Wo, L0_xattn_bo)
    x = x + _L0_ffn_ref(_layernorm(x, axis=-1), L0_ffn_W_in, L0_ffn_b_in, L0_ffn_W_out)
    x = x + _L1_attn_ref(_layernorm(x, axis=-1), L1_attn_Wq, L1_attn_bq, L1_attn_Wk, L1_attn_bk, L1_attn_Wv, L1_attn_bv, L1_attn_Wo, L1_attn_bo)
    x = x + _L1_xattn_ref(_layernorm(x, axis=-1), ctx_1024, L1_xattn_Wq, L1_xattn_bq, L1_xattn_Wk, L1_xattn_bk, L1_xattn_Wv, L1_xattn_bv, L1_xattn_We, L1_xattn_be)
    x = x + _L1_ffn_ref(_layernorm(x, axis=-1), L1_ffn_mosa_router_w, L1_ffn_mosa_wqkv, L1_ffn_mosa_wo, L1_ffn_dense_wqkv, L1_ffn_dense_wo)
    return x

_drawn_inputs = setup_inputs


def setup_inputs(seed=0):
    import zlib

    import numpy as np

    out = dict(_drawn_inputs(seed))
    spreads = {'L0_xattn_bq': (0.0, 0.1),
     'L0_xattn_bk': (0.0, 0.357),
     'L0_xattn_bv': (0.0, 0.1),
     'L0_xattn_bo': (0.0, 0.1),
     'L1_attn_bq': (0.0, 0.1),
     'L1_attn_bk': (0.0, 0.8),
     'L1_attn_bv': (0.0, 0.1),
     'L1_attn_bo': (0.0, 0.1),
     'L1_xattn_bq': (0.0, 0.8),
     'L1_xattn_bk': (0.0, 0.8),
     'L1_xattn_bv': (0.0, 0.1),
     'L1_xattn_be': (0.0, 0.696)}
    factors = {'L1_ffn_mosa_router_w': 5.752, 'L1_ffn_mosa_wqkv': 5.471, 'L1_ffn_mosa_wo': 5.417}
    for name, (base, spread) in spreads.items():
        noise = np.random.default_rng([zlib.crc32(name.encode()), seed]).standard_normal(out[name].shape)
        drawn = base * np.exp(spread * noise) if base else spread * noise
        out[name] = jnp.asarray(drawn.astype(out[name].dtype))
    for name, factor in factors.items():
        out[name] = (out[name] * factor).astype(out[name].dtype)
    return out
```

```python
from contextlib import ExitStack

import numpy as np
import concourse.bass as bass
from concourse import mybir

ALU = mybir.AluOpType
ACT = mybir.ActivationFunctionType
AX_X = mybir.AxisListType.X
F32 = mybir.dt.float32
BF16 = mybir.dt.bfloat16
I32 = mybir.dt.int32
ds = bass.ds

P = 128
B = 8
T = 256
TILES = B * T // P
H = 16
DH = P // H
UNITS = B * H
TOPK = 32
TERMS = ((0, 0), (0, 1), (0, 2), (1, 0), (1, 1), (2, 0))
KROWS = 72
LOW = -3.0e38
EPS = 1e-5


class Sems:

    def __init__(self, nc, ctx, stage):
        self.nc, self.ctx, self.stage, self.made = nc, ctx, stage, {}

    def __call__(self, name):
        if name not in self.made:
            self.made[name] = self.ctx.enter_context(self.nc.semaphore(f"{self.stage}_{name}"))
        return self.made[name]

    def clear(self):
        numbers = sorted(s.num for s in self.made.values())
        first = 0
        for i in range(1, len(numbers) + 1):
            if i == len(numbers) or numbers[i] != numbers[i - 1] + 1:
                self.nc.gpsimd.sem_clear(range(numbers[first], numbers[i - 1] + 1))
                first = i
        self.nc.all_engine_barrier()


def layernorm_stats(v, sem, X, stats, mean, rstd, tmp):
    chain = sem("ln_chain")
    with v.Fori(0, TILES) as t:
        v.bn_stats(stats[:, ds(t, 1), :], X[:, ds(t, 1), :]).then_inc(sem("ln_stats"), 1)
    v.wait_ge(sem("ln_stats"), TILES)
    me, ve, mo, vo = (stats[:, :, i] for i in (1, 2, 4, 5))
    n = [0]

    def step(ins):
        n[0] += 1
        ins.then_inc(chain, 1)
        v.wait_ge(chain, n[0])

    var, y, y2, d = (tmp[:, i, :] for i in range(4))
    step(v.tensor_tensor(mean[:], me, mo, ALU.add))
    step(v.tensor_scalar(mean[:], mean[:], 0.5, None, ALU.mult))
    step(v.tensor_tensor(d, me, mo, ALU.subtract))
    step(v.scalar_tensor_tensor(d, d, 0.25, d, ALU.mult, ALU.mult))
    step(v.tensor_tensor(var, ve, vo, ALU.add))
    step(v.scalar_tensor_tensor(var, var, 1.0 / P, d, ALU.mult, ALU.add))
    step(v.tensor_scalar(var, var, EPS, None, ALU.add))
    step(v.tensor_scalar(y.bitcast(I32), var.bitcast(I32), 1, None, ALU.logical_shift_right))
    step(v.tensor_scalar(y.bitcast(I32), y.bitcast(I32), -1.0, float(0x5F3759DF), ALU.mult, ALU.add))
    for i in range(3):
        step(v.tensor_tensor(y2, y, y, ALU.mult))
        step(v.scalar_tensor_tensor(y2, y2, -0.5, var, ALU.mult, ALU.mult))
        step(v.scalar_tensor_tensor(rstd[:] if i == 2 else y, y2, 1.5, y, ALU.add, ALU.mult))


def before(i):
    return i + 1


def after(i):
    return i + 2


def prepare_heads(nc, stage, X, ctxT, consts, tensors, drams, topk):
    ident = consts["ident"]
    qs, ks, vaug, w, bias, bo = tensors
    w_dram, b_dram, bo_dram, rope_dram = drams
    with ExitStack() as ctx:
        def sb(name, shape, dt=F32):
            return ctx.enter_context(nc.sbuf_tensor(f"{stage}_{name}", shape, dt))

        def bank(name):
            return ctx.enter_context(nc.psum_tensor(f"{stage}_{name}", [P, 2, T], F32))

        sem = Sems(nc, ctx, stage + "p")
        stats = sb("stats", [P, TILES, 6])
        mean = sb("mean", [P, TILES])
        rstd = sb("rstd", [P, TILES])
        lntmp = sb("lntmp", [P, 4, TILES])
        xn = sb("xn", [P, 2, 2, P])
        xnT = sb("xnT", [P, 2, T])
        kvT = sb("kvT", [P, 2, T]) if ctxT is not None else xnT
        r = sb("r", [P, 2, 2, T])
        r2 = sb("r2", [P, 2, 2, T]) if not topk else None
        d1 = sb("d1", [P, 2, 2, T])
        parts = [sb(f"part{i}", [P, 2, 2, T], BF16) for i in range(3)]
        rope = sb("rope", [P, 4, T]) if not topk else None
        pT = [bank(f"pT{i}")[:, 0, :] for i in range(2)]
        pA = [bank(f"pA{i}") for i in range(2)]
        pB = [bank(f"pB{i}") for i in range(2)]
        pV = [bank(f"pV{i}")[:, :, 0:P] for i in range(2)]

        def pair(name):
            return [sem(f"{name}{i}") for i in range(2)]

        xn_made, xT_done, xnT_made, qk_done, v_done, v_made, r_made, part0_made, d1_made, part1_made, parts_made, stacked = (
            pair(n) for n in ("xn_made", "xT_done", "xnT_made", "qk_done", "v_done", "v_made", "r_made", "part0_made",
                              "d1_made", "part1_made", "parts_made", "stacked"))
        credited = xT_done + xnT_made + v_done + v_made + r_made + d1_made + stacked + xn_made + qk_done + part0_made + part1_made + parts_made
        stack_inc = 16 * 2 * len(TERMS)
        w_in, rope_in = sem("w_in"), sem("rope_in")

        with nc.Block() as block:
            @block.sync
            def _(sp):
                sp.dma_start(w[:], w_dram).then_inc(w_in, 16)
                if b_dram is not None:
                    sp.dma_start(bias[:], b_dram).then_inc(w_in, 16)
                    sp.dma_start(bo[:], bo_dram).then_inc(w_in, 16)
                if rope is not None:
                    sp.dma_start(rope[:], rope_dram).then_inc(rope_in, 16)
                with sp.Fori(0, B // 2) as i:
                    for par in range(2):
                        sp.wait_ge(parts_made[par], after(i))
                        for side, stack in ((0, qs), (1, ks)):
                            for t, term in enumerate(TERMS):
                                sp.dma_start(
                                    stack[DH * t:DH * (t + 1), ds((i * 2 + par) * H, H), :],
                                    parts[term[side]][:, par, side, :],
                                ).then_inc(stacked[par], 16)
                for par in range(2):
                    sp.wait_ge(stacked[par], stack_inc * (B // 2) + 1)

            @block.gpsimd
            def _(pool):
                for s in credited:
                    pool.sem_inc(s, 1)
                pool.memset(vaug[:, :, :, DH:DH + 1], 1.0).then_inc(sem("ones_made"), 1)
                if b_dram is None:
                    pool.memset(bias[:], 0.0).then_inc(w_in, 16)
                    pool.memset(bo[:], 0.0).then_inc(w_in, 16)
                with pool.Fori(0, B // 2) as i:
                    for par in range(2):
                        pool.wait_ge(part0_made[par], after(i))
                        pool.tensor_tensor(d1[:, par], r[:, par], parts[0][:, par], ALU.subtract).then_inc(d1_made[par], 1)
                        pool.wait_ge(part1_made[par], after(i))
                        pool.tensor_tensor(parts[2][:, par], d1[:, par], parts[1][:, par], ALU.subtract).then_inc(parts_made[par], 1)

            @block.vector
            def _(v):
                layernorm_stats(v, sem, X, stats, mean, rstd, lntmp)
                v.wait_ge(w_in, 48)
                if rope is not None:
                    v.wait_ge(rope_in, 16)
                chain = sem("rope_chain")
                with v.Fori(0, B // 2) as i:
                    for par in range(2):
                        v.wait_ge(xT_done[par], before(i))
                        for kt in range(2):
                            tile = i * 4 + par * 2 + kt
                            ins = v.tensor_scalar(xn[:, par, kt, :], X[:, ds(tile, 1), :], mean[:, ds(tile, 1)],
                                                  rstd[:, ds(tile, 1)], ALU.subtract, ALU.mult)
                        ins.then_inc(xn_made[par], 1)
                    for par in range(2):
                        A, C = pA[par], pB[par]
                        v.wait_ge(qk_done[par], after(i))
                        v.wait_ge(d1_made[par], before(i))
                        if topk:
                            v.tensor_scalar(r[:, par, 0, :], A[:, 0, :], bias[:, 0:1], DH ** -0.5, ALU.add, ALU.mult)
                            v.tensor_scalar(r[:, par, 1, :], A[:, 1, :], bias[:, 2:3], None, ALU.add).then_inc(r_made[par], 1)
                        else:
                            for s in range(2):
                                v.scalar_tensor_tensor(r[:, par, s, :], A[:, s, :], bias[:, 2 * s:2 * s + 1], rope[:, s, :],
                                                       ALU.add, ALU.mult).then_inc(chain, 1)
                                v.scalar_tensor_tensor(r2[:, par, s, :], C[:, s, :], bias[:, 2 * s + 1:2 * s + 2],
                                                       rope[:, 2 + s, :], ALU.add, ALU.mult).then_inc(chain, 1)
                            v.wait_ge(chain, 4)
                            v.sem_clear(chain)
                            v.tensor_tensor(r[:, par], r[:, par], r2[:, par], ALU.add).then_inc(r_made[par], 1)

            @block.scalar
            def _(act):
                with act.Fori(0, B // 2) as i:
                    for par in range(2):
                        act.wait_ge(xT_done[par], after(i))
                        act.wait_ge(v_done[par], before(i))
                        ins = act.copy(xnT[:, par, :], pT[par])
                        if ctxT is not None:
                            ins = act.copy(kvT[:, par, :], ctxT[:, ds((i * 2 + par) * T, T)])
                        ins.then_inc(xnT_made[par], 1)
                    for par in range(2):
                        act.wait_ge(v_done[par], after(i))
                        act.copy(vaug[:, :, ds((i * 2 + par) * H, H), 0:DH],
                                 pV[par].rearrange("p k (h d) -> p k h d", d=DH)).then_inc(v_made[par], 1)
                        act.wait_ge(r_made[par], after(i))
                        act.wait_ge(stacked[par], i * stack_inc + 1)
                        act.copy(parts[0][:, par], r[:, par]).then_inc(part0_made[par], 1)
                    for par in range(2):
                        act.wait_ge(d1_made[par], after(i))
                        act.copy(parts[1][:, par], d1[:, par]).then_inc(part1_made[par], 1)

            @block.tensor
            def _(pe):
                pe.wait_ge(w_in, 48)
                with pe.Fori(0, B // 2) as i:
                    for par in range(2):
                        pe.wait_ge(xn_made[par], after(i))
                        pe.wait_ge(xnT_made[par], before(i))
                        for kt in range(2):
                            ins = pe.transpose(pT[par][:, kt * P:(kt + 1) * P], xn[:, par, kt, :], ident[:])
                        ins.then_inc(xT_done[par], 1)
                    for par in range(2):
                        pe.wait_ge(xnT_made[par], after(i))
                        pe.wait_ge(r_made[par], before(i))
                        src = (xnT, kvT)
                        for s in range(2):
                            ins = pe.matmul(pA[par][:, s, :], w[:, 2 * s, :], src[s][:, par, :], start=True, stop=True)
                            if not topk:
                                ins = pe.matmul(pB[par][:, s, :], w[:, 2 * s + 1, :], src[s][:, par, :], start=True, stop=True)
                        ins.then_inc(qk_done[par], 1)
                        pe.wait_ge(v_made[par], before(i))
                        for kt in range(2):
                            ins = pe.matmul(pV[par][:, kt, :], kvT[:, par, kt * P:(kt + 1) * P], w[:, 4, :], start=True, stop=True)
                        ins.then_inc(v_done[par], 1)

        sem.clear()


def attend_heads(nc, stage, X, consts, tensors, topk):
    ident, ones = consts["ident"], consts["ones"]
    qs, ks, vaug, w, bias, bo = tensors
    PAIRS = UNITS // 2
    with ExitStack() as ctx:
        def sb(name, shape, dt=F32):
            return ctx.enter_context(nc.sbuf_tensor(f"{stage}_{name}", shape, dt))

        def bank(name):
            return ctx.enter_context(nc.psum_tensor(f"{stage}_{name}", [P, 2, T], F32))

        sem = Sems(nc, ctx, stage + "a")
        m8 = sb("m8", [P, 2, 2, 4, 8]) if topk else None
        nmax = sb("nmax", [P, 2, 2])
        prob = sb("prob", [P, 2, 2, T])
        rest = sb("rest", [P, 2, 2, T]) if topk else None
        prest = sb("prest", [P, 2, 2, T]) if topk else None
        probT = sb("probT", [P, 2, 2, T])
        oall = sb("oall", [P, UNITS, 2, DH + 1])
        rsum = sb("rsum", [P, 2, 2, H])
        on = sb("on", [P, 2, 2, H, DH])
        onT = sb("onT", [P, 2, T])
        pS = [bank(f"pS{i}") for i in range(2)]
        pPT = [bank(f"pPT{i}") for i in range(2)]
        pO = bank("pO")[:, 0, 0:4 * (DH + 1)].rearrange("p (a q d) -> p a q d", a=2, q=2)
        pOT = [t[:, 0, :] for t in pS]
        pY = [t[:, :, 0:P] for t in pPT]

        def pair(name):
            return [sem(f"{name}{i}") for i in range(2)]

        s_done, nmax_made, exp_done, p_made, t_done, probT_made, pv_done, topk_done, o_kept = (
            pair(n) for n in ("s_done", "nmax_made", "exp_done", "p_made", "t_done", "probT_made", "pv_done", "topk_done", "o_kept"))
        norm_done, oT_done, onT_made, y_done, x_done = (
            pair(n) for n in ("norm_done", "oT_done", "onT_made", "y_done", "x_done"))
        credited = (s_done + nmax_made + exp_done + p_made + t_done + probT_made + pv_done + topk_done + o_kept
                    + norm_done + oT_done + onT_made + y_done + x_done)
        dve_evacuates = [] if topk else [0]

        def pairs(eng, step, finish):
            step(0, True)
            with eng.Fori(1, PAIRS) as u:
                step(u, False)
            finish(PAIRS - 1)

        with nc.Block() as block:
            @block.gpsimd
            def _(pool):
                for s in credited:
                    pool.sem_inc(s, 1)
                if topk:
                    with pool.Fori(0, PAIRS) as u:
                        for par in range(2):
                            pool.wait_ge(topk_done[par], after(u))
                            pool.wait_ge(exp_done[par], before(u))
                            pool.sem_inc(sem("waited_pool"), 1)
                            pool.tensor_scalar(nmax[:, par, :], m8[:, par, :, 0, 0], -1.0, 0.0, ALU.mult, ALU.add)\
                                .then_inc(nmax_made[par], 1)
                            pool.wait_ge(exp_done[par], after(u))
                            pool.tensor_tensor(prob[:, par], prob[:, par], prest[:, par], ALU.subtract).then_inc(p_made[par], 1)

            @block.vector
            def _(v):
                chain = sem("topk_chain")

                def largest(u, par):
                    v.wait_ge(s_done[par], after(u))
                    v.wait_ge(exp_done[par], before(u))
                    v.sem_inc(sem("waited_dve"), 1)
                    n = 0
                    for rnd in range(TOPK // 8):
                        src = pS[par] if rnd == 0 else rest[:, par]
                        for qt in range(2):
                            if rnd:
                                v.wait_ge(chain, n - 1)
                            v.max(m8[:, par, qt, rnd, :], src[:, qt, :]).then_inc(chain, 1)
                            n += 1
                        for qt in range(2):
                            v.wait_ge(chain, n - 1)
                            ins = v.match_replace(rest[:, par, qt, :], m8[:, par, qt, rnd, :], src[:, qt, :], LOW)
                            if n < 4 * TOPK // 8 - 1:
                                ins.then_inc(chain, 1)
                            else:
                                ins.then_inc(topk_done[par], 1)
                            n += 1
                    v.wait_ge(chain, 4 * TOPK // 8 - 1)
                    v.sem_clear(chain)

                def maxima(u, par):
                    v.wait_ge(s_done[par], after(u))
                    v.wait_ge(exp_done[par], before(u))
                    v.tensor_reduce(nmax[:, par, :], pS[par][:], AX_X, ALU.max, negate=True).then_inc(nmax_made[par], 1)

                def evacuate(u, par):
                    v.wait_ge(t_done[par], after(u))
                    v.wait_ge(pv_done[par], before(u))
                    v.tensor_copy(probT[:, par], pPT[par][:]).then_inc(probT_made[par], 1)

                def step(u, first):
                    for par in range(2):
                        if topk:
                            largest(u, par)
                        else:
                            maxima(u, par)
                            if not first and par in dve_evacuates:
                                evacuate(u - 1, par)

                def finish(last):
                    for par in dve_evacuates:
                        evacuate(last, par)

                pairs(v, step, finish)
                v.wait_ge(o_kept[0], after(PAIRS - 1))
                tail = sem("tail_chain")
                with v.Fori(0, B // 2) as i:
                    for par in range(2):
                        units = oall[:, ds((i * 2 + par) * H, H), :, :].rearrange("p h q d -> p q h d")
                        v.wait_ge(oT_done[par], before(i))
                        v.reciprocal(rsum[:, par], units[:, :, :, DH]).then_inc(tail, 1)
                        v.wait_ge(tail, 1)
                        v.sem_clear(tail)
                        v.tensor_tensor(on[:, par], units[:, :, :, 0:DH],
                                        rsum[:, par].unsqueeze(3).broadcast_to([P, 2, H, DH]), ALU.mult).then_inc(norm_done[par], 1)
                    for par in range(2):
                        tiles = X[:, ds(i * 4 + par * 2, 2), :]
                        v.wait_ge(y_done[par], after(i))
                        v.tensor_tensor(tiles, tiles, pY[par], ALU.add).then_inc(x_done[par], 1)

            @block.scalar
            def _(act):
                def exponentials(u, par):
                    act.wait_ge(nmax_made[par], after(u))
                    act.wait_ge(t_done[par], before(u))
                    if topk:
                        for qt in range(2):
                            act.activation(prest[:, par, qt, :], rest[:, par, qt, :], ACT.Exp, bias=nmax[:, par, qt:qt + 1])
                    for qt in range(2):
                        ins = act.activation(prob[:, par, qt, :], pS[par][:, qt, :], ACT.Exp, bias=nmax[:, par, qt:qt + 1])
                    ins.then_inc(exp_done[par], 1)

                def evacuate(u, par):
                    act.wait_ge(t_done[par], after(u))
                    act.wait_ge(pv_done[par], before(u))
                    act.copy(probT[:, par], pPT[par][:]).then_inc(probT_made[par], 1)

                def keep(u):
                    act.wait_ge(pv_done[0], after(u))
                    act.wait_ge(pv_done[1], after(u))
                    act.copy(oall[:, ds(u * 2, 2), :, :], pO).then_inc(o_kept[0], 1)

                def step(u, first):
                    exponentials(u, 0)
                    if not first and 0 not in dve_evacuates:
                        evacuate(u - 1, 0)
                    exponentials(u, 1)
                    if not first:
                        evacuate(u - 1, 1)
                        keep(u - 1)

                def finish(last):
                    for par in range(2):
                        if par not in dve_evacuates:
                            evacuate(last, par)
                    keep(last)

                pairs(act, step, finish)
                with act.Fori(0, B // 2) as i:
                    for par in range(2):
                        act.wait_ge(oT_done[par], after(i))
                        act.wait_ge(y_done[par], before(i))
                        act.activation(onT[:, par], pOT[par], ACT.Identity, bias=bias[:, 4:5]).then_inc(onT_made[par], 1)

            @block.tensor
            def _(pe):
                def scores(u, par):
                    for qt in range(2):
                        ins = pe.matmul(pS[par][:, qt, :], qs[0:KROWS, ds(u * 2 + par, 1), qt * P:(qt + 1) * P],
                                        ks[0:KROWS, ds(u * 2 + par, 1), :], start=True, stop=True)
                    ins.then_inc(s_done[par], 1)

                def transposes(u, par):
                    pe.wait_ge(probT_made[par], before(u))
                    for kt in range(2):
                        for qt in range(2):
                            ins = pe.transpose(pPT[par][:, kt, qt * P:(qt + 1) * P], prob[:, par, qt, kt * P:(kt + 1) * P], ident[:])
                    ins.then_inc(t_done[par], 1)

                def products(u, par):
                    pe.wait_ge(probT_made[par], after(u))
                    pe.wait_ge(o_kept[0], before(u))
                    for qt in range(2):
                        for kt in range(2):
                            ins = pe.matmul(pO[:, par, qt, :], probT[:, par, kt, qt * P:(qt + 1) * P],
                                            vaug[:, kt, ds(u * 2 + par, 1), :], start=(kt == 0), stop=(kt == 1))
                    ins.then_inc(pv_done[par], 1)

                def step(u, first):
                    for par in range(2):
                        pe.wait_ge(exp_done[par], after(u))
                        scores(u + 1, par)
                        if topk:
                            pe.wait_ge(p_made[par], after(u))
                        transposes(u, par)
                        if not first:
                            products(u - 1, par)

                def finish(last):
                    products(last, 0)
                    products(last, 1)

                pe.wait_ge(consts["zeroed"], consts["zeroed_by"])
                scores(0, 0)
                scores(0, 1)
                pairs(pe, step, finish)
                with pe.Fori(0, B // 2) as i:
                    for par in range(2):
                        pe.wait_ge(norm_done[par], after(i))
                        pe.wait_ge(onT_made[par], before(i))
                        for qt in range(2):
                            ins = pe.transpose(pOT[par][:, qt * P:(qt + 1) * P],
                                               on[:, par, qt].rearrange("p h d -> p (h d)"), ident[:])
                        ins.then_inc(oT_done[par], 1)
                    for par in range(2):
                        pe.wait_ge(onT_made[par], after(i))
                        pe.wait_ge(x_done[par], before(i))
                        for qt in range(2):
                            pe.matmul(pY[par][:, qt, :], onT[:, par, qt * P:(qt + 1) * P], w[:, 5, :], start=True, stop=False)
                            ins = pe.matmul(pY[par][:, qt, :], ones[0:1, :], bo[:], start=False, stop=True)
                        ins.then_inc(y_done[par], 1)

        sem.clear()


def head_attention(nc, stage, X, ctxT, consts, drams, topk):
    with ExitStack() as ctx:
        def sb(name, shape, dt=F32):
            return ctx.enter_context(nc.sbuf_tensor(f"{stage}_{name}", shape, dt))

        tensors = (
            consts["qs"],
            consts["ks"],
            sb("vaug", [P, 2, UNITS, DH + 1]),
            sb("w", [P, 6, P]),
            sb("bias", [P, 5]),
            sb("bo", [1, P]),
        )
        prepare_heads(nc, stage, X, ctxT, consts, tensors, drams, topk)
        attend_heads(nc, stage, X, consts, tensors, topk)


DEPTH = 7
TREES = 8
NODES = 2 ** (DEPTH + 1) - 1
WIDTH = TREES * NODES


def level(d):
    return slice(TREES * (2 ** d - 1), TREES * (2 ** (d + 1) - 1))


CHUNKS = [slice(0, level(5).stop), level(6), slice(level(7).start, level(7).start + 512),
          slice(level(7).start + 512, WIDTH)]
NCHUNK = -(-WIDTH // P)


def tree_ffn(nc, stage, X, consts, drams):
    ident = consts["ident"]
    win_dram, bin_dram, wout_dram = drams
    with ExitStack() as ctx:
        def sb(name, shape, dt=F32):
            return ctx.enter_context(nc.sbuf_tensor(f"{stage}_{name}", shape, dt))

        def bank(name):
            return ctx.enter_context(nc.psum_tensor(f"{stage}_{name}", [P, 512], F32))

        sem = Sems(nc, ctx, stage)
        stats = sb("stats", [P, TILES, 6])
        mean = sb("mean", [P, TILES])
        rstd = sb("rstd", [P, TILES])
        lntmp = sb("lntmp", [P, 4, TILES])
        win = sb("win", [P, WIDTH])
        wout = sb("wout", [P, NCHUNK, P])
        b3 = consts["qs"][0:3].rearrange("p u n -> p (u n)")[:, 0:WIDTH]
        ones3 = sb("ones3", [3, P], BF16)
        xn = sb("xn", [P, 2, P])
        xnT = sb("xnT", [P, 2, P])
        acts = sb("acts", [P, 2, WIDTH])
        path = sb("path", [P, 2, WIDTH], BF16)
        actsT = sb("actsT", [P, 2, NCHUNK, P])
        brow = actsT[0:1, 0].rearrange("p k n -> p (k n)")[:, 0:WIDTH]
        bparts = acts[0:1].rearrange("p a n -> p (a n)").bitcast(BF16)[:, 0:3 * WIDTH].rearrange("p (c n) -> p c n", c=3)
        pL = [bank(f"pL{c}") for c in range(4)]
        pX = bank("pX")
        pT = [bank(f"pT{c}") for c in range(2)]
        pY = bank("pY")

        def pair(name):
            return [sem(f"{name}{i}") for i in range(2)]

        xn_made, xT_done, xnT_made, y_done, x_done = (pair(n) for n in ("xn_made", "xT_done", "xnT_made", "y_done", "x_done"))
        logits, silu_made, decided, masked, aT_done, aT_made = (
            [pair(f"{n}{c}_") for c in range(4)] for n in ("logits", "silu", "decided", "masked", "aT_done", "aT_made"))
        credited = xn_made + xT_done + xnT_made + y_done + x_done + sum(
            logits + silu_made + decided[:2] + masked + aT_done + aT_made, [])

        def tiles(eng, step, finish):
            step(0, 0, None, 1)
            step(0, 1, 0, 0)
            with eng.Fori(1, TILES // 2) as i:
                step(i, 0, i - 1, 1)
                step(i, 1, i, 0)
            finish(TILES // 2 - 1, 1)

        def chunk_groups(g):
            return range(4 * g, 4 * g + 4)

        def rows(k):
            return min(P, WIDTH - k * P)

        with nc.Block() as block:
            @block.sync
            def _(sp):
                sp.dma_start(win[:], win_dram).then_inc(sem("w_in"), 16)
                sp.dma_start(brow, bin_dram).then_inc(sem("b_in"), 16)
                full = (NCHUNK - 1) * P
                sp.dma_start(wout[:, 0:NCHUNK - 1, :], wout_dram[0:full, :].rearrange("(k p) n -> p k n", p=P)).then_inc(sem("w_in"), 16)
                sp.dma_start(wout[0:WIDTH - full, NCHUNK - 1, :], wout_dram[full:WIDTH, :]).then_inc(sem("w_in"), 16)
                sp.wait_ge(sem("b_split"), 4)
                for i in range(3):
                    sp.dma_start(b3[i:i + 1, :], bparts[0:1, i, :]).then_inc(sem("b3_in"), 16)
                sp.wait_ge(sem("b3_in"), 48)

            @block.gpsimd
            def _(pool):
                for s in credited:
                    pool.sem_inc(s, 1)
                pool.memset(ones3[:], 1.0).then_inc(sem("ones3_made"), 1)
                pool.memset(path[:, :, level(0)], 1.0).then_inc(sem("root_made"), 1)
                split = sem("b_split")
                pool.wait_ge(sem("b_in"), 16)
                pool.tensor_copy(bparts[0:1, 0, :], brow).then_inc(split, 1)
                pool.wait_ge(split, 1)
                pool.tensor_tensor(brow, brow, bparts[0:1, 0, :], ALU.subtract).then_inc(split, 1)
                pool.wait_ge(split, 2)
                pool.tensor_copy(bparts[0:1, 1, :], brow).then_inc(split, 1)
                pool.wait_ge(split, 3)
                pool.tensor_tensor(bparts[0:1, 2, :], brow, bparts[0:1, 1, :], ALU.subtract).then_inc(split, 1)

            @block.vector
            def _(v):
                layernorm_stats(v, sem, X, stats, mean, rstd, lntmp)
                chain = sem("path_chain")

                def start(i, par):
                    v.wait_ge(xT_done[par], before(i))
                    v.tensor_scalar(xn[:, par], X[:, ds(i * 2 + par, 1), :], mean[:, ds(i * 2 + par, 1)],
                                    rstd[:, ds(i * 2 + par, 1)], ALU.subtract, ALU.mult).then_inc(xn_made[par], 1)

                def end(i, par):
                    n = 0
                    for d in range(DEPTH):
                        lv, up = level(d), level(d + 1)
                        mid = up.start + TREES * 2 ** d
                        c = 0 if d < DEPTH - 1 else 1
                        if d in (0, DEPTH - 1):
                            v.wait_ge(silu_made[c][par], after(i))
                        if n:
                            v.wait_ge(chain, n)
                        off = CHUNKS[c].start
                        ins = v.scalar_tensor_tensor(path[:, par, mid:up.stop], pL[c][:, lv.start - off:lv.stop - off], 0.0,
                                                     path[:, par, lv], ALU.is_gt, ALU.mult).then_inc(chain, 1)
                        n += 1
                        v.wait_ge(chain, n)
                        v.tensor_tensor(path[:, par, up.start:mid], path[:, par, lv], path[:, par, mid:up.stop],
                                        ALU.subtract).then_inc(chain, 1)
                        n += 1
                        if d >= DEPTH - 2:
                            v.wait_ge(chain, n)
                            v.sem_inc(decided[c][par], 1)
                    v.sem_clear(chain)
                    for c in range(4):
                        v.wait_ge(silu_made[c][par], after(i))
                        v.tensor_tensor(acts[:, par, CHUNKS[c]], acts[:, par, CHUNKS[c]], path[:, par, CHUNKS[c]],
                                        ALU.mult).then_inc(masked[c][par], 1)
                    v.wait_ge(y_done[par], after(i))
                    v.tensor_tensor(X[:, ds(i * 2 + par, 1), :], X[:, ds(i * 2 + par, 1), :], pY[:, 0:P].unsqueeze(1),
                                    ALU.add).then_inc(x_done[par], 1)

                def step(i, par, before_i, before_par):
                    start(i, par)
                    if before_i is not None:
                        end(before_i, before_par)

                v.wait_ge(sem("root_made"), 1)
                tiles(v, step, end)

            @block.scalar
            def _(act):
                def start(i, par):
                    act.wait_ge(xT_done[par], after(i))
                    act.wait_ge(logits[3][par], before(i))
                    act.copy(xnT[:, par], pX[:, 0:P]).then_inc(xnT_made[par], 1)
                    for c in range(4):
                        act.wait_ge(logits[c][par], after(i))
                        if c == 0:
                            act.wait_ge(aT_done[3][par], before(i))
                        size = CHUNKS[c].stop - CHUNKS[c].start
                        act.activation(acts[:, par, CHUNKS[c]], pL[c][:, 0:size], ACT.Silu).then_inc(silu_made[c][par], 1)

                def end(i, par):
                    for g in range(4):
                        act.wait_ge(aT_done[g][par], after(i))
                        if g == 0:
                            act.wait_ge(y_done[par], before(i))
                        for k in chunk_groups(g)[-1:]:
                            n = rows(k)
                        if n == P:
                            ins = act.copy(actsT[:, par, 4 * g:4 * g + 4, :].rearrange("p k n -> p (k n)"), pT[g % 2][:])
                        else:
                            act.copy(actsT[:, par, 4 * g:4 * g + 3, :].rearrange("p k n -> p (k n)"), pT[g % 2][:, 0:3 * P])
                            ins = act.copy(actsT[0:n, par, 4 * g + 3, :], pT[g % 2][0:n, 3 * P:4 * P])
                        ins.then_inc(aT_made[g][par], 1)

                def step(i, par, before_i, before_par):
                    start(i, par)
                    if before_i is not None:
                        end(before_i, before_par)

                tiles(act, step, end)

            @block.tensor
            def _(pe):
                pe.wait_ge(sem("w_in"), 48)
                pe.wait_ge(sem("b3_in"), 48)
                pe.wait_ge(sem("ones3_made"), 1)

                def start(i, par, before_i, before_par):
                    pe.wait_ge(xn_made[par], after(i))
                    if before_i is not None:
                        pe.wait_ge(xnT_made[before_par], after(before_i))
                    pe.transpose(pX[:, 0:P], xn[:, par], ident[:]).then_inc(xT_done[par], 1)
                    pe.wait_ge(xnT_made[par], after(i))
                    for c in range(4):
                        size = CHUNKS[c].stop - CHUNKS[c].start
                        if before_i is not None:
                            pe.wait_ge((decided[c] if c < 2 else silu_made[c])[before_par], after(before_i))
                        pe.matmul(pL[c][:, 0:size], xnT[:, par], win[:, CHUNKS[c]], start=True, stop=False)
                        pe.matmul(pL[c][:, 0:size], ones3[:], b3[:, CHUNKS[c]], start=False, stop=True).then_inc(logits[c][par], 1)

                def end(i, par):
                    for g in range(4):
                        for c in range(4):
                            if CHUNKS[c].start < 512 * (g + 1) and CHUNKS[c].stop > 512 * g:
                                pe.wait_ge(masked[c][par], after(i))
                        if g >= 2:
                            pe.wait_ge(aT_made[g - 2][par], after(i))
                        for k in chunk_groups(g):
                            n = rows(k)
                            ins = pe.transpose(pT[g % 2][0:n, (k % 4) * P:(k % 4 + 1) * P], acts[:, par, k * P:k * P + n], ident[:])
                        ins.then_inc(aT_done[g][par], 1)
                    pe.wait_ge(x_done[1 - par], after(i - 1) if par == 0 else after(i))
                    for g in range(4):
                        pe.wait_ge(aT_made[g][par], after(i))
                        for k in chunk_groups(g):
                            n = rows(k)
                            ins = pe.matmul(pY[:, 0:P], actsT[0:n, par, k, :], wout[0:n, k, :], start=(k == 0), stop=(k == NCHUNK - 1))
                    ins.then_inc(y_done[par], 1)

                def step(i, par, before_i, before_par):
                    start(i, par, before_i, before_par)
                    if before_i is not None:
                        end(before_i, before_par)

                tiles(pe, step, end)

        sem.clear()


def entangled_attention(nc, stage, X, ctxT, consts, drams):
    ident, ones = consts["ident"], consts["ones"]
    w_dram, b_dram, bvrow_dram = drams
    with ExitStack() as ctx:
        def sb(name, shape, dt=F32):
            return ctx.enter_context(nc.sbuf_tensor(f"{stage}_{name}", shape, dt))

        def bank(name):
            return ctx.enter_context(nc.psum_tensor(f"{stage}_{name}", [P, 2, T], F32))

        sem = Sems(nc, ctx, stage)
        stats = sb("stats", [P, TILES, 6])
        mean = sb("mean", [P, TILES])
        rstd = sb("rstd", [P, TILES])
        lntmp = sb("lntmp", [P, 4, TILES])
        w = sb("w", [P, 5, P])
        bias = sb("bias", [P, 4])
        bvrow = sb("bvrow", [1, P])
        xn = sb("xn", [P, 2, 2, P])
        xnT = sb("xnT", [P, 2, T])
        kvT = sb("kvT", [P, 2, T])
        qkT = sb("qkT", [P, 2, 2, T])
        vT = sb("vT", [P, 2, T])
        vaug = sb("vaug", [P, 2, 2, P + 1])
        entT = sb("entT", [P, 2, T])
        nmax = sb("nmax", [P, 2, 2])
        prob = sb("prob", [P, 2, 2, T])
        probT = sb("probT", [P, 2, 2, T])
        rsum = sb("rsum", [P, 2, 2])
        pX, pQK, pVT, pV, pE, pS, pPT, pO = (bank(n) for n in ("pX", "pQK", "pVT", "pV", "pE", "pS", "pPT", "pO"))

        def pair(name):
            return [sem(f"{name}{i}") for i in range(2)]

        names = ("xn_made", "xT_done", "xnT_made", "qk_done", "qk_made", "vT_done", "vT_made", "v_done", "v_made",
                 "e_done", "e_made", "s_done", "nmax_made", "exp_done", "t_done", "probT_made", "o_done", "x_done")
        made = {n: pair(n) for n in names}
        (xn_made, xT_done, xnT_made, qk_done, qk_made, vT_done, vT_made, v_done, v_made, e_done, e_made, s_done,
         nmax_made, exp_done, t_done, probT_made, o_done, x_done) = (made[n] for n in names)

        def batches(eng, start, end):
            start(0, 0, None, None)
            start(0, 1, 0, 0)
            end(0, 0)
            with eng.Fori(1, B // 2) as i:
                start(i, 0, i - 1, 1)
                end(i - 1, 1)
                start(i, 1, i, 0)
                end(i, 0)
            end(B // 2 - 1, 1)

        with nc.Block() as block:
            @block.sync
            def _(sp):
                sp.dma_start(w[:], w_dram).then_inc(sem("w_in"), 16)
                sp.dma_start(bias[:], b_dram).then_inc(sem("w_in"), 16)
                sp.dma_start(bvrow[:], bvrow_dram).then_inc(sem("w_in"), 16)

            @block.gpsimd
            def _(pool):
                for s in sum(made.values(), []):
                    pool.sem_inc(s, 1)
                pool.memset(vaug[:, :, :, P:P + 1], 1.0).then_inc(sem("ones_made"), 1)

            @block.vector
            def _(v):
                layernorm_stats(v, sem, X, stats, mean, rstd, lntmp)
                v.wait_ge(sem("w_in"), 48)

                def start(i, par, pi, ppar):
                    v.wait_ge(xT_done[par], before(i))
                    for kt in range(2):
                        tile = i * 4 + par * 2 + kt
                        ins = v.tensor_scalar(xn[:, par, kt, :], X[:, ds(tile, 1), :], mean[:, ds(tile, 1)],
                                              rstd[:, ds(tile, 1)], ALU.subtract, ALU.mult)
                    ins.then_inc(xn_made[par], 1)
                    v.wait_ge(qk_done[par], after(i))
                    v.wait_ge(e_done[par], before(i))
                    v.tensor_scalar(qkT[:, par, 0, :], pQK[:, 0, :], bias[:, 0:1], None, ALU.add)
                    v.tensor_scalar(qkT[:, par, 1, :], pQK[:, 1, :], bias[:, 1:2], None, ALU.add).then_inc(qk_made[par], 1)
                    v.wait_ge(vT_done[par], after(i))
                    v.wait_ge(s_done[par], before(i))
                    v.tensor_scalar(vT[:, par, :], pVT[:, 0, :], bias[:, 2:3], float(P) ** -0.5, ALU.add, ALU.mult)\
                        .then_inc(vT_made[par], 1)

                def end(i, par):
                    v.wait_ge(s_done[par], after(i))
                    v.wait_ge(exp_done[par], before(i))
                    v.tensor_reduce(nmax[:, par, :], pS[:], AX_X, ALU.max, negate=True).then_inc(nmax_made[par], 1)
                    v.wait_ge(t_done[par], after(i))
                    v.wait_ge(o_done[par], before(i))
                    v.tensor_copy(probT[:, par], pPT[:]).then_inc(probT_made[par], 1)
                    chain = sem("out_chain")
                    v.wait_ge(o_done[par], after(i))
                    v.reciprocal(rsum[:, par, :], pO[:, :, P]).then_inc(chain, 1)
                    v.wait_ge(chain, 1)
                    v.sem_clear(chain)
                    for qt in range(2):
                        tile = X[:, ds(i * 4 + par * 2 + qt, 1), :]
                        ins = v.scalar_tensor_tensor(tile, pO[:, qt, 0:P].unsqueeze(1), rsum[:, par, qt:qt + 1], tile, ALU.mult, ALU.add)
                    ins.then_inc(x_done[par], 1)

                batches(v, start, end)

            @block.scalar
            def _(act):
                def start(i, par, pi, ppar):
                    act.wait_ge(xT_done[par], after(i))
                    act.wait_ge(v_done[par], before(i))
                    act.copy(xnT[:, par, :], pX[:, 0, :])
                    act.copy(kvT[:, par, :], ctxT[:, ds((i * 2 + par) * T, T)]).then_inc(xnT_made[par], 1)
                    act.wait_ge(v_done[par], after(i))
                    act.wait_ge(o_done[par], before(i))
                    act.copy(vaug[:, par, :, 0:P], pV[:, :, 0:P]).then_inc(v_made[par], 1)
                    act.wait_ge(e_done[par], after(i))
                    act.wait_ge(s_done[par], before(i))
                    act.activation(entT[:, par, :], pE[:, 0, :], ACT.Tanh, bias=bias[:, 3:4]).then_inc(e_made[par], 1)

                def end(i, par):
                    act.wait_ge(nmax_made[par], after(i))
                    act.wait_ge(t_done[par], before(i))
                    for qt in range(2):
                        ins = act.activation(prob[:, par, qt, :], pS[:, qt, :], ACT.Exp, bias=nmax[:, par, qt:qt + 1])
                    ins.then_inc(exp_done[par], 1)

                act.wait_ge(sem("w_in"), 48)
                batches(act, start, end)

            @block.tensor
            def _(pe):
                pe.wait_ge(sem("w_in"), 48)
                pe.wait_ge(sem("ones_made"), 1)

                def start(i, par, pi, ppar):
                    pe.wait_ge(xn_made[par], after(i))
                    if pi is not None:
                        pe.wait_ge(xnT_made[ppar], after(pi))
                        pe.wait_ge(qk_made[ppar], after(pi))
                        pe.wait_ge(vT_made[ppar], after(pi))
                        pe.wait_ge(v_made[ppar], after(pi))
                        pe.wait_ge(e_made[ppar], after(pi))
                    for kt in range(2):
                        ins = pe.transpose(pX[:, 0, kt * P:(kt + 1) * P], xn[:, par, kt, :], ident[:])
                    ins.then_inc(xT_done[par], 1)
                    pe.wait_ge(xnT_made[par], after(i))
                    pe.matmul(pQK[:, 0, :], w[:, 0, :], xnT[:, par, :], start=True, stop=True)
                    pe.matmul(pQK[:, 1, :], w[:, 1, :], kvT[:, par, :], start=True, stop=True).then_inc(qk_done[par], 1)
                    pe.matmul(pVT[:, 0, :], w[:, 2, :], kvT[:, par, :], start=True, stop=True).then_inc(vT_done[par], 1)
                    for kt in range(2):
                        pe.matmul(pV[:, kt, 0:P], kvT[:, par, kt * P:(kt + 1) * P], w[:, 2, :], start=True, stop=False)
                        ins = pe.matmul(pV[:, kt, 0:P], ones[0:1, :], bvrow[:], start=False, stop=True)
                    ins.then_inc(v_done[par], 1)
                    pe.wait_ge(qk_made[par], after(i))
                    pe.matmul(pE[:, 0, :], w[:, 3, :], qkT[:, par, 0, :], start=True, stop=False)
                    pe.matmul(pE[:, 0, :], w[:, 4, :], qkT[:, par, 1, :], start=False, stop=True).then_inc(e_done[par], 1)

                def end(i, par):
                    other, oi = (1, i - 1) if par == 0 else (0, i)
                    pe.wait_ge(e_made[par], after(i))
                    pe.wait_ge(vT_made[par], after(i))
                    pe.wait_ge(exp_done[other], after(oi))
                    for qt in range(2):
                        ins = pe.matmul(pS[:, qt, :], entT[:, par, qt * P:(qt + 1) * P], vT[:, par, :], start=True, stop=True)
                    ins.then_inc(s_done[par], 1)
                    pe.wait_ge(exp_done[par], after(i))
                    pe.wait_ge(probT_made[other], after(oi))
                    for kt in range(2):
                        for qt in range(2):
                            ins = pe.transpose(pPT[:, kt, qt * P:(qt + 1) * P], prob[:, par, qt, kt * P:(kt + 1) * P], ident[:])
                    ins.then_inc(t_done[par], 1)
                    pe.wait_ge(probT_made[par], after(i))
                    pe.wait_ge(v_made[par], after(i))
                    pe.wait_ge(x_done[other], after(oi))
                    for qt in range(2):
                        for kt in range(2):
                            ins = pe.matmul(pO[:, qt, 0:P + 1], probT[:, par, kt, qt * P:(qt + 1) * P], vaug[:, par, kt, :],
                                            start=(kt == 0), stop=(kt == 1))
                    ins.then_inc(o_done[par], 1)

                batches(pe, start, end)

        sem.clear()


NH = 8
HW = 64
K = T // 8
MASKED = -1e30


def route_tokens(nc, stage, X, consts, shared, drams):
    ident = consts["ident"]
    xn_all, xnT_all, slots = shared
    with ExitStack() as ctx:
        def sb(name, shape, dt=F32):
            return ctx.enter_context(nc.sbuf_tensor(f"{stage}r_{name}", shape, dt))

        def bank(name):
            return ctx.enter_context(nc.psum_tensor(f"{stage}r_{name}", [P, 2, T], F32))

        sem = Sems(nc, ctx, stage + "r")
        ROWS = NH * B
        stats = sb("stats", [P, TILES, 6])
        mean = sb("mean", [P, TILES])
        rstd = sb("rstd", [P, TILES])
        lntmp = sb("lntmp", [P, 4, TILES])
        router = sb("router", [P, NH])
        xn = sb("xn", [P, 2, 2, P])
        scores8 = sb("scores8", [NH, B, T])
        scores = sb("scores", [ROWS, T])
        rest = sb("rest", [ROWS, T])
        taken = sb("taken", [ROWS, T])
        onesr = sb("onesr", [ROWS, T])
        slotgate = sb("slotgate", [ROWS, 2, T])
        m8 = sb("m8", [ROWS, 4, 8])
        pX = [bank(f"pX{i}") for i in range(2)]
        pR = [bank(f"pR{i}") for i in range(2)]
        pT = bank("pT")

        def pair(name):
            return [sem(f"{name}{i}") for i in range(2)]

        xn_made, xT_done, xnT_made, r_done, r_made = (pair(n) for n in ("xn_made", "xT_done", "xnT_made", "r_done", "r_made"))

        with nc.Block() as block:
            @block.sync
            def _(sp):
                sp.dma_start(router[:], drams["router"]).then_inc(sem("w_in"), 16)
                for par in range(2):
                    sp.wait_ge(r_made[par], after(B // 2 - 1))
                sp.dma_start(scores[:], scores8[:].rearrange("n b t -> n (b t)")).then_inc(sem("scores_in"), 16)
                sp.wait_ge(sem("scores_in"), 16)

            @block.gpsimd
            def _(pool):
                for s in xn_made + xT_done + xnT_made + r_done + r_made + [sem("kept0"), sem("kept1")]:
                    pool.sem_inc(s, 1)
                pool.memset(onesr[:], 1.0).then_inc(sem("ones_made"), 1)
                with pool.Fori(0, B // 2) as i:
                    for par in range(2):
                        pool.wait_ge(xn_made[par], after(i))
                        pool.tensor_copy(xn_all[:, ds(i * 4 + par * 2, 2), :], xn[:, par]).then_inc(sem(f"kept{par}"), 1)

            @block.vector
            def _(v):
                layernorm_stats(v, sem, X, stats, mean, rstd, lntmp)
                with v.Fori(0, B // 2) as i:
                    for par in range(2):
                        v.wait_ge(xT_done[par], before(i))
                        v.wait_ge(sem(f"kept{par}"), before(i))
                        for kt in range(2):
                            tile = i * 4 + par * 2 + kt
                            ins = v.tensor_scalar(xn[:, par, kt, :], X[:, ds(tile, 1), :], mean[:, ds(tile, 1)],
                                                  rstd[:, ds(tile, 1)], ALU.subtract, ALU.mult)
                        ins.then_inc(xn_made[par], 1)
                chain = sem("topk_chain")
                n = [0]

                def step(ins):
                    n[0] += 1
                    ins.then_inc(chain, 1)
                    v.wait_ge(chain, n[0])

                v.wait_ge(sem("scores_in"), 16)
                src = scores
                for rnd in range(K // 8):
                    step(v.max(m8[:, rnd, :], src[:]))
                    step(v.match_replace(rest[:], m8[:, rnd, :], src[:], LOW))
                    src = rest
                step(v.tensor_scalar(taken[:], rest[:], LOW, None, ALU.is_equal))
                v.wait_ge(sem("ones_made"), 1)
                step(v.tensor_tensor_scan(slotgate[:, 0, :], onesr[:], taken[:], 0.0, ALU.mult, ALU.add))
                v.tensor_tensor(slotgate[:, 0, :], slotgate[:, 0, :], taken[:], ALU.mult).then_inc(sem("slots_made"), 1)
                v.wait_ge(sem("tanh_made"), 1)
                v.tensor_scalar(slotgate[:, 1, :], scores[:], 0.5, 0.5, ALU.mult, ALU.add).then_inc(sem("slots_made"), 1)
                v.wait_ge(sem("slots_transposed"), 1)
                v.tensor_copy(slots[:], pT[:].rearrange("p a (k r) -> p (a k r)", k=4)[:, 0:4 * ROWS].rearrange("p (k r) -> p k r", r=ROWS))

            @block.scalar
            def _(act):
                with act.Fori(0, B // 2) as i:
                    for par in range(2):
                        act.wait_ge(xT_done[par], after(i))
                        act.copy(xnT_all[:, ds((i * 2 + par) * T, T)], pX[par][:, 0, :]).then_inc(xnT_made[par], 1)
                    for par in range(2):
                        act.wait_ge(r_done[par], after(i))
                        act.copy(scores8[:, ds(i * 2 + par, 1), :], pR[par][0:NH, 0, :].unsqueeze(1)).then_inc(r_made[par], 1)
                act.wait_ge(sem("slots_made"), 1)
                act.activation(scores[:], scores[:], ACT.Tanh, scale=0.5).then_inc(sem("tanh_made"), 1)

            @block.tensor
            def _(pe):
                pe.wait_ge(sem("w_in"), 16)
                with pe.Fori(0, B // 2) as i:
                    for par in range(2):
                        pe.wait_ge(xn_made[par], after(i))
                        pe.wait_ge(xnT_made[par], before(i))
                        for kt in range(2):
                            ins = pe.transpose(pX[par][:, 0, kt * P:(kt + 1) * P], xn[:, par, kt, :], ident[:])
                        ins.then_inc(xT_done[par], 1)
                    for par in range(2):
                        pe.wait_ge(xnT_made[par], after(i))
                        pe.wait_ge(r_made[par], before(i))
                        pe.matmul(pR[par][0:NH, 0, :], router[:], xnT_all[:, ds((i * 2 + par) * T, T)], start=True, stop=True)\
                            .then_inc(r_done[par], 1)
                pe.wait_ge(sem("slots_made"), 2)
                flat = pT[:].rearrange("p a t -> p (a t)")
                for a in range(2):
                    for kt in range(2):
                        at = (a * 2 + kt) * ROWS
                        ins = pe.transpose(flat[:, at:at + ROWS], slotgate[:, a, kt * P:(kt + 1) * P], ident[0:ROWS, 0:ROWS])
                ins.then_inc(sem("slots_transposed"), 1)

        sem.clear()


def dense_heads(nc, stage, X, consts, shared, drams):
    ident = consts["ident"]
    xn_all, xnT_all, slots = shared
    HP = NH // 2
    with ExitStack() as ctx:
        def sb(name, shape, dt=F32):
            return ctx.enter_context(nc.sbuf_tensor(f"{stage}d_{name}", shape, dt))

        def bank(name, shape=(P, 2, T)):
            return ctx.enter_context(nc.psum_tensor(f"{stage}d_{name}", list(shape), F32))

        sem = Sems(nc, ctx, stage + "d")
        w = sb("w", [P, 5, HP, P])
        wo = sb("wo", [P, HP, P])
        rope = sb("rope", [P, 4, T])
        identb = sb("identb", [P, P], BF16)
        causal = sb("causal", [P, P], BF16)
        xb = sb("xb", [P, T])
        r = sb("r", [P, 2, 2, T])
        r2 = sb("r2", [P, 2, 2, T])
        vaug = sb("vaug", [P, 2, 2, 2, HW + 1])
        nmax = sb("nmax", [P, 2, 2, 2])
        prob = sb("prob", [P, 2, 2, 2, T])
        probT = sb("probT", [P, 2, 3, P])
        rsum = sb("rsum", [P, 2, 2, 2])
        on = sb("on", [P, 2, HP, 2, HW])
        onT = sb("onT", [P, 2, HP, P])
        pA, pC, pV, pPT, pO, pM = (bank(n) for n in ("pA", "pC", "pV", "pPT", "pO", "pM"))
        pS = bank("pS", (P, 2, 2, T))

        def pair(name):
            return [sem(f"{name}{i}") for i in range(2)]

        names = ("qk_done", "r_made", "v_done", "v_made", "s_done", "nmax_made", "exp_done", "t0_done", "t1_done",
                 "probT0_made", "probT1_made", "o_done", "on_made")
        made = {n: pair(n) for n in names}
        (qk_done, r_made, v_done, v_made, s_done, nmax_made, exp_done, t0_done, t1_done, probT0_made, probT1_made,
         o_done, on_made) = (made[n] for n in names)
        t_done, probT_made = (t0_done, t1_done), (probT0_made, probT1_made)
        batch_names = ("xb_made", "oT0_done", "oT1_done", "onT0_made", "onT1_made", "y_done", "x_done")
        bmade = {n: sem(n) for n in batch_names}
        xb_made, oT0_done, oT1_done, onT0_made, onT1_made, y_done, x_done = (bmade[n] for n in batch_names)
        BLOCKS = ((0, 0), (0, 1), (1, 1))

        def units(eng, start, end, finish, begin=None):
            with eng.Fori(0, B) as b:
                def at(hp):
                    return b, hp, b * 2 + hp // 2, hp % 2
                if begin:
                    begin(b)
                start(*at(0))
                for hp in range(1, HP):
                    start(*at(hp))
                    end(*at(hp - 1))
                end(*at(HP - 1))
                finish(b)

        def last(i, par):
            return (i - 1, 1) if par == 0 else (i, 0)

        with nc.Block() as block:
            @block.sync
            def _(sp):
                sp.dma_start(w[:], drams["dense_w"]).then_inc(sem("w_in"), 16)
                sp.dma_start(wo[:], drams["dense_wo"]).then_inc(sem("w_in"), 16)
                sp.dma_start(rope[:], drams["dense_rope"]).then_inc(sem("w_in"), 16)

            @block.gpsimd
            def _(pool):
                for s in sum(made.values(), []) + list(bmade.values()):
                    pool.sem_inc(s, 1)
                c = sem("mask_made")
                pool.memset(causal[:], 0.0).then_inc(c, 1)
                pool.memset(vaug[:, :, :, :, HW:HW + 1], 1.0).then_inc(c, 1)
                pool.tensor_copy(identb[:], ident[:]).then_inc(c, 1)
                pool.wait_ge(c, 3)
                pool.affine_select(out=causal[:], in_=causal[:], compare_op=ALU.is_ge, fill=MASKED, base=0,
                                   pattern=[[-1, P]], channel_multiplier=1).then_inc(c, 1)
                with pool.Fori(0, B) as b:
                    pool.wait_ge(v_done[1], b * 2 + 1)
                    pool.tensor_copy(xb[:], xnT_all[:, ds(b * T, T)]).then_inc(xb_made, 1)

            @block.vector
            def _(v):
                v.wait_ge(sem("w_in"), 48)
                chain = sem("rope_chain")
                ochain = sem("out_chain")

                def start(b, hp, i, par):
                    v.wait_ge(qk_done[par], after(i))
                    v.wait_ge(s_done[par], before(i))
                    v.tensor_tensor(r[:, par], pA[:], rope[:, 0:2, :], ALU.mult).then_inc(chain, 1)
                    v.tensor_tensor(r2[:, par], pC[:], rope[:, 2:4, :], ALU.mult).then_inc(chain, 1)
                    v.wait_ge(chain, 2)
                    v.sem_clear(chain)
                    v.tensor_tensor(r[:, par], r[:, par], r2[:, par], ALU.add).then_inc(r_made[par], 1)

                def end(b, hp, i, par):
                    v.wait_ge(s_done[par], after(i))
                    v.wait_ge(exp_done[par], before(i))
                    v.tensor_reduce(nmax[:, par, 0, :], pS[:, :, 0, 0:P], AX_X, ALU.max, negate=True)
                    v.tensor_reduce(nmax[:, par, 1, :], pS[:, :, 1, :], AX_X, ALU.max, negate=True).then_inc(nmax_made[par], 1)
                    li, lp = last(i, par)
                    v.wait_ge(t_done[0][par], after(i))
                    v.wait_ge(o_done[lp], after(li))
                    v.tensor_copy(probT[:, 0], pPT[:].rearrange("p a t -> p (a t)")[:, 0:3 * P].rearrange("p (k q) -> p k q", k=3))\
                        .then_inc(probT_made[0][par], 1)
                    v.wait_ge(o_done[par], after(i))
                    v.wait_ge(oT1_done, b + 1)
                    o = pO[:].rearrange("p a t -> p (a t)")[:, 0:4 * (HW + 1)].rearrange("p (q x d) -> p q x d", q=2, x=2)
                    v.reciprocal(rsum[:, par], o[:, :, :, HW]).then_inc(ochain, 1)
                    v.wait_ge(ochain, 1)
                    v.sem_clear(ochain)
                    v.tensor_tensor(on[:, :, hp], o[:, :, :, 0:HW], rsum[:, par].unsqueeze(3).broadcast_to([P, 2, 2, HW]),
                                    ALU.mult).then_inc(on_made[par], 1)

                def finish(b):
                    v.wait_ge(oT1_done, after(b))
                    v.wait_ge(y_done, before(b))
                    v.tensor_copy(onT[:, 1], pPT[:].rearrange("p a (k q) -> p (a k) q", k=2)).then_inc(onT1_made, 1)
                    v.wait_ge(y_done, after(b))
                    v.tensor_tensor(X[:, ds(b * 2, 2), :], X[:, ds(b * 2, 2), :], pM[:, :, 0:P], ALU.add).then_inc(x_done, 1)

                units(v, start, end, finish)

            @block.scalar
            def _(act):
                def start(b, hp, i, par):
                    act.wait_ge(v_done[par], after(i))
                    act.wait_ge(o_done[par], before(i))
                    act.copy(vaug[:, par, :, :, 0:HW], pV[:, :, 0:P].rearrange("p k (x d) -> p k x d", x=2)).then_inc(v_made[par], 1)

                def end(b, hp, i, par):
                    act.wait_ge(nmax_made[par], after(i))
                    act.wait_ge(t_done[1][par], before(i))
                    for x in range(2):
                        for qt in range(2):
                            n = (qt + 1) * P
                            ins = act.activation(prob[:, par, x, qt, 0:n], pS[:, x, qt, 0:n], ACT.Exp, bias=nmax[:, par, qt, x:x + 1])
                    ins.then_inc(exp_done[par], 1)
                    li, lp = last(i, par)
                    act.wait_ge(t_done[1][par], after(i))
                    act.wait_ge(o_done[lp], after(li))
                    act.copy(probT[:, 1], pPT[:].rearrange("p a t -> p (a t)")[:, 0:3 * P].rearrange("p (k q) -> p k q", k=3))\
                        .then_inc(probT_made[1][par], 1)

                def finish(b):
                    act.wait_ge(oT0_done, after(b))
                    act.wait_ge(y_done, before(b))
                    act.copy(onT[:, 0], pM[:].rearrange("p a (k q) -> p (a k) q", k=2)).then_inc(onT0_made, 1)

                units(act, start, end, finish)

            @block.tensor
            def _(pe):
                pe.wait_ge(sem("w_in"), 48)
                pe.wait_ge(sem("mask_made"), 4)

                def start(b, hp, i, par):
                    li, lp = last(i, par)
                    if hp == 0:
                        pe.wait_ge(xb_made, after(b))
                    pe.wait_ge(r_made[lp], after(li))
                    for s in range(2):
                        pe.matmul(pA[:, s, :], w[:, 2 * s, hp, :], xb[:], start=True, stop=True)
                        ins = pe.matmul(pC[:, s, :], w[:, 2 * s + 1, hp, :], xb[:], start=True, stop=True)
                    ins.then_inc(qk_done[par], 1)
                    pe.wait_ge(v_made[lp], after(li))
                    for kt in range(2):
                        ins = pe.matmul(pV[:, kt, 0:P], xb[:, kt * P:(kt + 1) * P], w[:, 4, hp, :], start=True, stop=True)
                    ins.then_inc(v_done[par], 1)

                def end(b, hp, i, par):
                    li, lp = last(i, par)
                    pe.wait_ge(r_made[par], after(i))
                    pe.wait_ge(exp_done[lp], after(li))
                    for x in range(2):
                        rows = slice(x * HW, (x + 1) * HW)
                        for qt in range(2):
                            n = (qt + 1) * P
                            q = r[rows, par, 0, qt * P:(qt + 1) * P]
                            if qt:
                                pe.matmul(pS[:, x, qt, 0:P], q, r[rows, par, 1, 0:P], start=True, stop=True)
                            pe.matmul(pS[:, x, qt, n - P:n], q, r[rows, par, 1, n - P:n], start=True, stop=False)
                            ins = pe.matmul(pS[:, x, qt, n - P:n], identb[:], causal[:], start=False, stop=True)
                    ins.then_inc(s_done[par], 1)
                    pe.wait_ge(exp_done[par], after(i))
                    flat = pPT[:].rearrange("p a t -> p (a t)")
                    for x in range(2):
                        if x == 0:
                            pe.wait_ge(probT_made[1][lp], after(li))
                            if hp == 0:
                                pe.wait_ge(onT1_made, before(b))
                        else:
                            pe.wait_ge(probT_made[0][par], after(i))
                        for j, (kt, qt) in enumerate(BLOCKS):
                            ins = pe.transpose(flat[:, j * P:(j + 1) * P], prob[:, par, x, qt, kt * P:(kt + 1) * P], ident[:])
                        ins.then_inc(t_done[x][par], 1)
                    pe.wait_ge(v_made[par], after(i))
                    pe.wait_ge(on_made[lp], after(li))
                    o = pO[:].rearrange("p a t -> p (a t)")[:, 0:4 * (HW + 1)].rearrange("p (q x d) -> p q x d", q=2, x=2)
                    for x in range(2):
                        pe.wait_ge(probT_made[x][par], after(i))
                        pe.matmul(o[:, 0, x, :], probT[:, x, 0, :], vaug[:, par, 0, x, :], start=True, stop=True)
                        pe.matmul(o[:, 1, x, :], probT[:, x, 1, :], vaug[:, par, 0, x, :], start=True, stop=False)
                        ins = pe.matmul(o[:, 1, x, :], probT[:, x, 2, :], vaug[:, par, 1, x, :], start=False, stop=True)
                    ins.then_inc(o_done[par], 1)

                def finish(b):
                    pe.wait_ge(on_made[1], b * 2 + 3)
                    pe.wait_ge(x_done, before(b))
                    for qt, (dst, done) in enumerate(((pM, oT0_done), (pPT, oT1_done))):
                        flat = dst[:].rearrange("p a t -> p (a t)")
                        for hp in range(HP):
                            ins = pe.transpose(flat[:, hp * P:(hp + 1) * P], on[:, qt, hp].rearrange("p x d -> p (x d)"), ident[:])
                        ins.then_inc(done, 1)
                    pe.wait_ge(onT0_made, after(b))
                    pe.wait_ge(onT1_made, after(b))
                    for qt in range(2):
                        for hp in range(HP):
                            ins = pe.matmul(pM[:, qt, 0:P], onT[:, qt, hp, :], wo[:, hp, :], start=(hp == 0), stop=(hp == HP - 1))
                    ins.then_inc(y_done, 1)

                units(pe, start, end, finish)

        sem.clear()


def sparse_heads(nc, stage, X, consts, shared, drams):
    ident = consts["ident"]
    xn_all, xnT_all, slots = shared
    with ExitStack() as ctx:
        def sb(name, shape, dt=F32):
            return ctx.enter_context(nc.sbuf_tensor(f"{stage}m_{name}", shape, dt))

        def bank(name):
            return ctx.enter_context(nc.psum_tensor(f"{stage}m_{name}", [P, 2, T], F32))

        sem = Sems(nc, ctx, stage + "m")
        w = sb("w", [P, NH, 5, HW])
        wo = sb("wo", [HW, NH, P])
        rope = sb("rope", [P, 2, 2, HW])
        slot_no = sb("slot_no", [P, K])
        identb = sb("identb", [P, P], BF16)
        mask = sb("mask", [P, P], BF16)
        xs = sb("xs", [P, 2, P])
        pick = sb("pick", [P, 2, NH, K])
        gated = sb("gated", [P, 2, NH, K])
        xgT = sb("xgT", [P, NH * K])
        tg = sb("tg", [HW, 2, NH * K])
        r = sb("r", [HW, 2, NH * K])
        r2 = sb("r2", [HW, 2, NH * K])
        vaug = sb("vaug", [P, 2, HW + 1])
        nmax = sb("nmax", [P, 2])
        prob = sb("prob", [P, 2, P])
        probT = sb("probT", [P, 2, P])
        rsum = sb("rsum", [P, 2])
        av = sb("av", [P, 2, HW])
        avT = sb("avT", [HW, 2, P])
        z = sb("z", [P, 2, P])
        gT = sb("gT", [P, 2, T])
        pG, pQ, pQs, pV, pS, pT, pO, pY = (bank(n) for n in ("pG", "pQ", "pQs", "pV", "pS", "pT", "pO", "pY"))
        names = ("xs_made", "pick_made", "gated_made", "xg_done", "xg_made", "tg_done", "tg_made", "q_done", "r_made", "v_done", "v_made",
                 "s_done", "nmax_made", "exp_done", "t_done", "probT_made", "o_done", "av_made", "avT_done", "avT_made",
                 "z_done", "z_made", "gT_done", "gT_made", "y_done", "x_done")
        made = {n: sem(n) for n in names}

        with nc.Block() as block:
            @block.sync
            def _(sp):
                sp.dma_start(w[:], drams["mosa_w"]).then_inc(sem("w_in"), 16)
                sp.dma_start(wo[:], drams["mosa_wo"]).then_inc(sem("w_in"), 16)
                sp.dma_start(rope[:], drams["mosa_rope"]).then_inc(sem("w_in"), 16)

            @block.gpsimd
            def _(pool):
                for s in made.values():
                    pool.sem_inc(s, 1)
                c = sem("mask_made")
                pool.memset(mask[:], 0.0).then_inc(c, 1)
                pool.memset(vaug[:, :, HW:HW + 1], 1.0).then_inc(c, 1)
                pool.tensor_copy(identb[:], ident[:]).then_inc(c, 1)
                pool.iota(slot_no[:], pattern=[[1, K]], base=1, channel_multiplier=0,
                          allow_small_or_imprecise_dtypes=True).then_inc(c, 1)
                pool.wait_ge(c, 4)
                pool.affine_select(out=mask[:], in_=mask[:], compare_op=ALU.is_ge, fill=MASKED, base=0,
                                   pattern=[[-1, P]], channel_multiplier=1).then_inc(c, 1)
                pool.wait_ge(c, 5)
                pool.affine_select(out=mask[:].rearrange("p (h k) -> p h k", k=K), in_=mask[:].rearrange("p (h k) -> p h k", k=K),
                                   compare_op=ALU.is_ge, fill=MASKED, base=K - 1,
                                   pattern=[[K, P // K], [0, K]], channel_multiplier=-1).then_inc(c, 1)
                with pool.Fori(0, B) as b:
                    pool.wait_ge(made["xg_done"], before(b))
                    pool.tensor_copy(xs[:], xn_all[:, ds(b * 2, 2), :]).then_inc(made["xs_made"], 1)

            @block.vector
            def _(v):
                v.wait_ge(sem("w_in"), 48)
                v.wait_ge(sem("mask_made"), 6)
                chain = sem("rope_chain")
                ochain = sem("out_chain")
                with v.Fori(0, B) as b:
                    v.wait_ge(made["tg_done"], before(b))
                    sl = slots[:].rearrange("p k (n b) -> p k n b", b=B)[:, :, :, ds(b, 1)]
                    v.tensor_tensor(pick[:], sl[:, 0:2].broadcast_to([P, 2, NH, K]),
                                    slot_no[:].unsqueeze(1).unsqueeze(1).broadcast_to([P, 2, NH, K]), ALU.is_equal)\
                        .then_inc(made["pick_made"], 1)
                    v.wait_ge(made["gT_done"], before(b))
                    v.wait_ge(made["pick_made"], after(b))
                    v.tensor_tensor(gated[:], pick[:], sl[:, 2:4].broadcast_to([P, 2, NH, K]), ALU.mult)\
                        .then_inc(made["gated_made"], 1)
                    v.wait_ge(made["tg_done"], after(b))
                    v.tensor_copy(tg[:], pS[0:HW, :, :]).then_inc(made["tg_made"], 1)
                    v.wait_ge(made["q_done"], after(b))
                    v.wait_ge(made["tg_made"], after(b))
                    q = HW ** -0.5
                    v.scalar_tensor_tensor(r[:, 0, :], pQ[0:HW, 0, :], q, tg[:, 0, :], ALU.mult, ALU.mult).then_inc(chain, 1)
                    v.tensor_tensor(r[:, 1, :], pQ[0:HW, 1, :], tg[:, 0, :], ALU.mult).then_inc(chain, 1)
                    v.scalar_tensor_tensor(r2[:, 0, :], pQs[0:HW, 0, :], q, tg[:, 1, :], ALU.mult, ALU.mult).then_inc(chain, 1)
                    v.tensor_tensor(r2[:, 1, :], pQs[0:HW, 1, :], tg[:, 1, :], ALU.mult).then_inc(chain, 1)
                    v.wait_ge(chain, 4)
                    v.sem_clear(chain)
                    v.tensor_tensor(r[:], r[:], r2[:], ALU.add).then_inc(made["r_made"], 1)
                    v.wait_ge(made["s_done"], after(b))
                    v.tensor_reduce(nmax[:], pS[:, :, 0:P], AX_X, ALU.max, negate=True).then_inc(made["nmax_made"], 1)
                    v.wait_ge(made["t_done"], after(b))
                    v.tensor_copy(probT[:], pT[:, :, 0:P]).then_inc(made["probT_made"], 1)
                    v.wait_ge(made["o_done"], after(b))
                    v.reciprocal(rsum[:], pO[:, :, HW]).then_inc(ochain, 1)
                    v.wait_ge(ochain, 1)
                    v.sem_clear(ochain)
                    v.tensor_tensor(av[:], pO[:, :, 0:HW], rsum[:].unsqueeze(2).broadcast_to([P, 2, HW]), ALU.mult).then_inc(made["av_made"], 1)
                    v.wait_ge(made["avT_done"], after(b))
                    v.tensor_copy(avT[:], pT[0:HW, :, 0:P]).then_inc(made["avT_made"], 1)
                    v.wait_ge(made["y_done"], after(b))
                    v.tensor_tensor(X[:, ds(b * 2, 2), :], X[:, ds(b * 2, 2), :], pY[:, :, 0:P], ALU.add).then_inc(made["x_done"], 1)

            @block.scalar
            def _(act):
                with act.Fori(0, B) as b:
                    act.wait_ge(made["xg_done"], after(b))
                    act.wait_ge(made["v_done"], before(b))
                    act.copy(xgT[:], pG[:, 0, :]).then_inc(made["xg_made"], 1)
                    act.wait_ge(made["v_done"], after(b))
                    act.wait_ge(made["o_done"], before(b))
                    act.copy(vaug[:, :, 0:HW], pV[:, :, 0:HW]).then_inc(made["v_made"], 1)
                    act.wait_ge(made["gT_done"], after(b))
                    act.wait_ge(made["y_done"], before(b))
                    act.copy(gT[:], pY[:]).then_inc(made["gT_made"], 1)
                    act.wait_ge(made["nmax_made"], after(b))
                    for g in range(2):
                        ins = act.activation(prob[:, g, :], pS[:, g, 0:P], ACT.Exp, bias=nmax[:, g:g + 1])
                    ins.then_inc(made["exp_done"], 1)
                    act.wait_ge(made["z_done"], after(b))
                    act.copy(z[:], pG[:, :, 0:P]).then_inc(made["z_made"], 1)

            @block.tensor
            def _(pe):
                pe.wait_ge(sem("w_in"), 48)
                pe.wait_ge(sem("mask_made"), 6)
                with pe.Fori(0, B) as b:
                    pe.wait_ge(made["xs_made"], after(b))
                    pe.wait_ge(made["pick_made"], after(b))
                    pe.wait_ge(made["z_made"], before(b))
                    for kt in range(2):
                        ins = pe.matmul(pG[:, 0, :], xs[:, kt, :], pick[:, kt], start=(kt == 0), stop=(kt == 1))
                    ins.then_inc(made["xg_done"], 1)
                    pe.wait_ge(made["exp_done"], before(b))
                    for a in range(2):
                        for kt in range(2):
                            ins = pe.matmul(pS[0:HW, a, :], rope[:, kt, a, :], pick[:, kt], start=(kt == 0), stop=(kt == 1))
                    ins.then_inc(made["tg_done"], 1)
                    pe.wait_ge(made["gated_made"], after(b))
                    pe.wait_ge(made["x_done"], before(b))
                    for g in range(2):
                        for kt in range(2):
                            ins = pe.transpose(pY[:, g, kt * P:(kt + 1) * P],
                                               gated[:, kt, g * 4:(g + 1) * 4].rearrange("p n k -> p (n k)"), ident[:])
                    ins.then_inc(made["gT_done"], 1)
                    pe.wait_ge(made["xg_made"], after(b))
                    for n in range(NH):
                        xg = xgT[:, n * K:(n + 1) * K]
                        for s in range(2):
                            pe.matmul(pQ[0:HW, s, n * K:(n + 1) * K], w[:, n, 2 * s, :], xg, start=True, stop=True)
                            ins = pe.matmul(pQs[0:HW, s, n * K:(n + 1) * K], w[:, n, 2 * s + 1, :], xg, start=True, stop=True)
                    ins.then_inc(made["q_done"], 1)
                    pe.wait_ge(made["v_made"], before(b))
                    for n in range(NH):
                        rows = slice(n % 4 * K, n % 4 * K + K)
                        ins = pe.matmul(pV[rows, n // 4, 0:HW], xgT[:, n * K:(n + 1) * K], w[:, n, 4, :], start=True, stop=True,
                                        skip_group_check=True)
                    ins.then_inc(made["v_done"], 1)
                    pe.wait_ge(made["r_made"], after(b))
                    for g in range(2):
                        cols = slice(g * P, (g + 1) * P)
                        pe.matmul(pS[:, g, 0:P], r[:, 0, cols], r[:, 1, cols], start=True, stop=False)
                        ins = pe.matmul(pS[:, g, 0:P], identb[:], mask[:], start=False, stop=True)
                    ins.then_inc(made["s_done"], 1)
                    pe.wait_ge(made["exp_done"], after(b))
                    pe.wait_ge(made["avT_made"], before(b))
                    for g in range(2):
                        ins = pe.transpose(pT[:, g, 0:P], prob[:, g, :], ident[:])
                    ins.then_inc(made["t_done"], 1)
                    pe.wait_ge(made["probT_made"], after(b))
                    pe.wait_ge(made["v_made"], after(b))
                    pe.wait_ge(made["av_made"], before(b))
                    for g in range(2):
                        ins = pe.matmul(pO[:, g, 0:HW + 1], probT[:, g, :], vaug[:, g, :], start=True, stop=True)
                    ins.then_inc(made["o_done"], 1)
                    pe.wait_ge(made["av_made"], after(b))
                    pe.sem_inc(sem("waited_pe"), 1)
                    for g in range(2):
                        ins = pe.transpose(pT[0:HW, g, 0:P], av[:, g, :], ident[:])
                    ins.then_inc(made["avT_done"], 1)
                    pe.wait_ge(made["avT_made"], after(b))
                    pe.sem_inc(sem("waited_pe"), 1)
                    for n in range(NH):
                        rows = slice(n % 4 * K, n % 4 * K + K)
                        ins = pe.matmul(pG[rows, n // 4, 0:P], avT[:, n // 4, rows], wo[:, n, :], start=True, stop=True,
                                        skip_group_check=True)
                    ins.then_inc(made["z_done"], 1)
                    pe.wait_ge(made["z_made"], after(b))
                    pe.wait_ge(made["gT_made"], after(b))
                    for qt in range(2):
                        for g in range(2):
                            ins = pe.matmul(pY[:, qt, 0:P], gT[:, g, qt * P:(qt + 1) * P], z[:, g, :], start=(g == 0), stop=(g == 1))
                    ins.then_inc(made["y_done"], 1)

        sem.clear()


def mixed_attention(nc, stage, X, consts, drams):
    with ExitStack() as ctx:
        shared = (
            ctx.enter_context(nc.sbuf_tensor("xn_all", [P, TILES, P], F32)),
            ctx.enter_context(nc.sbuf_tensor("xnT_all", [P, B * T], F32)),
            ctx.enter_context(nc.sbuf_tensor("slots", [P, 4, NH * B], F32)),
        )
        route_tokens(nc, stage, X, consts, shared, drams)
        dense_heads(nc, stage, X, consts, shared, drams)
        sparse_heads(nc, stage, X, consts, shared, drams)


def build(nc, ins, out, stages=(1, 2, 3, 4, 5, 6)):
    with ExitStack() as ctx:
        def sb(name, shape, dt=F32):
            return ctx.enter_context(nc.sbuf_tensor(name, shape, dt))

        X = sb("X", [P, TILES, P])
        ctxT = sb("ctxT", [P, B * T])
        ident = sb("ident", [P, P])
        ones = sb("ones", [P, P])
        stack_ctx = ExitStack()
        qs = stack_ctx.enter_context(nc.sbuf_tensor("qs", [P, UNITS + 2, T], BF16))
        ks = stack_ctx.enter_context(nc.sbuf_tensor("ks", [P, UNITS + 2, T], BF16))
        zeros_ctx = ExitStack()
        zeros = zeros_ctx.enter_context(nc.sbuf_tensor("zeros", [P, H * T], BF16))
        loaded, made, zeroed = (ctx.enter_context(nc.semaphore(n)) for n in ("loaded", "consts_made", "zeroed"))
        consts = {"ident": ident, "ones": ones, "qs": qs, "ks": ks, "zeroed": zeroed, "zeroed_by": 16 * 2 * (B + 1)}
        with nc.Block() as block:
            @block.sync
            def _(sp):
                sp.dma_start(X[:], ins["x"].rearrange("(t p) d -> p t d", p=P)).then_inc(loaded, 16)
                sp.dma_start(ctxT[:], ins["ctxT"]).then_inc(loaded, 16)
                sp.wait_ge(made, 1)
                for stack in (qs, ks):
                    for b in range(B):
                        sp.dma_start(stack[DH * len(TERMS):KROWS, b * H:(b + 1) * H, :],
                                     zeros[DH * len(TERMS):KROWS, :]).then_inc(zeroed, 16)
                    sp.dma_start(stack[0:KROWS, UNITS:, :], zeros[0:KROWS, 0:2 * T]).then_inc(zeroed, 16)
                sp.wait_ge(loaded, 32)
                if 1 not in stages:
                    sp.wait_ge(zeroed, consts["zeroed_by"])

            @block.gpsimd
            def _(pool):
                pool.memset(zeros[:].bitcast(F32), 0.0).then_inc(made, 1)
                pool.memset(ident[:], 0.0).then_inc(made, 1)
                pool.memset(ones[:], 1.0).then_inc(made, 1)
                pool.wait_ge(made, 3)
                pool.affine_select(out=ident[:], in_=ident[:], compare_op=ALU.not_equal, fill=1.0, base=0,
                                   pattern=[[-1, P]], channel_multiplier=1).then_inc(made, 1)

        if 1 in stages:
            head_attention(nc, "s1", X, None, consts, (ins["w1"], None, None, ins["rope1"]), False)
        zeros_ctx.close()
        if 2 in stages:
            head_attention(nc, "s2", X, ctxT, consts, (ins["w2"], ins["b2"], ins["bo2"], ins["rope2"]), False)
        if 3 in stages:
            tree_ffn(nc, "s3", X, consts, (ins["win"], ins["bin"], ins["wout"]))
        if 4 in stages:
            head_attention(nc, "s4", X, None, consts, (ins["w4"], ins["b4"], ins["bo4"], None), True)
        stack_ctx.close()
        if 5 in stages:
            entangled_attention(nc, "s5", X, ctxT, consts, (ins["w5"], ins["b5"], ins["bv5"]))
        if 6 in stages:
            mixed_attention(nc, "s6", X, consts, {k: ins[k] for k in (
                "router", "dense_w", "dense_wo", "dense_rope", "mosa_w", "mosa_wo", "mosa_rope")})

        stored = ctx.enter_context(nc.semaphore("stored"))
        with nc.Block() as block:
            @block.sync
            def _(sp):
                sp.dma_start(out.rearrange("(t p) d -> p t d", p=P), X[:]).then_inc(stored, 16)
                sp.wait_ge(stored, 16)


def swap_pairs(w):
    return w.reshape(w.shape[0], -1, 2)[:, :, ::-1].reshape(w.shape)


def swap_halves(w, d):
    return w.reshape(w.shape[0], -1, 2, d // 2)[:, :, ::-1].reshape(w.shape)


def by_width(w):
    return w.reshape(w.shape[:-1] + (H, DH)).swapaxes(-1, -2).reshape(w.shape)


def rope_tables(angles, signs):
    cos = np.cos(angles).astype(np.float32)
    sin = (np.sin(angles) * signs).astype(np.float32)
    scale = np.float32(DH ** -0.5)
    return by_width(np.stack([cos * scale, cos, sin * scale, sin], axis=0)).transpose(2, 0, 1)


def lay_out(x):
    f = np.float32
    a = {k: np.asarray(v) for k, v in x.items()}
    o = {"x": a["x"].reshape(B * T, P), "ctxT": a["ctx_1024"].reshape(B * T, P).T}
    pos = np.arange(T, dtype=f)[:, None]
    f1 = np.exp(-np.float32(np.log(10000.0)) * np.arange(0, DH, 2, dtype=f) / DH).astype(f)
    ang1 = np.tile(np.repeat((pos * f1).astype(f), 2, axis=1), (1, H))
    o["rope1"] = rope_tables(ang1, np.tile([-1, 1], P // 2).astype(f))
    f2 = (1.0 / 10000.0 ** (np.arange(0, DH, 2, dtype=f) / DH)).astype(f)
    ang2 = np.tile((pos * np.concatenate([f2, f2])).astype(f), (1, H))
    o["rope2"] = rope_tables(ang2, np.tile(np.repeat([-1, 1], DH // 2), H).astype(f))

    def weights(q, k, v, out, swap):
        return np.stack([by_width(q.T), by_width(swap(q.T)), by_width(k.T), by_width(swap(k.T)), v.T, out.T], axis=1)

    def rows(q, k, v, swap):
        return np.stack([by_width(q), by_width(swap(q[None])[0]), by_width(k), by_width(swap(k[None])[0]), v], axis=1)

    def per_head(w):
        return np.repeat(w.reshape((4, DH) + w.shape[1:]), 4, axis=0).reshape((P,) + w.shape[1:])

    halves = lambda w: swap_halves(w, DH)
    o["w1"] = weights(a["L0_attn_W_q"], a["L0_attn_W_k"], a["L0_attn_W_v"], a["L0_attn_W_o"], swap_pairs)
    o["w2"] = weights(a["L0_xattn_Wq"], per_head(a["L0_xattn_Wk"]), per_head(a["L0_xattn_Wv"]), a["L0_xattn_Wo"], halves)
    o["b2"] = rows(a["L0_xattn_bq"], per_head(a["L0_xattn_bk"]), per_head(a["L0_xattn_bv"]), halves)
    o["bo2"] = a["L0_xattn_bo"][None]
    node = [2 ** d - 1 + sum(((pos >> k) & 1) << (d - 1 - k) for k in range(d)) for d in range(DEPTH + 1) for pos in range(2 ** d)]
    order = (np.arange(TREES)[None, :] * NODES + np.array(node)[:, None]).reshape(-1)
    o["win"] = a["L0_ffn_W_in"][order].T
    o["bin"] = a["L0_ffn_b_in"][order][None]
    o["wout"] = a["L0_ffn_W_out"][:, order].T
    o["w4"] = weights(a["L1_attn_Wq"], a["L1_attn_Wk"], a["L1_attn_Wv"], a["L1_attn_Wo"], halves)
    o["b4"] = rows(a["L1_attn_bq"], a["L1_attn_bk"], a["L1_attn_bv"], halves)
    o["bo4"] = a["L1_attn_bo"][None]
    we = a["L1_xattn_We"]
    o["w5"] = np.stack([a["L1_xattn_Wq"].T, a["L1_xattn_Wk"].T, a["L1_xattn_Wv"].T, we[:, :P].T, we[:, P:].T], axis=1)
    o["b5"] = np.stack([a["L1_xattn_bq"], a["L1_xattn_bk"], a["L1_xattn_bv"], a["L1_xattn_be"]], axis=1)
    o["bv5"] = a["L1_xattn_bv"][None]

    ROT = 32

    def swap_rot(w):
        return np.concatenate([w[..., ROT // 2:ROT], w[..., :ROT // 2], w[..., ROT:]], axis=-1)

    inv = (np.float32(10000.0) ** (-np.arange(ROT // 2, dtype=f) / np.float32(ROT // 2))).astype(f)
    ang = (pos * inv).astype(f)
    cos = np.concatenate([np.cos(ang), np.cos(ang), np.ones((T, HW - ROT), f)], axis=1).astype(f)
    sin = np.concatenate([-np.sin(ang), np.sin(ang), np.zeros((T, HW - ROT), f)], axis=1).astype(f)
    o["router"] = a["L1_ffn_mosa_router_w"]
    d = a["L1_ffn_dense_wqkv"]
    q, k, v = d[..., :HW], d[..., HW:2 * HW], d[..., 2 * HW:]
    o["dense_w"] = np.stack([q, swap_rot(q), k, swap_rot(k), v], axis=1).reshape(P, 5, NH // 2, P)
    o["dense_wo"] = a["L1_ffn_dense_wo"].reshape(NH // 2, P, P).transpose(1, 0, 2)
    eighth = np.float32(HW ** -0.5)
    o["dense_rope"] = np.tile(np.stack([cos * eighth, cos, sin * eighth, sin]).transpose(2, 0, 1), (2, 1, 1))
    m = a["L1_ffn_mosa_wqkv"]
    q, k, v = m[..., :HW], m[..., HW:2 * HW], m[..., 2 * HW:]
    o["mosa_w"] = np.stack([q, swap_rot(q), k, swap_rot(k), v], axis=2)
    o["mosa_wo"] = a["L1_ffn_mosa_wo"].reshape(NH, HW, P).transpose(1, 0, 2)
    o["mosa_rope"] = np.stack([cos, sin], axis=1).reshape(2, P, 2, HW).transpose(1, 0, 2, 3)
    return {k: np.ascontiguousarray(v) for k, v in o.items()}


def kernel(**inputs):
    import concourse.bacc as bacc
    from concourse.bass_utils import run_bass_kernel_spmd

    arrays = lay_out(inputs)
    nc = bacc.Bacc("TRN2", target_bir_lowering=False, num_devices=1)
    ins = {k: nc.dram_tensor(f"in_{k}", v.shape, mybir.dt.from_np(v.dtype), kind="ExternalInput").ap()
           for k, v in arrays.items()}
    out = nc.dram_tensor("out_0", (B * T, P), F32, kind="ExternalOutput").ap()
    build(nc, ins, out)
    r = run_bass_kernel_spmd(nc, [{f"in_{k}": v for k, v in arrays.items()}], core_ids=[0])
    return r.results[0]["out_0"].reshape(B, T, P)
```

```python
from contextlib import ExitStack

import numpy as np
import concourse.bass as bass
from concourse import mybir

ALU = mybir.AluOpType
ACT = mybir.ActivationFunctionType
AX_X = mybir.AxisListType.X
F32 = mybir.dt.float32
BF16 = mybir.dt.bfloat16
I32 = mybir.dt.int32
ds = bass.ds

P = 128
B = 8
T = 256
TILES = B * T // P
H = 16
DH = P // H
UNITS = B * H
BPAIRS = B // 2
TAIL = 4
SLOTS = 4
ROUNDS = UNITS // SLOTS
COLS = P // SLOTS
TOPK = 32
TERMS = ((0, 0), (0, 1), (0, 2), (1, 0), (1, 1), (2, 0))
KROWS = 72
LOW = -3.0e38
EPS = 1e-5


class Sems:

    def __init__(self, nc, ctx, stage):
        self.nc, self.ctx, self.stage, self.made = nc, ctx, stage, {}

    def __call__(self, name):
        if name not in self.made:
            self.made[name] = self.ctx.enter_context(self.nc.semaphore(f"{self.stage}_{name}"))
        return self.made[name]

    def clear(self):
        numbers = sorted(s.num for s in self.made.values())
        first = 0
        for i in range(1, len(numbers) + 1):
            if i == len(numbers) or numbers[i] != numbers[i - 1] + 1:
                self.nc.gpsimd.sem_clear(range(numbers[first], numbers[i - 1] + 1))
                first = i
        self.nc.all_engine_barrier()


def layernorm_stats(v, sem, X, stats, mean, rstd, tmp):
    chain = sem("ln_chain")
    with v.Fori(0, TILES // 8) as t:
        for k in range(8):
            v.bn_stats(stats[:, ds(t * 8 + k, 1), :], X[:, ds(t * 8 + k, 1), :]).then_inc(sem("ln_stats"), 1)
    v.wait_ge(sem("ln_stats"), TILES)
    me, ve, mo, vo = (stats[:, :, i] for i in (1, 2, 4, 5))
    n = [0]

    def step(ins):
        n[0] += 1
        ins.then_inc(chain, 1)
        v.wait_ge(chain, n[0])

    var, y, y2, d = (tmp[:, i, :] for i in range(4))
    step(v.tensor_tensor(mean[:], me, mo, ALU.add))
    step(v.tensor_scalar(mean[:], mean[:], 0.5, None, ALU.mult))
    step(v.tensor_tensor(d, me, mo, ALU.subtract))
    step(v.scalar_tensor_tensor(d, d, 0.25, d, ALU.mult, ALU.mult))
    step(v.tensor_tensor(var, ve, vo, ALU.add))
    step(v.scalar_tensor_tensor(var, var, 1.0 / P, d, ALU.mult, ALU.add))
    step(v.tensor_scalar(var, var, EPS, None, ALU.add))
    step(v.tensor_scalar(y.bitcast(I32), var.bitcast(I32), 1, None, ALU.logical_shift_right))
    step(v.tensor_scalar(y.bitcast(I32), y.bitcast(I32), -1.0, float(0x5F3759DF), ALU.mult, ALU.add))
    for i in range(3):
        step(v.tensor_tensor(y2, y, y, ALU.mult))
        step(v.scalar_tensor_tensor(y2, y2, -0.5, var, ALU.mult, ALU.mult))
        step(v.scalar_tensor_tensor(rstd[:] if i == 2 else y, y2, 1.5, y, ALU.add, ALU.mult))


def before(i):
    return i + 1


def after(i):
    return i + 2


def by_batch(t):
    return t.rearrange("p k (c h a) d -> p k c h a d", h=H, a=2)


def prepare_heads(nc, stage, X, ctxT, consts, tensors, drams, topk):
    ident = consts["ident"]
    qs, ks, vaug, w, bias, bo = tensors
    w_dram, b_dram, bo_dram, rope_dram = drams
    with ExitStack() as ctx:
        def sb(name, shape, dt=F32):
            return ctx.enter_context(nc.sbuf_tensor(f"{stage}_{name}", shape, dt))

        def bank(name):
            return ctx.enter_context(nc.psum_tensor(f"{stage}_{name}", [P, 2, T], F32))

        sem = Sems(nc, ctx, stage + "p")
        stats = sb("stats", [P, TILES, 6])
        mean = sb("mean", [P, TILES])
        rstd = sb("rstd", [P, TILES])
        lntmp = sb("lntmp", [P, 4, TILES])
        xn = sb("xn", [P, 2, 2, P])
        xnT = sb("xnT", [P, 2, T])
        kvT = sb("kvT", [P, 2, T]) if ctxT is not None else xnT
        r = sb("r", [P, 2, 2, T])
        r2 = sb("r2", [P, 2, 2, T]) if not topk else None
        d1 = sb("d1", [P, 2, 2, T])
        parts = [sb(f"part{i}", [P, BPAIRS, 2, 2, T], BF16) for i in range(3)]
        rope = sb("rope", [P, 4, T]) if not topk else None
        pT = [bank(f"pT{i}")[:, 0, :] for i in range(2)]
        pA = [bank(f"pA{i}") for i in range(2)]
        pB = [bank(f"pB{i}") for i in range(2)]
        pV = [bank(f"pV{i}")[:, :, 0:P] for i in range(2)]

        def pair(name):
            return [sem(f"{name}{i}") for i in range(2)]

        xn_made, xT_done, xnT_made, qk_done, v_done, v_made, r_made, part0_made, d1_made, part1_made, part2_made = (
            pair(n) for n in ("xn_made", "xT_done", "xnT_made", "qk_done", "v_done", "v_made", "r_made", "part0_made",
                              "d1_made", "part1_made", "part2_made"))
        credited = xT_done + xnT_made + v_done + v_made + r_made + d1_made + xn_made + qk_done + part0_made + part1_made + part2_made

        def chunks(eng, body):
            with eng.Fori(0, BPAIRS - 1) as i:
                body(i, True)
            body(BPAIRS - 1, False)

        w_in, rope_in = sem("w_in"), sem("rope_in")

        with nc.Block() as block:
            @block.sync
            def _(sp):
                sp.dma_start(w[:], w_dram).then_inc(w_in, 16)
                if b_dram is not None:
                    sp.dma_start(bias[:], b_dram).then_inc(w_in, 16)
                    sp.dma_start(bo[:], bo_dram).then_inc(w_in, 16)
                if rope is not None:
                    sp.dma_start(rope[:], rope_dram).then_inc(rope_in, 16)

                def stack_chunk(i, more):
                    for part, made in enumerate((part0_made, part1_made, part2_made)):
                        sp.wait_ge(made[0], after(i))
                        sp.wait_ge(made[1], after(i))
                        sp.sem_inc(sem("waited_sp"), 1)
                        for side, stack in ((0, qs), (1, ks)):
                            for t, term in enumerate(TERMS):
                                if term[side] == part:
                                    sp.dma_start(
                                        stack[DH * t:DH * (t + 1), ds(i * 2 * H, 2 * H), :]
                                        .rearrange("d (h a) n -> d h (a n)", a=2),
                                        parts[part][:, ds(i, 1), side].rearrange("p c a n -> p (c a n)"),
                                    ).then_inc(sem("stacked"), 16)

                chunks(sp, stack_chunk)
                sp.wait_ge(sem("stacked"), 16 * 2 * len(TERMS) * BPAIRS)

            @block.gpsimd
            def _(pool):
                for s in credited:
                    pool.sem_inc(s, 1)
                pool.memset(vaug[:, :, :, DH:DH + 1], 1.0).then_inc(sem("ones_made"), 1)
                if b_dram is None:
                    pool.memset(bias[:], 0.0).then_inc(w_in, 16)
                    pool.memset(bo[:], 0.0).then_inc(w_in, 16)
                def split_chunk(i, more):
                    for par in range(2):
                        pool.wait_ge(part0_made[par], after(i))
                        pool.tensor_tensor(d1[:, par].unsqueeze(1), r[:, par].unsqueeze(1), parts[0][:, ds(i, 1), :, par], ALU.subtract).then_inc(d1_made[par], 1)
                        pool.wait_ge(part1_made[par], after(i))
                        pool.tensor_tensor(parts[2][:, ds(i, 1), :, par], d1[:, par].unsqueeze(1), parts[1][:, ds(i, 1), :, par], ALU.subtract)\
                            .then_inc(part2_made[par], 1)

                chunks(pool, split_chunk)

            @block.vector
            def _(v):
                layernorm_stats(v, sem, X, stats, mean, rstd, lntmp)
                v.wait_ge(w_in, 48)
                if rope is not None:
                    v.wait_ge(rope_in, 16)
                chain = sem("rope_chain")
                def normalise_chunk(i):
                    for par in range(2):
                        v.wait_ge(xT_done[par], before(i))
                        for kt in range(2):
                            tile = i * 4 + par * 2 + kt
                            ins = v.tensor_scalar(xn[:, par, kt, :], X[:, ds(tile, 1), :], mean[:, ds(tile, 1)],
                                                  rstd[:, ds(tile, 1)], ALU.subtract, ALU.mult)
                        ins.then_inc(xn_made[par], 1)

                def rotate_chunk(i, more):
                    if more:
                        normalise_chunk(i + 1)
                    for par in range(2):
                        A, C = pA[par], pB[par]
                        v.wait_ge(qk_done[par], after(i))
                        v.wait_ge(d1_made[par], before(i))
                        if topk:
                            v.tensor_scalar(r[:, par, 0, :], A[:, 0, :], bias[:, 0:1], DH ** -0.5, ALU.add, ALU.mult)
                            v.tensor_scalar(r[:, par, 1, :], A[:, 1, :], bias[:, 2:3], None, ALU.add).then_inc(r_made[par], 1)
                        else:
                            for s in range(2):
                                v.scalar_tensor_tensor(r[:, par, s, :], A[:, s, :], bias[:, 2 * s:2 * s + 1], rope[:, s, :],
                                                       ALU.add, ALU.mult).then_inc(chain, 1)
                                v.scalar_tensor_tensor(r2[:, par, s, :], C[:, s, :], bias[:, 2 * s + 1:2 * s + 2],
                                                       rope[:, 2 + s, :], ALU.add, ALU.mult).then_inc(chain, 1)
                            v.wait_ge(chain, 4)
                            v.sem_clear(chain)
                            v.tensor_tensor(r[:, par], r[:, par], r2[:, par], ALU.add).then_inc(r_made[par], 1)

                normalise_chunk(0)
                chunks(v, rotate_chunk)

            @block.scalar
            def _(act):
                def copy_xnT(i, par):
                    act.wait_ge(xT_done[par], after(i))
                    act.wait_ge(v_done[par], before(i))
                    ins = act.copy(xnT[:, par, :], pT[par])
                    if ctxT is not None:
                        ins = act.copy(kvT[:, par, :], ctxT[:, ds((i * 2 + par) * T, T)])
                    ins.then_inc(xnT_made[par], 1)

                def copy_chunk(i, more):
                    for par in range(2):
                        act.wait_ge(v_done[par], after(i))
                        act.copy(by_batch(vaug)[:, :, ds(i, 1), :, par, 0:DH].rearrange("p k c h d -> p k (c h) d"),
                                 pV[par].rearrange("p k (h d) -> p k h d", d=DH)).then_inc(v_made[par], 1)
                        if more:
                            copy_xnT(i + 1, par)
                        act.wait_ge(r_made[par], after(i))
                        act.copy(parts[0][:, ds(i, 1), :, par], r[:, par].unsqueeze(1)).then_inc(part0_made[par], 1)
                    for par in range(2):
                        act.wait_ge(d1_made[par], after(i))
                        act.copy(parts[1][:, ds(i, 1), :, par], d1[:, par].unsqueeze(1)).then_inc(part1_made[par], 1)

                for par in range(2):
                    copy_xnT(0, par)
                chunks(act, copy_chunk)

            @block.tensor
            def _(pe):
                pe.wait_ge(w_in, 48)
                def transpose_xn(i, par):
                    pe.wait_ge(xn_made[par], after(i))
                    pe.wait_ge(xnT_made[par], before(i))
                    for kt in range(2):
                        ins = pe.transpose(pT[par][:, kt * P:(kt + 1) * P], xn[:, par, kt, :], ident[:])
                    ins.then_inc(xT_done[par], 1)

                def project_chunk(i, more):
                    for par in range(2):
                        pe.wait_ge(xnT_made[par], after(i))
                        pe.wait_ge(r_made[par], before(i))
                        src = (xnT, kvT)
                        for s in range(2):
                            ins = pe.matmul(pA[par][:, s, :], w[:, 2 * s, :], src[s][:, par, :], start=True, stop=True)
                            if not topk:
                                ins = pe.matmul(pB[par][:, s, :], w[:, 2 * s + 1, :], src[s][:, par, :], start=True, stop=True)
                        ins.then_inc(qk_done[par], 1)
                        pe.wait_ge(v_made[par], before(i))
                        for kt in range(2):
                            ins = pe.matmul(pV[par][:, kt, :], kvT[:, par, kt * P:(kt + 1) * P], w[:, 4, :], start=True, stop=True)
                        ins.then_inc(v_done[par], 1)
                        if more:
                            transpose_xn(i + 1, par)

                for par in range(2):
                    transpose_xn(0, par)
                chunks(pe, project_chunk)

        sem.clear()


def attend_heads(nc, stage, X, consts, tensors, topk):
    ident, ones = consts["ident"], consts["ones"]
    qs, ks, vaug, w, bias, bo = tensors
    with ExitStack() as ctx:
        def sb(name, shape, dt=F32):
            return ctx.enter_context(nc.sbuf_tensor(f"{stage}_{name}", shape, dt))

        def bank(name):
            return ctx.enter_context(nc.psum_tensor(f"{stage}_{name}", [P, 2, T], F32))

        sem = Sems(nc, ctx, stage + "a")
        m8 = sb("m8", [P, SLOTS, 2, 4, 8]) if topk else None
        nmax = sb("nmax", [P, SLOTS, 2])
        prob = sb("prob", [P, SLOTS, 2, T])
        rest = sb("rest", [P, SLOTS, 2, T]) if topk else None
        prest = sb("prest", [P, SLOTS, 2, T]) if topk else None
        probT = sb("probT", [P, SLOTS, 2, T])
        vslot = sb("vslot", [P, 2, SLOTS, COLS])
        oT = sb("oT", [P, T])
        oall = sb("oall", [P, UNITS, 2, DH + 1])
        rsum = sb("rsum", [P, TAIL, 2, H])
        on = prob[:, 0:TAIL, :, 0:P].rearrange("p j q (h d) -> p j q h d", d=DH)
        onT = probT[:, 0:TAIL, 0, :]
        pS = [bank(f"pS{i}") for i in range(SLOTS)]
        pPT = [bank(f"pPT{i}") for i in range(2)]
        bankO, bankQ = bank("pO"), bank("pQ")
        pO = bankO[:, 0, :]
        pQ = bankQ[:, :, 0:P]
        pOT = [t[:, 0, :] for t in pS]
        pY = [t[:, :, 0:P] for t in pPT + [bankO, bankQ]]

        s_done, nmax_made, exp_done, p_made, t_done, probT_made, pv_done, topk_done = (
            [sem(f"{n}{j}") for j in range(SLOTS)]
            for n in ("s_done", "nmax_made", "exp_done", "p_made", "t_done", "probT_made", "pv_done", "topk_done"))
        v_placed = [sem(f"v_placed{j}") for j in range(SLOTS)]
        o_lifted, o_turned, o_kept = sem("o_lifted"), sem("o_turned"), sem("o_kept")
        norm_done, oT_done, onT_made, y_done, x_done = (
            [sem(f"{n}{j}") for j in range(TAIL)] for n in ("norm_done", "oT_done", "onT_made", "y_done", "x_done"))
        credited = (s_done + nmax_made + exp_done + p_made + t_done + probT_made + pv_done + topk_done + v_placed
                    + [o_lifted, o_turned, o_kept] + norm_done + oT_done + onT_made + y_done + x_done)
        dve_evacuates = () if topk else (0, 2)

        def near(i, j):
            return i + j // SLOTS, j % SLOTS

        def keep(i, copy):
            copy(oall[:, ds(i * SLOTS, SLOTS), :, :].rearrange("p a q d -> p q a d"),
                 pQ.rearrange("p q (a d) -> p q a d", a=SLOTS)[:, :, :, 0:DH + 1]).then_inc(o_kept, 1)

        def rounds(eng, step, finish):
            for j in range(SLOTS):
                step(0, j, True, False)
            with eng.Fori(1, ROUNDS - 1) as i:
                for j in range(SLOTS):
                    step(i, j, False, False)
            for j in range(SLOTS):
                step(ROUNDS - 1, j, False, True)
            finish(ROUNDS - 1)

        with nc.Block() as block:
            @block.gpsimd
            def _(pool):
                for s in credited:
                    pool.sem_inc(s, 1)
                pool.memset(vslot[:], 0.0).then_inc(sem("vslot_cleared"), 1)
                pool.wait_ge(sem("vslot_cleared"), 1)
                with pool.Fori(0, ROUNDS) as i:
                    for j in range(SLOTS):
                        pool.wait_ge(pv_done[j], before(i))
                        pool.tensor_copy(vslot[:, :, j, 0:DH + 1].unsqueeze(2), vaug[:, :, ds(i * SLOTS + j, 1), :])\
                            .then_inc(v_placed[j], 1)
                        if topk:
                            pool.wait_ge(topk_done[j], after(i))
                            pool.wait_ge(exp_done[j], before(i))
                            pool.sem_inc(sem("waited_pool"), 1)
                            pool.tensor_scalar(nmax[:, j, :], m8[:, j, :, 0, 0], -1.0, 0.0, ALU.mult, ALU.add)\
                                .then_inc(nmax_made[j], 1)
                            pool.wait_ge(exp_done[j], after(i))
                            pool.tensor_tensor(prob[:, j], prob[:, j], prest[:, j], ALU.subtract).then_inc(p_made[j], 1)

            @block.vector
            def _(v):
                chain = sem("topk_chain")

                def largest(i, j):
                    v.wait_ge(s_done[j], after(i))
                    v.wait_ge(exp_done[j], before(i))
                    v.sem_inc(sem("waited_dve"), 1)
                    n = 0
                    for rnd in range(TOPK // 8):
                        src = pS[j] if rnd == 0 else rest[:, j]
                        for qt in range(2):
                            if rnd:
                                v.wait_ge(chain, n - 1)
                            v.max(m8[:, j, qt, rnd, :], src[:, qt, :]).then_inc(chain, 1)
                            n += 1
                        for qt in range(2):
                            v.wait_ge(chain, n - 1)
                            ins = v.match_replace(rest[:, j, qt, :], m8[:, j, qt, rnd, :], src[:, qt, :], LOW)
                            if n < 4 * TOPK // 8 - 1:
                                ins.then_inc(chain, 1)
                            else:
                                ins.then_inc(topk_done[j], 1)
                            n += 1
                    v.wait_ge(chain, 4 * TOPK // 8 - 1)
                    v.sem_clear(chain)

                def maxima(i, j):
                    v.wait_ge(s_done[j], after(i))
                    v.wait_ge(exp_done[j], before(i))
                    v.tensor_reduce(nmax[:, j, :], pS[j][:], AX_X, ALU.max, negate=True).then_inc(nmax_made[j], 1)

                def evacuate(i, j):
                    if j in dve_evacuates:
                        v.wait_ge(t_done[j], after(i))
                        v.wait_ge(pv_done[j], before(i))
                        v.tensor_copy(probT[:, j], pPT[j % 2][:]).then_inc(probT_made[j], 1)

                search = largest if topk else maxima

                def step(i, j, first, last):
                    if not last or j + 2 < SLOTS:
                        search(*near(i, j + 2))
                    if not first or j > 0:
                        evacuate(*near(i, j - 1))
                    if not first and j == 3:
                        keep_round(i - 1)

                def keep_round(i):
                    if not topk:
                        v.wait_ge(o_turned, after(i))
                        keep(i, v.tensor_copy)

                def finish(i):
                    evacuate(i, SLOTS - 1)
                    keep_round(i)

                search(0, 0)
                search(0, 1)
                rounds(v, step, finish)
                v.wait_ge(o_kept, after(ROUNDS - 1))
                tail = sem("tail_chain")
                with v.Fori(0, B // TAIL) as i:
                    for j in range(TAIL):
                        units = oall[:, ds(i * (TAIL * H) + j // 2 * 2 * H + j % 2, H, step=2), :, :].rearrange("p h q d -> p q h d")
                        v.wait_ge(oT_done[j], before(i))
                        v.reciprocal(rsum[:, j], units[:, :, :, DH]).then_inc(tail, 1)
                        v.wait_ge(tail, 1)
                        v.sem_clear(tail)
                        v.tensor_tensor(on[:, j], units[:, :, :, 0:DH],
                                        rsum[:, j].unsqueeze(3).broadcast_to([P, 2, H, DH]), ALU.mult).then_inc(norm_done[j], 1)
                    for j in range(TAIL):
                        tiles = X[:, ds(i * (2 * TAIL) + j * 2, 2), :]
                        v.wait_ge(y_done[j], after(i))
                        v.tensor_tensor(tiles, tiles, pY[j], ALU.add).then_inc(x_done[j], 1)

            @block.scalar
            def _(act):
                def exponentials(i, j):
                    act.wait_ge(nmax_made[j], after(i))
                    act.wait_ge(t_done[j], before(i))
                    if topk:
                        for qt in range(2):
                            act.activation(prest[:, j, qt, :], rest[:, j, qt, :], ACT.Exp, bias=nmax[:, j, qt:qt + 1])
                    for qt in range(2):
                        ins = act.activation(prob[:, j, qt, :], pS[j][:, qt, :], ACT.Exp, bias=nmax[:, j, qt:qt + 1])
                    ins.then_inc(exp_done[j], 1)

                def evacuate(i, j):
                    if j not in dve_evacuates:
                        act.wait_ge(t_done[j], after(i))
                        act.wait_ge(pv_done[j], before(i))
                        act.copy(probT[:, j], pPT[j % 2][:]).then_inc(probT_made[j], 1)

                def lift(i):
                    act.wait_ge(pv_done[SLOTS - 1], after(i))
                    act.wait_ge(o_turned, before(i))
                    act.copy(oT[:], pO).then_inc(o_lifted, 1)

                def keep_round(i):
                    if topk:
                        act.wait_ge(o_turned, after(i))
                        keep(i, act.copy)

                def step(i, j, first, last):
                    if not first and j == 2:
                        lift(i - 1)
                    if not last or j + 1 < SLOTS:
                        exponentials(*near(i, j + 1))
                    if not first or j > 0:
                        evacuate(*near(i, j - 1))
                    if not first and j == 3:
                        keep_round(i - 1)

                def finish(i):
                    evacuate(i, SLOTS - 1)
                    lift(i)
                    keep_round(i)

                exponentials(0, 0)
                rounds(act, step, finish)
                with act.Fori(0, B // TAIL) as i:
                    for j in range(TAIL):
                        act.wait_ge(oT_done[j], after(i))
                        act.wait_ge(y_done[j], before(i))
                        act.activation(onT[:, j], pOT[j], ACT.Identity, bias=bias[:, 4:5]).then_inc(onT_made[j], 1)

            @block.tensor
            def _(pe):
                def scores(i, j):
                    pe.wait_ge(exp_done[j], before(i))
                    unit = ds(i * SLOTS + j, 1)
                    for qt in range(2):
                        ins = pe.matmul(pS[j][:, qt, :], qs[0:KROWS, unit, qt * P:(qt + 1) * P],
                                        ks[0:KROWS, unit, :], start=True, stop=True)
                    ins.then_inc(s_done[j], 1)

                def transposes(i, j):
                    pe.wait_ge((p_made if topk else exp_done)[j], after(i))
                    li, lj = near(i, j - 2)
                    pe.wait_ge(probT_made[lj], after(li))
                    for kt in range(2):
                        for qt in range(2):
                            ins = pe.transpose(pPT[j % 2][:, kt, qt * P:(qt + 1) * P], prob[:, j, qt, kt * P:(kt + 1) * P], ident[:])
                    ins.then_inc(t_done[j], 1)

                def products(i, j):
                    pe.wait_ge(probT_made[j], after(i))
                    pe.wait_ge(v_placed[j], after(i))
                    if j == 0:
                        pe.wait_ge(o_lifted, before(i))
                    for kt in range(2):
                        ins = pe.matmul(pO[j * COLS:(j + 1) * COLS, :], vslot[:, kt, j, :], probT[:, j, kt, :],
                                        start=(kt == 0), stop=(kt == 1), skip_group_check=True)
                    ins.then_inc(pv_done[j], 1)

                def turn(i):
                    pe.wait_ge(o_lifted, after(i))
                    pe.wait_ge(o_kept, before(i))
                    for qt in range(2):
                        ins = pe.transpose(pQ[:, qt, :], oT[:, qt * P:(qt + 1) * P], ident[:])
                    ins.then_inc(o_turned, 1)

                def step(i, j, first, last):
                    if not last or j + 3 < SLOTS:
                        scores(*near(i, j + 3))
                    if not first and j == 3:
                        turn(i - 1)
                    transposes(i, j)
                    if not first or j >= 2:
                        products(*near(i, j - 2))

                def finish(i):
                    products(i, SLOTS - 2)
                    products(i, SLOTS - 1)
                    turn(i)

                pe.wait_ge(consts["zeroed"], consts["zeroed_by"])
                for j in range(3):
                    scores(0, j)
                rounds(pe, step, finish)
                with pe.Fori(0, B // TAIL) as i:
                    for j in range(TAIL):
                        pe.wait_ge(norm_done[j], after(i))
                        pe.wait_ge(onT_made[j], before(i))
                        for qt in range(2):
                            ins = pe.transpose(pOT[j][:, qt * P:(qt + 1) * P],
                                               on[:, j, qt].rearrange("p h d -> p (h d)"), ident[:])
                        ins.then_inc(oT_done[j], 1)
                    for j in range(TAIL):
                        pe.wait_ge(onT_made[j], after(i))
                        pe.wait_ge(x_done[j], before(i))
                        for qt in range(2):
                            pe.matmul(pY[j][:, qt, :], onT[:, j, qt * P:(qt + 1) * P], w[:, 5, :], start=True, stop=False)
                            ins = pe.matmul(pY[j][:, qt, :], ones[0:1, :], bo[:], start=False, stop=True)
                        ins.then_inc(y_done[j], 1)

        sem.clear()


def head_attention(nc, stage, X, ctxT, consts, drams, topk):
    with ExitStack() as ctx:
        def sb(name, shape, dt=F32):
            return ctx.enter_context(nc.sbuf_tensor(f"{stage}_{name}", shape, dt))

        tensors = (
            consts["qs"],
            consts["ks"],
            sb("vaug", [P, 2, UNITS, DH + 1]),
            sb("w", [P, 6, P]),
            sb("bias", [P, 5]),
            sb("bo", [1, P]),
        )
        prepare_heads(nc, stage, X, ctxT, consts, tensors, drams, topk)
        attend_heads(nc, stage, X, consts, tensors, topk)


DEPTH = 7
TREES = 8
NODES = 2 ** (DEPTH + 1) - 1
WIDTH = TREES * NODES


def level(d):
    return slice(TREES * (2 ** d - 1), TREES * (2 ** (d + 1) - 1))


CHUNKS = [slice(0, level(5).stop), level(6), slice(level(7).start, level(7).start + 512),
          slice(level(7).start + 512, WIDTH)]
NCHUNK = -(-WIDTH // P)


def tree_ffn(nc, stage, X, consts, drams):
    ident = consts["ident"]
    win_dram, bin_dram, wout_dram = drams
    with ExitStack() as ctx:
        def sb(name, shape, dt=F32):
            return ctx.enter_context(nc.sbuf_tensor(f"{stage}_{name}", shape, dt))

        def bank(name):
            return ctx.enter_context(nc.psum_tensor(f"{stage}_{name}", [P, 512], F32))

        sem = Sems(nc, ctx, stage)
        stats = sb("stats", [P, TILES, 6])
        mean = sb("mean", [P, TILES])
        rstd = sb("rstd", [P, TILES])
        lntmp = sb("lntmp", [P, 4, TILES])
        win = sb("win", [P, WIDTH])
        wout = sb("wout", [P, NCHUNK, P])
        b3 = consts["qs"][0:3].rearrange("p u n -> p (u n)")[:, 0:WIDTH]
        ones3 = sb("ones3", [3, P], BF16)
        xn = sb("xn", [P, 2, P])
        xnT = sb("xnT", [P, 2, P])
        acts = sb("acts", [P, 2, WIDTH])
        path = sb("path", [P, 2, WIDTH], BF16)
        actsT = sb("actsT", [P, 2, NCHUNK, P])
        brow = actsT[0:1, 0].rearrange("p k n -> p (k n)")[:, 0:WIDTH]
        bparts = acts[0:1].rearrange("p a n -> p (a n)").bitcast(BF16)[:, 0:3 * WIDTH].rearrange("p (c n) -> p c n", c=3)
        pL = [bank(f"pL{c}") for c in range(4)]
        pX = bank("pX")
        pT = [bank(f"pT{c}") for c in range(2)]
        pY = bank("pY")

        def pair(name):
            return [sem(f"{name}{i}") for i in range(2)]

        xn_made, xT_done, xnT_made, y_done, x_done = (pair(n) for n in ("xn_made", "xT_done", "xnT_made", "y_done", "x_done"))
        logits, silu_made, decided, masked, aT_done, aT_made = (
            [pair(f"{n}{c}_") for c in range(4)] for n in ("logits", "silu", "decided", "masked", "aT_done", "aT_made"))
        credited = xn_made + xT_done + xnT_made + y_done + x_done + sum(
            logits + silu_made + decided[:2] + masked + aT_done + aT_made, [])

        def tiles(eng, step, finish):
            step(0, 0, None, 1)
            step(0, 1, 0, 0)
            with eng.Fori(1, TILES // 2) as i:
                step(i, 0, i - 1, 1)
                step(i, 1, i, 0)
            finish(TILES // 2 - 1, 1)

        def chunk_groups(g):
            return range(4 * g, 4 * g + 4)

        def rows(k):
            return min(P, WIDTH - k * P)

        with nc.Block() as block:
            @block.sync
            def _(sp):
                sp.dma_start(win[:], win_dram).then_inc(sem("w_in"), 16)
                sp.dma_start(brow, bin_dram).then_inc(sem("b_in"), 16)
                full = (NCHUNK - 1) * P
                sp.dma_start(wout[:, 0:NCHUNK - 1, :], wout_dram[0:full, :].rearrange("(k p) n -> p k n", p=P)).then_inc(sem("w_in"), 16)
                sp.dma_start(wout[0:WIDTH - full, NCHUNK - 1, :], wout_dram[full:WIDTH, :]).then_inc(sem("w_in"), 16)
                sp.wait_ge(sem("b_split"), 4)
                for i in range(3):
                    sp.dma_start(b3[i:i + 1, :], bparts[0:1, i, :]).then_inc(sem("b3_in"), 16)
                sp.wait_ge(sem("b3_in"), 48)

            @block.gpsimd
            def _(pool):
                for s in credited:
                    pool.sem_inc(s, 1)
                pool.memset(ones3[:], 1.0).then_inc(sem("ones3_made"), 1)
                pool.memset(path[:, :, level(0)], 1.0).then_inc(sem("root_made"), 1)
                split = sem("b_split")
                pool.wait_ge(sem("b_in"), 16)
                pool.tensor_copy(bparts[0:1, 0, :], brow).then_inc(split, 1)
                pool.wait_ge(split, 1)
                pool.tensor_tensor(brow, brow, bparts[0:1, 0, :], ALU.subtract).then_inc(split, 1)
                pool.wait_ge(split, 2)
                pool.tensor_copy(bparts[0:1, 1, :], brow).then_inc(split, 1)
                pool.wait_ge(split, 3)
                pool.tensor_tensor(bparts[0:1, 2, :], brow, bparts[0:1, 1, :], ALU.subtract).then_inc(split, 1)

            @block.vector
            def _(v):
                layernorm_stats(v, sem, X, stats, mean, rstd, lntmp)
                chain = sem("path_chain")

                def start(i, par):
                    v.wait_ge(xT_done[par], before(i))
                    v.tensor_scalar(xn[:, par], X[:, ds(i * 2 + par, 1), :], mean[:, ds(i * 2 + par, 1)],
                                    rstd[:, ds(i * 2 + par, 1)], ALU.subtract, ALU.mult).then_inc(xn_made[par], 1)

                def end(i, par):
                    n = 0
                    for d in range(DEPTH):
                        lv, up = level(d), level(d + 1)
                        mid = up.start + TREES * 2 ** d
                        c = 0 if d < DEPTH - 1 else 1
                        if d in (0, DEPTH - 1):
                            v.wait_ge(silu_made[c][par], after(i))
                        if n:
                            v.wait_ge(chain, n)
                        off = CHUNKS[c].start
                        ins = v.scalar_tensor_tensor(path[:, par, mid:up.stop], pL[c][:, lv.start - off:lv.stop - off], 0.0,
                                                     path[:, par, lv], ALU.is_gt, ALU.mult).then_inc(chain, 1)
                        n += 1
                        v.wait_ge(chain, n)
                        v.tensor_tensor(path[:, par, up.start:mid], path[:, par, lv], path[:, par, mid:up.stop],
                                        ALU.subtract).then_inc(chain, 1)
                        n += 1
                        if d >= DEPTH - 2:
                            v.wait_ge(chain, n)
                            v.sem_inc(decided[c][par], 1)
                    v.sem_clear(chain)
                    for c in range(4):
                        v.wait_ge(silu_made[c][par], after(i))
                        v.tensor_tensor(acts[:, par, CHUNKS[c]], acts[:, par, CHUNKS[c]], path[:, par, CHUNKS[c]],
                                        ALU.mult).then_inc(masked[c][par], 1)
                    v.wait_ge(y_done[par], after(i))
                    v.tensor_tensor(X[:, ds(i * 2 + par, 1), :], X[:, ds(i * 2 + par, 1), :], pY[:, 0:P].unsqueeze(1),
                                    ALU.add).then_inc(x_done[par], 1)

                def step(i, par, before_i, before_par):
                    start(i, par)
                    if before_i is not None:
                        end(before_i, before_par)

                v.wait_ge(sem("root_made"), 1)
                tiles(v, step, end)

            @block.scalar
            def _(act):
                def start(i, par):
                    act.wait_ge(xT_done[par], after(i))
                    act.wait_ge(logits[3][par], before(i))
                    act.copy(xnT[:, par], pX[:, 0:P]).then_inc(xnT_made[par], 1)
                    for c in range(4):
                        act.wait_ge(logits[c][par], after(i))
                        if c == 0:
                            act.wait_ge(aT_done[3][par], before(i))
                        size = CHUNKS[c].stop - CHUNKS[c].start
                        act.activation(acts[:, par, CHUNKS[c]], pL[c][:, 0:size], ACT.Silu).then_inc(silu_made[c][par], 1)

                def end(i, par):
                    for g in range(4):
                        act.wait_ge(aT_done[g][par], after(i))
                        if g == 0:
                            act.wait_ge(y_done[par], before(i))
                        for k in chunk_groups(g)[-1:]:
                            n = rows(k)
                        if n == P:
                            ins = act.copy(actsT[:, par, 4 * g:4 * g + 4, :].rearrange("p k n -> p (k n)"), pT[g % 2][:])
                        else:
                            act.copy(actsT[:, par, 4 * g:4 * g + 3, :].rearrange("p k n -> p (k n)"), pT[g % 2][:, 0:3 * P])
                            ins = act.copy(actsT[0:n, par, 4 * g + 3, :], pT[g % 2][0:n, 3 * P:4 * P])
                        ins.then_inc(aT_made[g][par], 1)

                def step(i, par, before_i, before_par):
                    start(i, par)
                    if before_i is not None:
                        end(before_i, before_par)

                tiles(act, step, end)

            @block.tensor
            def _(pe):
                pe.wait_ge(sem("w_in"), 48)
                pe.wait_ge(sem("b3_in"), 48)
                pe.wait_ge(sem("ones3_made"), 1)

                def start(i, par, before_i, before_par):
                    pe.wait_ge(xn_made[par], after(i))
                    if before_i is not None:
                        pe.wait_ge(xnT_made[before_par], after(before_i))
                    pe.transpose(pX[:, 0:P], xn[:, par], ident[:]).then_inc(xT_done[par], 1)
                    pe.wait_ge(xnT_made[par], after(i))
                    for c in range(4):
                        size = CHUNKS[c].stop - CHUNKS[c].start
                        if before_i is not None:
                            pe.wait_ge((decided[c] if c < 2 else silu_made[c])[before_par], after(before_i))
                        pe.matmul(pL[c][:, 0:size], xnT[:, par], win[:, CHUNKS[c]], start=True, stop=False)
                        pe.matmul(pL[c][:, 0:size], ones3[:], b3[:, CHUNKS[c]], start=False, stop=True).then_inc(logits[c][par], 1)

                def end(i, par):
                    for g in range(4):
                        for c in range(4):
                            if CHUNKS[c].start < 512 * (g + 1) and CHUNKS[c].stop > 512 * g:
                                pe.wait_ge(masked[c][par], after(i))
                        if g >= 2:
                            pe.wait_ge(aT_made[g - 2][par], after(i))
                        for k in chunk_groups(g):
                            n = rows(k)
                            ins = pe.transpose(pT[g % 2][0:n, (k % 4) * P:(k % 4 + 1) * P], acts[:, par, k * P:k * P + n], ident[:])
                        ins.then_inc(aT_done[g][par], 1)
                    pe.wait_ge(x_done[1 - par], after(i - 1) if par == 0 else after(i))
                    for g in range(4):
                        pe.wait_ge(aT_made[g][par], after(i))
                        for k in chunk_groups(g):
                            n = rows(k)
                            ins = pe.matmul(pY[:, 0:P], actsT[0:n, par, k, :], wout[0:n, k, :], start=(k == 0), stop=(k == NCHUNK - 1))
                    ins.then_inc(y_done[par], 1)

                def step(i, par, before_i, before_par):
                    start(i, par, before_i, before_par)
                    if before_i is not None:
                        end(before_i, before_par)

                tiles(pe, step, end)

        sem.clear()


def entangled_attention(nc, stage, X, ctxT, consts, drams):
    ident, ones = consts["ident"], consts["ones"]
    w_dram, b_dram, bvrow_dram = drams
    with ExitStack() as ctx:
        def sb(name, shape, dt=F32):
            return ctx.enter_context(nc.sbuf_tensor(f"{stage}_{name}", shape, dt))

        def bank(name):
            return ctx.enter_context(nc.psum_tensor(f"{stage}_{name}", [P, 2, T], F32))

        sem = Sems(nc, ctx, stage)
        stats = sb("stats", [P, TILES, 6])
        mean = sb("mean", [P, TILES])
        rstd = sb("rstd", [P, TILES])
        lntmp = sb("lntmp", [P, 4, TILES])
        w = sb("w", [P, 5, P])
        bias = sb("bias", [P, 4])
        bvrow = sb("bvrow", [1, P])
        xn = sb("xn", [P, 2, 2, P])
        xnT = sb("xnT", [P, 2, T])
        kvT = sb("kvT", [P, 2, T])
        qkT = sb("qkT", [P, 2, 2, T])
        vT = sb("vT", [P, 2, T])
        vaug = sb("vaug", [P, 2, 2, P + 1])
        entT = sb("entT", [P, 2, T])
        nmax = sb("nmax", [P, 2, 2])
        prob = sb("prob", [P, 2, 2, T])
        probT = sb("probT", [P, 2, 2, T])
        rsum = sb("rsum", [P, 2, 2])
        pX, pQK, pVT, pV, pE, pS, pPT, pO = (bank(n) for n in ("pX", "pQK", "pVT", "pV", "pE", "pS", "pPT", "pO"))

        def pair(name):
            return [sem(f"{name}{i}") for i in range(2)]

        names = ("xn_made", "xT_done", "xnT_made", "qk_done", "qk_made", "vT_done", "vT_made", "v_done", "v_made",
                 "e_done", "e_made", "s_done", "nmax_made", "exp_done", "t_done", "probT_made", "o_done", "x_done")
        made = {n: pair(n) for n in names}
        (xn_made, xT_done, xnT_made, qk_done, qk_made, vT_done, vT_made, v_done, v_made, e_done, e_made, s_done,
         nmax_made, exp_done, t_done, probT_made, o_done, x_done) = (made[n] for n in names)

        def batches(eng, start, end):
            start(0, 0, None, None)
            start(0, 1, 0, 0)
            end(0, 0)
            with eng.Fori(1, B // 2) as i:
                start(i, 0, i - 1, 1)
                end(i - 1, 1)
                start(i, 1, i, 0)
                end(i, 0)
            end(B // 2 - 1, 1)

        with nc.Block() as block:
            @block.sync
            def _(sp):
                sp.dma_start(w[:], w_dram).then_inc(sem("w_in"), 16)
                sp.dma_start(bias[:], b_dram).then_inc(sem("w_in"), 16)
                sp.dma_start(bvrow[:], bvrow_dram).then_inc(sem("w_in"), 16)

            @block.gpsimd
            def _(pool):
                for s in sum(made.values(), []):
                    pool.sem_inc(s, 1)
                pool.memset(vaug[:, :, :, P:P + 1], 1.0).then_inc(sem("ones_made"), 1)

            @block.vector
            def _(v):
                layernorm_stats(v, sem, X, stats, mean, rstd, lntmp)
                v.wait_ge(sem("w_in"), 48)

                def start(i, par, pi, ppar):
                    v.wait_ge(xT_done[par], before(i))
                    for kt in range(2):
                        tile = i * 4 + par * 2 + kt
                        ins = v.tensor_scalar(xn[:, par, kt, :], X[:, ds(tile, 1), :], mean[:, ds(tile, 1)],
                                              rstd[:, ds(tile, 1)], ALU.subtract, ALU.mult)
                    ins.then_inc(xn_made[par], 1)
                    v.wait_ge(qk_done[par], after(i))
                    v.wait_ge(e_done[par], before(i))
                    v.tensor_scalar(qkT[:, par, 0, :], pQK[:, 0, :], bias[:, 0:1], None, ALU.add)
                    v.tensor_scalar(qkT[:, par, 1, :], pQK[:, 1, :], bias[:, 1:2], None, ALU.add).then_inc(qk_made[par], 1)
                    v.wait_ge(vT_done[par], after(i))
                    v.wait_ge(s_done[par], before(i))
                    v.tensor_scalar(vT[:, par, :], pVT[:, 0, :], bias[:, 2:3], float(P) ** -0.5, ALU.add, ALU.mult)\
                        .then_inc(vT_made[par], 1)

                def end(i, par):
                    v.wait_ge(s_done[par], after(i))
                    v.wait_ge(exp_done[par], before(i))
                    v.tensor_reduce(nmax[:, par, :], pS[:], AX_X, ALU.max, negate=True).then_inc(nmax_made[par], 1)
                    v.wait_ge(t_done[par], after(i))
                    v.wait_ge(o_done[par], before(i))
                    v.tensor_copy(probT[:, par], pPT[:]).then_inc(probT_made[par], 1)
                    chain = sem("out_chain")
                    v.wait_ge(o_done[par], after(i))
                    v.reciprocal(rsum[:, par, :], pO[:, :, P]).then_inc(chain, 1)
                    v.wait_ge(chain, 1)
                    v.sem_clear(chain)
                    for qt in range(2):
                        tile = X[:, ds(i * 4 + par * 2 + qt, 1), :]
                        ins = v.scalar_tensor_tensor(tile, pO[:, qt, 0:P].unsqueeze(1), rsum[:, par, qt:qt + 1], tile, ALU.mult, ALU.add)
                    ins.then_inc(x_done[par], 1)

                batches(v, start, end)

            @block.scalar
            def _(act):
                def start(i, par, pi, ppar):
                    act.wait_ge(xT_done[par], after(i))
                    act.wait_ge(v_done[par], before(i))
                    act.copy(xnT[:, par, :], pX[:, 0, :])
                    act.copy(kvT[:, par, :], ctxT[:, ds((i * 2 + par) * T, T)]).then_inc(xnT_made[par], 1)
                    act.wait_ge(v_done[par], after(i))
                    act.wait_ge(o_done[par], before(i))
                    act.copy(vaug[:, par, :, 0:P], pV[:, :, 0:P]).then_inc(v_made[par], 1)
                    act.wait_ge(e_done[par], after(i))
                    act.wait_ge(s_done[par], before(i))
                    act.activation(entT[:, par, :], pE[:, 0, :], ACT.Tanh, bias=bias[:, 3:4]).then_inc(e_made[par], 1)

                def end(i, par):
                    act.wait_ge(nmax_made[par], after(i))
                    act.wait_ge(t_done[par], before(i))
                    for qt in range(2):
                        ins = act.activation(prob[:, par, qt, :], pS[:, qt, :], ACT.Exp, bias=nmax[:, par, qt:qt + 1])
                    ins.then_inc(exp_done[par], 1)

                act.wait_ge(sem("w_in"), 48)
                batches(act, start, end)

            @block.tensor
            def _(pe):
                pe.wait_ge(sem("w_in"), 48)
                pe.wait_ge(sem("ones_made"), 1)

                def start(i, par, pi, ppar):
                    pe.wait_ge(xn_made[par], after(i))
                    if pi is not None:
                        pe.wait_ge(xnT_made[ppar], after(pi))
                        pe.wait_ge(qk_made[ppar], after(pi))
                        pe.wait_ge(vT_made[ppar], after(pi))
                        pe.wait_ge(v_made[ppar], after(pi))
                        pe.wait_ge(e_made[ppar], after(pi))
                    for kt in range(2):
                        ins = pe.transpose(pX[:, 0, kt * P:(kt + 1) * P], xn[:, par, kt, :], ident[:])
                    ins.then_inc(xT_done[par], 1)
                    pe.wait_ge(xnT_made[par], after(i))
                    pe.matmul(pQK[:, 0, :], w[:, 0, :], xnT[:, par, :], start=True, stop=True)
                    pe.matmul(pQK[:, 1, :], w[:, 1, :], kvT[:, par, :], start=True, stop=True).then_inc(qk_done[par], 1)
                    pe.matmul(pVT[:, 0, :], w[:, 2, :], kvT[:, par, :], start=True, stop=True).then_inc(vT_done[par], 1)
                    for kt in range(2):
                        pe.matmul(pV[:, kt, 0:P], kvT[:, par, kt * P:(kt + 1) * P], w[:, 2, :], start=True, stop=False)
                        ins = pe.matmul(pV[:, kt, 0:P], ones[0:1, :], bvrow[:], start=False, stop=True)
                    ins.then_inc(v_done[par], 1)
                    pe.wait_ge(qk_made[par], after(i))
                    pe.matmul(pE[:, 0, :], w[:, 3, :], qkT[:, par, 0, :], start=True, stop=False)
                    pe.matmul(pE[:, 0, :], w[:, 4, :], qkT[:, par, 1, :], start=False, stop=True).then_inc(e_done[par], 1)

                def end(i, par):
                    other, oi = (1, i - 1) if par == 0 else (0, i)
                    pe.wait_ge(e_made[par], after(i))
                    pe.wait_ge(vT_made[par], after(i))
                    pe.wait_ge(exp_done[other], after(oi))
                    for qt in range(2):
                        ins = pe.matmul(pS[:, qt, :], entT[:, par, qt * P:(qt + 1) * P], vT[:, par, :], start=True, stop=True)
                    ins.then_inc(s_done[par], 1)
                    pe.wait_ge(exp_done[par], after(i))
                    pe.wait_ge(probT_made[other], after(oi))
                    for kt in range(2):
                        for qt in range(2):
                            ins = pe.transpose(pPT[:, kt, qt * P:(qt + 1) * P], prob[:, par, qt, kt * P:(kt + 1) * P], ident[:])
                    ins.then_inc(t_done[par], 1)
                    pe.wait_ge(probT_made[par], after(i))
                    pe.wait_ge(v_made[par], after(i))
                    pe.wait_ge(x_done[other], after(oi))
                    for qt in range(2):
                        for kt in range(2):
                            ins = pe.matmul(pO[:, qt, 0:P + 1], probT[:, par, kt, qt * P:(qt + 1) * P], vaug[:, par, kt, :],
                                            start=(kt == 0), stop=(kt == 1))
                    ins.then_inc(o_done[par], 1)

                batches(pe, start, end)

        sem.clear()


NH = 8
HW = 64
K = T // 8
MASKED = -1e30


def route_tokens(nc, stage, X, consts, shared, drams):
    ident = consts["ident"]
    xn_all, xnT_all, slots = shared
    with ExitStack() as ctx:
        def sb(name, shape, dt=F32):
            return ctx.enter_context(nc.sbuf_tensor(f"{stage}r_{name}", shape, dt))

        def bank(name):
            return ctx.enter_context(nc.psum_tensor(f"{stage}r_{name}", [P, 2, T], F32))

        sem = Sems(nc, ctx, stage + "r")
        ROWS = NH * B
        stats = sb("stats", [P, TILES, 6])
        mean = sb("mean", [P, TILES])
        rstd = sb("rstd", [P, TILES])
        lntmp = sb("lntmp", [P, 4, TILES])
        router = sb("router", [P, NH])
        xn = sb("xn", [P, 2, 2, P])
        scores8 = sb("scores8", [NH, B, T])
        scores = sb("scores", [ROWS, T])
        rest = sb("rest", [ROWS, T])
        taken = sb("taken", [ROWS, T])
        onesr = sb("onesr", [ROWS, T])
        slotgate = sb("slotgate", [ROWS, 2, T])
        m8 = sb("m8", [ROWS, 4, 8])
        pX = [bank(f"pX{i}") for i in range(2)]
        pR = [bank(f"pR{i}") for i in range(2)]
        pT = bank("pT")

        def pair(name):
            return [sem(f"{name}{i}") for i in range(2)]

        xn_made, xT_done, xnT_made, r_done, r_made = (pair(n) for n in ("xn_made", "xT_done", "xnT_made", "r_done", "r_made"))

        with nc.Block() as block:
            @block.sync
            def _(sp):
                sp.dma_start(router[:], drams["router"]).then_inc(sem("w_in"), 16)
                for par in range(2):
                    sp.wait_ge(r_made[par], after(B // 2 - 1))
                sp.dma_start(scores[:], scores8[:].rearrange("n b t -> n (b t)")).then_inc(sem("scores_in"), 16)
                sp.wait_ge(sem("scores_in"), 16)

            @block.gpsimd
            def _(pool):
                for s in xn_made + xT_done + xnT_made + r_done + r_made + [sem("kept0"), sem("kept1")]:
                    pool.sem_inc(s, 1)
                pool.memset(onesr[:], 1.0).then_inc(sem("ones_made"), 1)
                with pool.Fori(0, B // 2) as i:
                    for par in range(2):
                        pool.wait_ge(xn_made[par], after(i))
                        pool.tensor_copy(xn_all[:, ds(i * 4 + par * 2, 2), :], xn[:, par]).then_inc(sem(f"kept{par}"), 1)

            @block.vector
            def _(v):
                layernorm_stats(v, sem, X, stats, mean, rstd, lntmp)
                with v.Fori(0, B // 2) as i:
                    for par in range(2):
                        v.wait_ge(xT_done[par], before(i))
                        v.wait_ge(sem(f"kept{par}"), before(i))
                        for kt in range(2):
                            tile = i * 4 + par * 2 + kt
                            ins = v.tensor_scalar(xn[:, par, kt, :], X[:, ds(tile, 1), :], mean[:, ds(tile, 1)],
                                                  rstd[:, ds(tile, 1)], ALU.subtract, ALU.mult)
                        ins.then_inc(xn_made[par], 1)
                chain = sem("topk_chain")
                n = [0]

                def step(ins):
                    n[0] += 1
                    ins.then_inc(chain, 1)
                    v.wait_ge(chain, n[0])

                v.wait_ge(sem("scores_in"), 16)
                src = scores
                for rnd in range(K // 8):
                    step(v.max(m8[:, rnd, :], src[:]))
                    step(v.match_replace(rest[:], m8[:, rnd, :], src[:], LOW))
                    src = rest
                step(v.tensor_scalar(taken[:], rest[:], LOW, None, ALU.is_equal))
                v.wait_ge(sem("ones_made"), 1)
                step(v.tensor_tensor_scan(slotgate[:, 0, :], onesr[:], taken[:], 0.0, ALU.mult, ALU.add))
                v.tensor_tensor(slotgate[:, 0, :], slotgate[:, 0, :], taken[:], ALU.mult).then_inc(sem("slots_made"), 1)
                v.wait_ge(sem("tanh_made"), 1)
                v.tensor_scalar(slotgate[:, 1, :], scores[:], 0.5, 0.5, ALU.mult, ALU.add).then_inc(sem("slots_made"), 1)
                v.wait_ge(sem("slots_transposed"), 1)
                v.tensor_copy(slots[:], pT[:].rearrange("p a (k r) -> p (a k r)", k=4)[:, 0:4 * ROWS].rearrange("p (k r) -> p k r", r=ROWS))

            @block.scalar
            def _(act):
                with act.Fori(0, B // 2) as i:
                    for par in range(2):
                        act.wait_ge(xT_done[par], after(i))
                        act.copy(xnT_all[:, ds((i * 2 + par) * T, T)], pX[par][:, 0, :]).then_inc(xnT_made[par], 1)
                    for par in range(2):
                        act.wait_ge(r_done[par], after(i))
                        act.copy(scores8[:, ds(i * 2 + par, 1), :], pR[par][0:NH, 0, :].unsqueeze(1)).then_inc(r_made[par], 1)
                act.wait_ge(sem("slots_made"), 1)
                act.activation(scores[:], scores[:], ACT.Tanh, scale=0.5).then_inc(sem("tanh_made"), 1)

            @block.tensor
            def _(pe):
                pe.wait_ge(sem("w_in"), 16)
                with pe.Fori(0, B // 2) as i:
                    for par in range(2):
                        pe.wait_ge(xn_made[par], after(i))
                        pe.wait_ge(xnT_made[par], before(i))
                        for kt in range(2):
                            ins = pe.transpose(pX[par][:, 0, kt * P:(kt + 1) * P], xn[:, par, kt, :], ident[:])
                        ins.then_inc(xT_done[par], 1)
                    for par in range(2):
                        pe.wait_ge(xnT_made[par], after(i))
                        pe.wait_ge(r_made[par], before(i))
                        pe.matmul(pR[par][0:NH, 0, :], router[:], xnT_all[:, ds((i * 2 + par) * T, T)], start=True, stop=True)\
                            .then_inc(r_done[par], 1)
                pe.wait_ge(sem("slots_made"), 2)
                flat = pT[:].rearrange("p a t -> p (a t)")
                for a in range(2):
                    for kt in range(2):
                        at = (a * 2 + kt) * ROWS
                        ins = pe.transpose(flat[:, at:at + ROWS], slotgate[:, a, kt * P:(kt + 1) * P], ident[0:ROWS, 0:ROWS])
                ins.then_inc(sem("slots_transposed"), 1)

        sem.clear()


def dense_heads(nc, stage, X, consts, shared, drams):
    ident = consts["ident"]
    xn_all, xnT_all, slots = shared
    HP = NH // 2
    with ExitStack() as ctx:
        def sb(name, shape, dt=F32):
            return ctx.enter_context(nc.sbuf_tensor(f"{stage}d_{name}", shape, dt))

        def bank(name, shape=(P, 2, T)):
            return ctx.enter_context(nc.psum_tensor(f"{stage}d_{name}", list(shape), F32))

        sem = Sems(nc, ctx, stage + "d")
        w = sb("w", [P, 5, HP, P])
        wo = sb("wo", [P, HP, P])
        rope = sb("rope", [P, 4, T])
        identb = sb("identb", [P, P], BF16)
        causal = sb("causal", [P, P], BF16)
        xb = sb("xb", [P, T])
        r = sb("r", [P, 2, 2, T])
        r2 = sb("r2", [P, 2, 2, T])
        vaug = sb("vaug", [P, 2, 2, 2, HW + 1])
        nmax = sb("nmax", [P, 2, 2, 2])
        prob = sb("prob", [P, 2, 2, 2, T])
        probT = sb("probT", [P, 2, 3, P])
        rsum = sb("rsum", [P, 2, 2, 2])
        on = sb("on", [P, 2, HP, 2, HW])
        onT = sb("onT", [P, 2, HP, P])
        pA, pC, pV, pPT, pO, pM = (bank(n) for n in ("pA", "pC", "pV", "pPT", "pO", "pM"))
        pS = bank("pS", (P, 2, 2, T))

        def pair(name):
            return [sem(f"{name}{i}") for i in range(2)]

        names = ("qk_done", "r_made", "v_done", "v_made", "s_done", "nmax_made", "exp_done", "t0_done", "t1_done",
                 "probT0_made", "probT1_made", "o_done", "on_made")
        made = {n: pair(n) for n in names}
        (qk_done, r_made, v_done, v_made, s_done, nmax_made, exp_done, t0_done, t1_done, probT0_made, probT1_made,
         o_done, on_made) = (made[n] for n in names)
        t_done, probT_made = (t0_done, t1_done), (probT0_made, probT1_made)
        batch_names = ("xb_made", "oT0_done", "oT1_done", "onT0_made", "onT1_made", "y_done", "x_done")
        bmade = {n: sem(n) for n in batch_names}
        xb_made, oT0_done, oT1_done, onT0_made, onT1_made, y_done, x_done = (bmade[n] for n in batch_names)
        BLOCKS = ((0, 0), (0, 1), (1, 1))

        def units(eng, start, end, finish, begin=None):
            with eng.Fori(0, B) as b:
                def at(hp):
                    return b, hp, b * 2 + hp // 2, hp % 2
                if begin:
                    begin(b)
                start(*at(0))
                for hp in range(1, HP):
                    start(*at(hp))
                    end(*at(hp - 1))
                end(*at(HP - 1))
                finish(b)

        def last(i, par):
            return (i - 1, 1) if par == 0 else (i, 0)

        with nc.Block() as block:
            @block.sync
            def _(sp):
                sp.dma_start(w[:], drams["dense_w"]).then_inc(sem("w_in"), 16)
                sp.dma_start(wo[:], drams["dense_wo"]).then_inc(sem("w_in"), 16)
                sp.dma_start(rope[:], drams["dense_rope"]).then_inc(sem("w_in"), 16)

            @block.gpsimd
            def _(pool):
                for s in sum(made.values(), []) + list(bmade.values()):
                    pool.sem_inc(s, 1)
                c = sem("mask_made")
                pool.memset(causal[:], 0.0).then_inc(c, 1)
                pool.memset(vaug[:, :, :, :, HW:HW + 1], 1.0).then_inc(c, 1)
                pool.tensor_copy(identb[:], ident[:]).then_inc(c, 1)
                pool.wait_ge(c, 3)
                pool.affine_select(out=causal[:], in_=causal[:], compare_op=ALU.is_ge, fill=MASKED, base=0,
                                   pattern=[[-1, P]], channel_multiplier=1).then_inc(c, 1)
                with pool.Fori(0, B) as b:
                    pool.wait_ge(v_done[1], b * 2 + 1)
                    pool.tensor_copy(xb[:], xnT_all[:, ds(b * T, T)]).then_inc(xb_made, 1)

            @block.vector
            def _(v):
                v.wait_ge(sem("w_in"), 48)
                chain = sem("rope_chain")
                ochain = sem("out_chain")

                def start(b, hp, i, par):
                    v.wait_ge(qk_done[par], after(i))
                    v.wait_ge(s_done[par], before(i))
                    v.tensor_tensor(r[:, par], pA[:], rope[:, 0:2, :], ALU.mult).then_inc(chain, 1)
                    v.tensor_tensor(r2[:, par], pC[:], rope[:, 2:4, :], ALU.mult).then_inc(chain, 1)
                    v.wait_ge(chain, 2)
                    v.sem_clear(chain)
                    v.tensor_tensor(r[:, par], r[:, par], r2[:, par], ALU.add).then_inc(r_made[par], 1)

                def end(b, hp, i, par):
                    v.wait_ge(s_done[par], after(i))
                    v.wait_ge(exp_done[par], before(i))
                    v.tensor_reduce(nmax[:, par, 0, :], pS[:, :, 0, 0:P], AX_X, ALU.max, negate=True)
                    v.tensor_reduce(nmax[:, par, 1, :], pS[:, :, 1, :], AX_X, ALU.max, negate=True).then_inc(nmax_made[par], 1)
                    li, lp = last(i, par)
                    v.wait_ge(t_done[0][par], after(i))
                    v.wait_ge(o_done[lp], after(li))
                    v.tensor_copy(probT[:, 0], pPT[:].rearrange("p a t -> p (a t)")[:, 0:3 * P].rearrange("p (k q) -> p k q", k=3))\
                        .then_inc(probT_made[0][par], 1)
                    v.wait_ge(o_done[par], after(i))
                    v.wait_ge(oT1_done, b + 1)
                    o = pO[:].rearrange("p a t -> p (a t)")[:, 0:4 * (HW + 1)].rearrange("p (q x d) -> p q x d", q=2, x=2)
                    v.reciprocal(rsum[:, par], o[:, :, :, HW]).then_inc(ochain, 1)
                    v.wait_ge(ochain, 1)
                    v.sem_clear(ochain)
                    v.tensor_tensor(on[:, :, hp], o[:, :, :, 0:HW], rsum[:, par].unsqueeze(3).broadcast_to([P, 2, 2, HW]),
                                    ALU.mult).then_inc(on_made[par], 1)

                def finish(b):
                    v.wait_ge(oT1_done, after(b))
                    v.wait_ge(y_done, before(b))
                    v.tensor_copy(onT[:, 1], pPT[:].rearrange("p a (k q) -> p (a k) q", k=2)).then_inc(onT1_made, 1)
                    v.wait_ge(y_done, after(b))
                    v.tensor_tensor(X[:, ds(b * 2, 2), :], X[:, ds(b * 2, 2), :], pM[:, :, 0:P], ALU.add).then_inc(x_done, 1)

                units(v, start, end, finish)

            @block.scalar
            def _(act):
                def start(b, hp, i, par):
                    act.wait_ge(v_done[par], after(i))
                    act.wait_ge(o_done[par], before(i))
                    act.copy(vaug[:, par, :, :, 0:HW], pV[:, :, 0:P].rearrange("p k (x d) -> p k x d", x=2)).then_inc(v_made[par], 1)

                def end(b, hp, i, par):
                    act.wait_ge(nmax_made[par], after(i))
                    act.wait_ge(t_done[1][par], before(i))
                    for x in range(2):
                        for qt in range(2):
                            n = (qt + 1) * P
                            ins = act.activation(prob[:, par, x, qt, 0:n], pS[:, x, qt, 0:n], ACT.Exp, bias=nmax[:, par, qt, x:x + 1])
                    ins.then_inc(exp_done[par], 1)
                    li, lp = last(i, par)
                    act.wait_ge(t_done[1][par], after(i))
                    act.wait_ge(o_done[lp], after(li))
                    act.copy(probT[:, 1], pPT[:].rearrange("p a t -> p (a t)")[:, 0:3 * P].rearrange("p (k q) -> p k q", k=3))\
                        .then_inc(probT_made[1][par], 1)

                def finish(b):
                    act.wait_ge(oT0_done, after(b))
                    act.wait_ge(y_done, before(b))
                    act.copy(onT[:, 0], pM[:].rearrange("p a (k q) -> p (a k) q", k=2)).then_inc(onT0_made, 1)

                units(act, start, end, finish)

            @block.tensor
            def _(pe):
                pe.wait_ge(sem("w_in"), 48)
                pe.wait_ge(sem("mask_made"), 4)

                def start(b, hp, i, par):
                    li, lp = last(i, par)
                    if hp == 0:
                        pe.wait_ge(xb_made, after(b))
                    pe.wait_ge(r_made[lp], after(li))
                    for s in range(2):
                        pe.matmul(pA[:, s, :], w[:, 2 * s, hp, :], xb[:], start=True, stop=True)
                        ins = pe.matmul(pC[:, s, :], w[:, 2 * s + 1, hp, :], xb[:], start=True, stop=True)
                    ins.then_inc(qk_done[par], 1)
                    pe.wait_ge(v_made[lp], after(li))
                    for kt in range(2):
                        ins = pe.matmul(pV[:, kt, 0:P], xb[:, kt * P:(kt + 1) * P], w[:, 4, hp, :], start=True, stop=True)
                    ins.then_inc(v_done[par], 1)

                def end(b, hp, i, par):
                    li, lp = last(i, par)
                    pe.wait_ge(r_made[par], after(i))
                    pe.wait_ge(exp_done[lp], after(li))
                    for x in range(2):
                        rows = slice(x * HW, (x + 1) * HW)
                        for qt in range(2):
                            n = (qt + 1) * P
                            q = r[rows, par, 0, qt * P:(qt + 1) * P]
                            if qt:
                                pe.matmul(pS[:, x, qt, 0:P], q, r[rows, par, 1, 0:P], start=True, stop=True)
                            pe.matmul(pS[:, x, qt, n - P:n], q, r[rows, par, 1, n - P:n], start=True, stop=False)
                            ins = pe.matmul(pS[:, x, qt, n - P:n], identb[:], causal[:], start=False, stop=True)
                    ins.then_inc(s_done[par], 1)
                    pe.wait_ge(exp_done[par], after(i))
                    flat = pPT[:].rearrange("p a t -> p (a t)")
                    for x in range(2):
                        if x == 0:
                            pe.wait_ge(probT_made[1][lp], after(li))
                            if hp == 0:
                                pe.wait_ge(onT1_made, before(b))
                        else:
                            pe.wait_ge(probT_made[0][par], after(i))
                        for j, (kt, qt) in enumerate(BLOCKS):
                            ins = pe.transpose(flat[:, j * P:(j + 1) * P], prob[:, par, x, qt, kt * P:(kt + 1) * P], ident[:])
                        ins.then_inc(t_done[x][par], 1)
                    pe.wait_ge(v_made[par], after(i))
                    pe.wait_ge(on_made[lp], after(li))
                    o = pO[:].rearrange("p a t -> p (a t)")[:, 0:4 * (HW + 1)].rearrange("p (q x d) -> p q x d", q=2, x=2)
                    for x in range(2):
                        pe.wait_ge(probT_made[x][par], after(i))
                        pe.matmul(o[:, 0, x, :], probT[:, x, 0, :], vaug[:, par, 0, x, :], start=True, stop=True)
                        pe.matmul(o[:, 1, x, :], probT[:, x, 1, :], vaug[:, par, 0, x, :], start=True, stop=False)
                        ins = pe.matmul(o[:, 1, x, :], probT[:, x, 2, :], vaug[:, par, 1, x, :], start=False, stop=True)
                    ins.then_inc(o_done[par], 1)

                def finish(b):
                    pe.wait_ge(on_made[1], b * 2 + 3)
                    pe.wait_ge(x_done, before(b))
                    for qt, (dst, done) in enumerate(((pM, oT0_done), (pPT, oT1_done))):
                        flat = dst[:].rearrange("p a t -> p (a t)")
                        for hp in range(HP):
                            ins = pe.transpose(flat[:, hp * P:(hp + 1) * P], on[:, qt, hp].rearrange("p x d -> p (x d)"), ident[:])
                        ins.then_inc(done, 1)
                    pe.wait_ge(onT0_made, after(b))
                    pe.wait_ge(onT1_made, after(b))
                    for qt in range(2):
                        for hp in range(HP):
                            ins = pe.matmul(pM[:, qt, 0:P], onT[:, qt, hp, :], wo[:, hp, :], start=(hp == 0), stop=(hp == HP - 1))
                    ins.then_inc(y_done, 1)

                units(pe, start, end, finish)

        sem.clear()


def sparse_heads(nc, stage, X, consts, shared, drams):
    ident = consts["ident"]
    xn_all, xnT_all, slots = shared
    with ExitStack() as ctx:
        def sb(name, shape, dt=F32):
            return ctx.enter_context(nc.sbuf_tensor(f"{stage}m_{name}", shape, dt))

        def bank(name):
            return ctx.enter_context(nc.psum_tensor(f"{stage}m_{name}", [P, 2, T], F32))

        sem = Sems(nc, ctx, stage + "m")
        w = sb("w", [P, NH, 5, HW])
        wo = sb("wo", [HW, NH, P])
        rope = sb("rope", [P, 2, 2, HW])
        slot_no = sb("slot_no", [P, K])
        identb = sb("identb", [P, P], BF16)
        mask = sb("mask", [P, P], BF16)
        xs = sb("xs", [P, 2, P])
        pick = sb("pick", [P, 2, NH, K])
        gated = sb("gated", [P, 2, NH, K])
        xgT = sb("xgT", [P, NH * K])
        tg = sb("tg", [HW, 2, NH * K])
        r = sb("r", [HW, 2, NH * K])
        r2 = sb("r2", [HW, 2, NH * K])
        vaug = sb("vaug", [P, 2, HW + 1])
        nmax = sb("nmax", [P, 2])
        prob = sb("prob", [P, 2, P])
        probT = sb("probT", [P, 2, P])
        rsum = sb("rsum", [P, 2])
        av = sb("av", [P, 2, HW])
        avT = sb("avT", [HW, 2, P])
        z = sb("z", [P, 2, P])
        gT = sb("gT", [P, 2, T])
        pG, pQ, pQs, pV, pS, pT, pO, pY = (bank(n) for n in ("pG", "pQ", "pQs", "pV", "pS", "pT", "pO", "pY"))
        names = ("xs_made", "pick_made", "gated_made", "xg_done", "xg_made", "tg_done", "tg_made", "q_done", "r_made", "v_done", "v_made",
                 "s_done", "nmax_made", "exp_done", "t_done", "probT_made", "o_done", "av_made", "avT_done", "avT_made",
                 "z_done", "z_made", "gT_done", "gT_made", "y_done", "x_done")
        made = {n: sem(n) for n in names}

        with nc.Block() as block:
            @block.sync
            def _(sp):
                sp.dma_start(w[:], drams["mosa_w"]).then_inc(sem("w_in"), 16)
                sp.dma_start(wo[:], drams["mosa_wo"]).then_inc(sem("w_in"), 16)
                sp.dma_start(rope[:], drams["mosa_rope"]).then_inc(sem("w_in"), 16)

            @block.gpsimd
            def _(pool):
                for s in made.values():
                    pool.sem_inc(s, 1)
                c = sem("mask_made")
                pool.memset(mask[:], 0.0).then_inc(c, 1)
                pool.memset(vaug[:, :, HW:HW + 1], 1.0).then_inc(c, 1)
                pool.tensor_copy(identb[:], ident[:]).then_inc(c, 1)
                pool.iota(slot_no[:], pattern=[[1, K]], base=1, channel_multiplier=0,
                          allow_small_or_imprecise_dtypes=True).then_inc(c, 1)
                pool.wait_ge(c, 4)
                pool.affine_select(out=mask[:], in_=mask[:], compare_op=ALU.is_ge, fill=MASKED, base=0,
                                   pattern=[[-1, P]], channel_multiplier=1).then_inc(c, 1)
                pool.wait_ge(c, 5)
                pool.affine_select(out=mask[:].rearrange("p (h k) -> p h k", k=K), in_=mask[:].rearrange("p (h k) -> p h k", k=K),
                                   compare_op=ALU.is_ge, fill=MASKED, base=K - 1,
                                   pattern=[[K, P // K], [0, K]], channel_multiplier=-1).then_inc(c, 1)
                with pool.Fori(0, B) as b:
                    pool.wait_ge(made["xg_done"], before(b))
                    pool.tensor_copy(xs[:], xn_all[:, ds(b * 2, 2), :]).then_inc(made["xs_made"], 1)

            @block.vector
            def _(v):
                v.wait_ge(sem("w_in"), 48)
                v.wait_ge(sem("mask_made"), 6)
                chain = sem("rope_chain")
                ochain = sem("out_chain")
                with v.Fori(0, B) as b:
                    v.wait_ge(made["tg_done"], before(b))
                    sl = slots[:].rearrange("p k (n b) -> p k n b", b=B)[:, :, :, ds(b, 1)]
                    v.tensor_tensor(pick[:], sl[:, 0:2].broadcast_to([P, 2, NH, K]),
                                    slot_no[:].unsqueeze(1).unsqueeze(1).broadcast_to([P, 2, NH, K]), ALU.is_equal)\
                        .then_inc(made["pick_made"], 1)
                    v.wait_ge(made["gT_done"], before(b))
                    v.wait_ge(made["pick_made"], after(b))
                    v.tensor_tensor(gated[:], pick[:], sl[:, 2:4].broadcast_to([P, 2, NH, K]), ALU.mult)\
                        .then_inc(made["gated_made"], 1)
                    v.wait_ge(made["tg_done"], after(b))
                    v.tensor_copy(tg[:], pS[0:HW, :, :]).then_inc(made["tg_made"], 1)
                    v.wait_ge(made["q_done"], after(b))
                    v.wait_ge(made["tg_made"], after(b))
                    q = HW ** -0.5
                    v.scalar_tensor_tensor(r[:, 0, :], pQ[0:HW, 0, :], q, tg[:, 0, :], ALU.mult, ALU.mult).then_inc(chain, 1)
                    v.tensor_tensor(r[:, 1, :], pQ[0:HW, 1, :], tg[:, 0, :], ALU.mult).then_inc(chain, 1)
                    v.scalar_tensor_tensor(r2[:, 0, :], pQs[0:HW, 0, :], q, tg[:, 1, :], ALU.mult, ALU.mult).then_inc(chain, 1)
                    v.tensor_tensor(r2[:, 1, :], pQs[0:HW, 1, :], tg[:, 1, :], ALU.mult).then_inc(chain, 1)
                    v.wait_ge(chain, 4)
                    v.sem_clear(chain)
                    v.tensor_tensor(r[:], r[:], r2[:], ALU.add).then_inc(made["r_made"], 1)
                    v.wait_ge(made["s_done"], after(b))
                    v.tensor_reduce(nmax[:], pS[:, :, 0:P], AX_X, ALU.max, negate=True).then_inc(made["nmax_made"], 1)
                    v.wait_ge(made["t_done"], after(b))
                    v.tensor_copy(probT[:], pT[:, :, 0:P]).then_inc(made["probT_made"], 1)
                    v.wait_ge(made["o_done"], after(b))
                    v.reciprocal(rsum[:], pO[:, :, HW]).then_inc(ochain, 1)
                    v.wait_ge(ochain, 1)
                    v.sem_clear(ochain)
                    v.tensor_tensor(av[:], pO[:, :, 0:HW], rsum[:].unsqueeze(2).broadcast_to([P, 2, HW]), ALU.mult).then_inc(made["av_made"], 1)
                    v.wait_ge(made["avT_done"], after(b))
                    v.tensor_copy(avT[:], pT[0:HW, :, 0:P]).then_inc(made["avT_made"], 1)
                    v.wait_ge(made["y_done"], after(b))
                    v.tensor_tensor(X[:, ds(b * 2, 2), :], X[:, ds(b * 2, 2), :], pY[:, :, 0:P], ALU.add).then_inc(made["x_done"], 1)

            @block.scalar
            def _(act):
                with act.Fori(0, B) as b:
                    act.wait_ge(made["xg_done"], after(b))
                    act.wait_ge(made["v_done"], before(b))
                    act.copy(xgT[:], pG[:, 0, :]).then_inc(made["xg_made"], 1)
                    act.wait_ge(made["v_done"], after(b))
                    act.wait_ge(made["o_done"], before(b))
                    act.copy(vaug[:, :, 0:HW], pV[:, :, 0:HW]).then_inc(made["v_made"], 1)
                    act.wait_ge(made["gT_done"], after(b))
                    act.wait_ge(made["y_done"], before(b))
                    act.copy(gT[:], pY[:]).then_inc(made["gT_made"], 1)
                    act.wait_ge(made["nmax_made"], after(b))
                    for g in range(2):
                        ins = act.activation(prob[:, g, :], pS[:, g, 0:P], ACT.Exp, bias=nmax[:, g:g + 1])
                    ins.then_inc(made["exp_done"], 1)
                    act.wait_ge(made["z_done"], after(b))
                    act.copy(z[:], pG[:, :, 0:P]).then_inc(made["z_made"], 1)

            @block.tensor
            def _(pe):
                pe.wait_ge(sem("w_in"), 48)
                pe.wait_ge(sem("mask_made"), 6)
                with pe.Fori(0, B) as b:
                    pe.wait_ge(made["xs_made"], after(b))
                    pe.wait_ge(made["pick_made"], after(b))
                    pe.wait_ge(made["z_made"], before(b))
                    for kt in range(2):
                        ins = pe.matmul(pG[:, 0, :], xs[:, kt, :], pick[:, kt], start=(kt == 0), stop=(kt == 1))
                    ins.then_inc(made["xg_done"], 1)
                    pe.wait_ge(made["exp_done"], before(b))
                    for a in range(2):
                        for kt in range(2):
                            ins = pe.matmul(pS[0:HW, a, :], rope[:, kt, a, :], pick[:, kt], start=(kt == 0), stop=(kt == 1))
                    ins.then_inc(made["tg_done"], 1)
                    pe.wait_ge(made["gated_made"], after(b))
                    pe.wait_ge(made["x_done"], before(b))
                    for g in range(2):
                        for kt in range(2):
                            ins = pe.transpose(pY[:, g, kt * P:(kt + 1) * P],
                                               gated[:, kt, g * 4:(g + 1) * 4].rearrange("p n k -> p (n k)"), ident[:])
                    ins.then_inc(made["gT_done"], 1)
                    pe.wait_ge(made["xg_made"], after(b))
                    for n in range(NH):
                        xg = xgT[:, n * K:(n + 1) * K]
                        for s in range(2):
                            pe.matmul(pQ[0:HW, s, n * K:(n + 1) * K], w[:, n, 2 * s, :], xg, start=True, stop=True)
                            ins = pe.matmul(pQs[0:HW, s, n * K:(n + 1) * K], w[:, n, 2 * s + 1, :], xg, start=True, stop=True)
                    ins.then_inc(made["q_done"], 1)
                    pe.wait_ge(made["v_made"], before(b))
                    for n in range(NH):
                        rows = slice(n % 4 * K, n % 4 * K + K)
                        ins = pe.matmul(pV[rows, n // 4, 0:HW], xgT[:, n * K:(n + 1) * K], w[:, n, 4, :], start=True, stop=True,
                                        skip_group_check=True)
                    ins.then_inc(made["v_done"], 1)
                    pe.wait_ge(made["r_made"], after(b))
                    for g in range(2):
                        cols = slice(g * P, (g + 1) * P)
                        pe.matmul(pS[:, g, 0:P], r[:, 0, cols], r[:, 1, cols], start=True, stop=False)
                        ins = pe.matmul(pS[:, g, 0:P], identb[:], mask[:], start=False, stop=True)
                    ins.then_inc(made["s_done"], 1)
                    pe.wait_ge(made["exp_done"], after(b))
                    pe.wait_ge(made["avT_made"], before(b))
                    for g in range(2):
                        ins = pe.transpose(pT[:, g, 0:P], prob[:, g, :], ident[:])
                    ins.then_inc(made["t_done"], 1)
                    pe.wait_ge(made["probT_made"], after(b))
                    pe.wait_ge(made["v_made"], after(b))
                    pe.wait_ge(made["av_made"], before(b))
                    for g in range(2):
                        ins = pe.matmul(pO[:, g, 0:HW + 1], probT[:, g, :], vaug[:, g, :], start=True, stop=True)
                    ins.then_inc(made["o_done"], 1)
                    pe.wait_ge(made["av_made"], after(b))
                    pe.sem_inc(sem("waited_pe"), 1)
                    for g in range(2):
                        ins = pe.transpose(pT[0:HW, g, 0:P], av[:, g, :], ident[:])
                    ins.then_inc(made["avT_done"], 1)
                    pe.wait_ge(made["avT_made"], after(b))
                    pe.sem_inc(sem("waited_pe"), 1)
                    for n in range(NH):
                        rows = slice(n % 4 * K, n % 4 * K + K)
                        ins = pe.matmul(pG[rows, n // 4, 0:P], avT[:, n // 4, rows], wo[:, n, :], start=True, stop=True,
                                        skip_group_check=True)
                    ins.then_inc(made["z_done"], 1)
                    pe.wait_ge(made["z_made"], after(b))
                    pe.wait_ge(made["gT_made"], after(b))
                    for qt in range(2):
                        for g in range(2):
                            ins = pe.matmul(pY[:, qt, 0:P], gT[:, g, qt * P:(qt + 1) * P], z[:, g, :], start=(g == 0), stop=(g == 1))
                    ins.then_inc(made["y_done"], 1)

        sem.clear()


def mixed_attention(nc, stage, X, consts, drams):
    with ExitStack() as ctx:
        shared = (
            ctx.enter_context(nc.sbuf_tensor("xn_all", [P, TILES, P], F32)),
            ctx.enter_context(nc.sbuf_tensor("xnT_all", [P, B * T], F32)),
            ctx.enter_context(nc.sbuf_tensor("slots", [P, 4, NH * B], F32)),
        )
        route_tokens(nc, stage, X, consts, shared, drams)
        dense_heads(nc, stage, X, consts, shared, drams)
        sparse_heads(nc, stage, X, consts, shared, drams)


def build(nc, ins, out, stages=(1, 2, 3, 4, 5, 6)):
    with ExitStack() as ctx:
        def sb(name, shape, dt=F32):
            return ctx.enter_context(nc.sbuf_tensor(name, shape, dt))

        X = sb("X", [P, TILES, P])
        ctxT = sb("ctxT", [P, B * T])
        ident = sb("ident", [P, P])
        ones = sb("ones", [P, P])
        stack_ctx = ExitStack()
        qs = stack_ctx.enter_context(nc.sbuf_tensor("qs", [P, UNITS, T], BF16))
        ks = stack_ctx.enter_context(nc.sbuf_tensor("ks", [P, UNITS, T], BF16))
        zeros_ctx = ExitStack()
        zeros = zeros_ctx.enter_context(nc.sbuf_tensor("zeros", [P, H * T // 2], BF16))
        loaded, made, zeroed = (ctx.enter_context(nc.semaphore(n)) for n in ("loaded", "consts_made", "zeroed"))
        consts = {"ident": ident, "ones": ones, "qs": qs, "ks": ks, "zeroed": zeroed, "zeroed_by": 16 * 2}
        with nc.Block() as block:
            @block.sync
            def _(sp):
                sp.dma_start(X[:], ins["x"].rearrange("(t p) d -> p t d", p=P)).then_inc(loaded, 16)
                sp.dma_start(ctxT[:], ins["ctxT"]).then_inc(loaded, 16)
                sp.wait_ge(made, 1)
                for stack in (qs, ks):
                    zero_rows = zeros[DH * len(TERMS):KROWS, :].unsqueeze(1).broadcast_to([KROWS - DH * len(TERMS), 2 * B, H * T // 2])
                    sp.dma_start(stack[DH * len(TERMS):KROWS, 0:UNITS, :].rearrange("p (b h) n -> p b (h n)", h=H // 2),
                                 zero_rows).then_inc(zeroed, 16)
                sp.wait_ge(loaded, 32)
                if 1 not in stages:
                    sp.wait_ge(zeroed, consts["zeroed_by"])

            @block.gpsimd
            def _(pool):
                pool.memset(zeros[:].bitcast(F32), 0.0).then_inc(made, 1)
                pool.memset(ident[:], 0.0).then_inc(made, 1)
                pool.memset(ones[:], 1.0).then_inc(made, 1)
                pool.wait_ge(made, 3)
                pool.affine_select(out=ident[:], in_=ident[:], compare_op=ALU.not_equal, fill=1.0, base=0,
                                   pattern=[[-1, P]], channel_multiplier=1).then_inc(made, 1)

        if 1 in stages:
            head_attention(nc, "s1", X, None, consts, (ins["w1"], None, None, ins["rope1"]), False)
        zeros_ctx.close()
        if 2 in stages:
            head_attention(nc, "s2", X, ctxT, consts, (ins["w2"], ins["b2"], ins["bo2"], ins["rope2"]), False)
        if 3 in stages:
            tree_ffn(nc, "s3", X, consts, (ins["win"], ins["bin"], ins["wout"]))
        if 4 in stages:
            head_attention(nc, "s4", X, None, consts, (ins["w4"], ins["b4"], ins["bo4"], None), True)
        stack_ctx.close()
        if 5 in stages:
            entangled_attention(nc, "s5", X, ctxT, consts, (ins["w5"], ins["b5"], ins["bv5"]))
        if 6 in stages:
            mixed_attention(nc, "s6", X, consts, {k: ins[k] for k in (
                "router", "dense_w", "dense_wo", "dense_rope", "mosa_w", "mosa_wo", "mosa_rope")})

        stored = ctx.enter_context(nc.semaphore("stored"))
        with nc.Block() as block:
            @block.sync
            def _(sp):
                sp.dma_start(out.rearrange("(t p) d -> p t d", p=P), X[:]).then_inc(stored, 16)
                sp.wait_ge(stored, 16)


def swap_pairs(w):
    return w.reshape(w.shape[0], -1, 2)[:, :, ::-1].reshape(w.shape)


def swap_halves(w, d):
    return w.reshape(w.shape[0], -1, 2, d // 2)[:, :, ::-1].reshape(w.shape)


def by_width(w):
    return w.reshape(w.shape[:-1] + (H, DH)).swapaxes(-1, -2).reshape(w.shape)


def rope_tables(angles, signs):
    cos = np.cos(angles).astype(np.float32)
    sin = (np.sin(angles) * signs).astype(np.float32)
    scale = np.float32(DH ** -0.5)
    return by_width(np.stack([cos * scale, cos, sin * scale, sin], axis=0)).transpose(2, 0, 1)


def lay_out(x):
    f = np.float32
    a = {k: np.asarray(v) for k, v in x.items()}
    o = {"x": a["x"].reshape(B * T, P), "ctxT": a["ctx_1024"].reshape(B * T, P).T}
    pos = np.arange(T, dtype=f)[:, None]
    f1 = np.exp(-np.float32(np.log(10000.0)) * np.arange(0, DH, 2, dtype=f) / DH).astype(f)
    ang1 = np.tile(np.repeat((pos * f1).astype(f), 2, axis=1), (1, H))
    o["rope1"] = rope_tables(ang1, np.tile([-1, 1], P // 2).astype(f))
    f2 = (1.0 / 10000.0 ** (np.arange(0, DH, 2, dtype=f) / DH)).astype(f)
    ang2 = np.tile((pos * np.concatenate([f2, f2])).astype(f), (1, H))
    o["rope2"] = rope_tables(ang2, np.tile(np.repeat([-1, 1], DH // 2), H).astype(f))

    def weights(q, k, v, out, swap):
        return np.stack([by_width(q.T), by_width(swap(q.T)), by_width(k.T), by_width(swap(k.T)), v.T, out.T], axis=1)

    def rows(q, k, v, swap):
        return np.stack([by_width(q), by_width(swap(q[None])[0]), by_width(k), by_width(swap(k[None])[0]), v], axis=1)

    def per_head(w):
        return np.repeat(w.reshape((4, DH) + w.shape[1:]), 4, axis=0).reshape((P,) + w.shape[1:])

    halves = lambda w: swap_halves(w, DH)
    o["w1"] = weights(a["L0_attn_W_q"], a["L0_attn_W_k"], a["L0_attn_W_v"], a["L0_attn_W_o"], swap_pairs)
    o["w2"] = weights(a["L0_xattn_Wq"], per_head(a["L0_xattn_Wk"]), per_head(a["L0_xattn_Wv"]), a["L0_xattn_Wo"], halves)
    o["b2"] = rows(a["L0_xattn_bq"], per_head(a["L0_xattn_bk"]), per_head(a["L0_xattn_bv"]), halves)
    o["bo2"] = a["L0_xattn_bo"][None]
    node = [2 ** d - 1 + sum(((pos >> k) & 1) << (d - 1 - k) for k in range(d)) for d in range(DEPTH + 1) for pos in range(2 ** d)]
    order = (np.arange(TREES)[None, :] * NODES + np.array(node)[:, None]).reshape(-1)
    o["win"] = a["L0_ffn_W_in"][order].T
    o["bin"] = a["L0_ffn_b_in"][order][None]
    o["wout"] = a["L0_ffn_W_out"][:, order].T
    o["w4"] = weights(a["L1_attn_Wq"], a["L1_attn_Wk"], a["L1_attn_Wv"], a["L1_attn_Wo"], halves)
    o["b4"] = rows(a["L1_attn_bq"], a["L1_attn_bk"], a["L1_attn_bv"], halves)
    o["bo4"] = a["L1_attn_bo"][None]
    we = a["L1_xattn_We"]
    o["w5"] = np.stack([a["L1_xattn_Wq"].T, a["L1_xattn_Wk"].T, a["L1_xattn_Wv"].T, we[:, :P].T, we[:, P:].T], axis=1)
    o["b5"] = np.stack([a["L1_xattn_bq"], a["L1_xattn_bk"], a["L1_xattn_bv"], a["L1_xattn_be"]], axis=1)
    o["bv5"] = a["L1_xattn_bv"][None]

    ROT = 32

    def swap_rot(w):
        return np.concatenate([w[..., ROT // 2:ROT], w[..., :ROT // 2], w[..., ROT:]], axis=-1)

    inv = (np.float32(10000.0) ** (-np.arange(ROT // 2, dtype=f) / np.float32(ROT // 2))).astype(f)
    ang = (pos * inv).astype(f)
    cos = np.concatenate([np.cos(ang), np.cos(ang), np.ones((T, HW - ROT), f)], axis=1).astype(f)
    sin = np.concatenate([-np.sin(ang), np.sin(ang), np.zeros((T, HW - ROT), f)], axis=1).astype(f)
    o["router"] = a["L1_ffn_mosa_router_w"]
    d = a["L1_ffn_dense_wqkv"]
    q, k, v = d[..., :HW], d[..., HW:2 * HW], d[..., 2 * HW:]
    o["dense_w"] = np.stack([q, swap_rot(q), k, swap_rot(k), v], axis=1).reshape(P, 5, NH // 2, P)
    o["dense_wo"] = a["L1_ffn_dense_wo"].reshape(NH // 2, P, P).transpose(1, 0, 2)
    eighth = np.float32(HW ** -0.5)
    o["dense_rope"] = np.tile(np.stack([cos * eighth, cos, sin * eighth, sin]).transpose(2, 0, 1), (2, 1, 1))
    m = a["L1_ffn_mosa_wqkv"]
    q, k, v = m[..., :HW], m[..., HW:2 * HW], m[..., 2 * HW:]
    o["mosa_w"] = np.stack([q, swap_rot(q), k, swap_rot(k), v], axis=2)
    o["mosa_wo"] = a["L1_ffn_mosa_wo"].reshape(NH, HW, P).transpose(1, 0, 2)
    o["mosa_rope"] = np.stack([cos, sin], axis=1).reshape(2, P, 2, HW).transpose(1, 0, 2, 3)
    return {k: np.ascontiguousarray(v) for k, v in o.items()}


def kernel(**inputs):
    import concourse.bacc as bacc
    from concourse.bass_utils import run_bass_kernel_spmd

    arrays = lay_out(inputs)
    nc = bacc.Bacc("TRN2", target_bir_lowering=False, num_devices=1)
    ins = {k: nc.dram_tensor(f"in_{k}", v.shape, mybir.dt.from_np(v.dtype), kind="ExternalInput").ap()
           for k, v in arrays.items()}
    out = nc.dram_tensor("out_0", (B * T, P), F32, kind="ExternalOutput").ap()
    build(nc, ins, out)
    r = run_bass_kernel_spmd(nc, [{f"in_{k}": v for k, v in arrays.items()}], core_ids=[0])
    return r.results[0]["out_0"].reshape(B, T, P)
```

```python
from contextlib import ExitStack

import numpy as np
import concourse.bass as bass
from concourse import mybir

ALU = mybir.AluOpType
ACT = mybir.ActivationFunctionType
AX_X = mybir.AxisListType.X
F32 = mybir.dt.float32
BF16 = mybir.dt.bfloat16
I32 = mybir.dt.int32
ds = bass.ds

P = 128
B = 8
T = 256
TILES = B * T // P
H = 16
DH = P // H
UNITS = B * H
BPAIRS = B // 2
TAIL = 4
SLOTS = 4
ROUNDS = UNITS // SLOTS
COLS = P // SLOTS
TOPK = 32
TERMS = ((0, 0), (0, 1), (0, 2), (1, 0), (1, 1), (2, 0))
KROWS = 72
LOW = -3.0e38
EPS = 1e-5


class Sems:

    def __init__(self, nc, ctx, stage):
        self.nc, self.ctx, self.stage, self.made = nc, ctx, stage, {}

    def __call__(self, name):
        if name not in self.made:
            self.made[name] = self.ctx.enter_context(self.nc.semaphore(f"{self.stage}_{name}"))
        return self.made[name]

    def clear(self):
        numbers = sorted(s.num for s in self.made.values())
        first = 0
        for i in range(1, len(numbers) + 1):
            if i == len(numbers) or numbers[i] != numbers[i - 1] + 1:
                self.nc.gpsimd.sem_clear(range(numbers[first], numbers[i - 1] + 1))
                first = i
        self.nc.all_engine_barrier()


def layernorm_stats(v, sem, X, stats, mean, rstd, tmp):
    chain = sem("ln_chain")
    with v.Fori(0, TILES // 8) as t:
        for k in range(8):
            v.bn_stats(stats[:, ds(t * 8 + k, 1), :], X[:, ds(t * 8 + k, 1), :]).then_inc(sem("ln_stats"), 1)
    v.wait_ge(sem("ln_stats"), TILES)
    me, ve, mo, vo = (stats[:, :, i] for i in (1, 2, 4, 5))
    n = [0]

    def step(ins):
        n[0] += 1
        ins.then_inc(chain, 1)
        v.wait_ge(chain, n[0])

    var, y, y2, d = (tmp[:, i, :] for i in range(4))
    step(v.tensor_tensor(mean[:], me, mo, ALU.add))
    step(v.tensor_scalar(mean[:], mean[:], 0.5, None, ALU.mult))
    step(v.tensor_tensor(d, me, mo, ALU.subtract))
    step(v.scalar_tensor_tensor(d, d, 0.25, d, ALU.mult, ALU.mult))
    step(v.tensor_tensor(var, ve, vo, ALU.add))
    step(v.scalar_tensor_tensor(var, var, 1.0 / P, d, ALU.mult, ALU.add))
    step(v.tensor_scalar(var, var, EPS, None, ALU.add))
    step(v.tensor_scalar(y.bitcast(I32), var.bitcast(I32), 1, None, ALU.logical_shift_right))
    step(v.tensor_scalar(y.bitcast(I32), y.bitcast(I32), -1.0, float(0x5F3759DF), ALU.mult, ALU.add))
    for i in range(3):
        step(v.tensor_tensor(y2, y, y, ALU.mult))
        step(v.scalar_tensor_tensor(y2, y2, -0.5, var, ALU.mult, ALU.mult))
        step(v.scalar_tensor_tensor(rstd[:] if i == 2 else y, y2, 1.5, y, ALU.add, ALU.mult))


def before(i):
    return i + 1


def after(i):
    return i + 2


def by_batch(t):
    return t.rearrange("p k (c h a) d -> p k c h a d", h=H, a=2)


def stack_part(sp, i, part, tensors, stacked):
    qs, ks, parts = tensors[0], tensors[1], tensors[-1]
    for side, stack in ((0, qs), (1, ks)):
        for t, term in enumerate(TERMS):
            if term[side] == part:
                sp.dma_start(stack[DH * t:DH * (t + 1), i * 2 * H:(i + 1) * 2 * H, :].rearrange("d (h a) n -> d h (a n)", a=2),
                             parts[:, i, part, side].rearrange("p a n -> p (a n)")).then_inc(stacked, 16)


def prepare_heads(nc, stage, X, ctx_dram, consts, tensors, drams, topk):
    ident = consts["ident"]
    _, _, vaug, w, bias, bo, parts = tensors
    w_dram, b_dram, bo_dram, rope_dram = drams
    with ExitStack() as ctx:
        def sb(name, shape, dt=F32):
            return ctx.enter_context(nc.sbuf_tensor(f"{stage}_{name}", shape, dt))

        def bank(name):
            return ctx.enter_context(nc.psum_tensor(f"{stage}_{name}", [P, 2, T], F32))

        sem = Sems(nc, ctx, stage + "p")
        stats = sb("stats", [P, TILES, 6])
        mean = sb("mean", [P, TILES])
        rstd = sb("rstd", [P, TILES])
        lntmp = sb("lntmp", [P, 4, TILES])
        xn = sb("xn", [P, 2, 2, P])
        xnT = sb("xnT", [P, 2, T])
        kvT = sb("kvT", [P, 2, T]) if ctx_dram is not None else xnT
        ctxT = sb("ctxT", [P, B * T]) if ctx_dram is not None else None
        r = sb("r", [P, 2, 2, T])
        r2 = sb("r2", [P, 2, 2, T]) if not topk else None
        d1 = sb("d1", [P, 2, 2, T])
        rope = sb("rope", [P, 4, T]) if not topk else None
        pT = [bank(f"pT{i}")[:, 0, :] for i in range(2)]
        pA = [bank(f"pA{i}") for i in range(2)]
        pB = [bank(f"pB{i}") for i in range(2)]
        pV = [bank(f"pV{i}")[:, :, 0:P] for i in range(2)]

        def pair(name):
            return [sem(f"{name}{i}") for i in range(2)]

        xn_made, xT_done, xnT_made, qk_done, v_done, v_made, r_made, part0_made, d1_made, part1_made, part2_made = (
            pair(n) for n in ("xn_made", "xT_done", "xnT_made", "qk_done", "v_done", "v_made", "r_made", "part0_made",
                              "d1_made", "part1_made", "part2_made"))
        credited = xT_done + xnT_made + v_done + v_made + r_made + d1_made + xn_made + qk_done + part0_made + part1_made + part2_made

        def chunks(eng, body):
            with eng.Fori(0, BPAIRS - 1) as i:
                body(i, True)
            body(BPAIRS - 1, False)

        w_in, rope_in = sem("w_in"), sem("rope_in")

        with nc.Block() as block:
            @block.sync
            def _(sp):
                sp.dma_start(w[:], w_dram).then_inc(w_in, 16)
                if b_dram is not None:
                    sp.dma_start(bias[:], b_dram).then_inc(w_in, 16)
                    sp.dma_start(bo[:], bo_dram).then_inc(w_in, 16)
                if rope is not None:
                    sp.dma_start(rope[:], rope_dram).then_inc(rope_in, 16)
                if ctxT is not None:
                    sp.dma_start(ctxT[:], ctx_dram).then_inc(sem("ctx_in"), 16)

                for i in range(BPAIRS // 2):
                    for part, made in enumerate((part0_made, part1_made, part2_made)):
                        sp.wait_ge(made[0], after(i))
                        sp.wait_ge(made[1], after(i))
                        stack_part(sp, i, part, tensors, consts["stacked"][0])

            @block.gpsimd
            def _(pool):
                for s in credited:
                    pool.sem_inc(s, 1)
                pool.memset(vaug[:, :, :, DH:DH + 1], 1.0).then_inc(sem("ones_made"), 1)
                if b_dram is None:
                    pool.memset(bias[:], 0.0).then_inc(w_in, 16)
                    pool.memset(bo[:], 0.0).then_inc(w_in, 16)
                def split_chunk(i, more):
                    for par in range(2):
                        pool.wait_ge(part0_made[par], after(i))
                        pool.tensor_tensor(d1[:, par].unsqueeze(1), r[:, par].unsqueeze(1), parts[:, ds(i, 1), 0, :, par], ALU.subtract).then_inc(d1_made[par], 1)
                        pool.wait_ge(part1_made[par], after(i))
                        pool.tensor_tensor(parts[:, ds(i, 1), 2, :, par], d1[:, par].unsqueeze(1), parts[:, ds(i, 1), 1, :, par], ALU.subtract)\
                            .then_inc(part2_made[par], 1)

                chunks(pool, split_chunk)

            @block.vector
            def _(v):
                layernorm_stats(v, sem, X, stats, mean, rstd, lntmp)
                v.wait_ge(w_in, 48)
                if rope is not None:
                    v.wait_ge(rope_in, 16)
                chain = sem("rope_chain")
                def normalise_chunk(i):
                    for par in range(2):
                        v.wait_ge(xT_done[par], before(i))
                        for kt in range(2):
                            tile = i * 4 + par * 2 + kt
                            ins = v.tensor_scalar(xn[:, par, kt, :], X[:, ds(tile, 1), :], mean[:, ds(tile, 1)],
                                                  rstd[:, ds(tile, 1)], ALU.subtract, ALU.mult)
                        ins.then_inc(xn_made[par], 1)

                def rotate_chunk(i, more):
                    if more:
                        normalise_chunk(i + 1)
                    for par in range(2):
                        A, C = pA[par], pB[par]
                        v.wait_ge(qk_done[par], after(i))
                        v.wait_ge(d1_made[par], before(i))
                        if topk:
                            v.tensor_scalar(r[:, par, 0, :], A[:, 0, :], bias[:, 0:1], DH ** -0.5, ALU.add, ALU.mult)
                            v.tensor_scalar(r[:, par, 1, :], A[:, 1, :], bias[:, 2:3], None, ALU.add).then_inc(r_made[par], 1)
                        else:
                            for s in range(2):
                                v.scalar_tensor_tensor(r[:, par, s, :], A[:, s, :], bias[:, 2 * s:2 * s + 1], rope[:, s, :],
                                                       ALU.add, ALU.mult).then_inc(chain, 1)
                                v.scalar_tensor_tensor(r2[:, par, s, :], C[:, s, :], bias[:, 2 * s + 1:2 * s + 2],
                                                       rope[:, 2 + s, :], ALU.add, ALU.mult).then_inc(chain, 1)
                            v.wait_ge(chain, 4)
                            v.sem_clear(chain)
                            v.tensor_tensor(r[:, par], r[:, par], r2[:, par], ALU.add).then_inc(r_made[par], 1)

                normalise_chunk(0)
                chunks(v, rotate_chunk)

            @block.scalar
            def _(act):
                def copy_xnT(i, par):
                    act.wait_ge(xT_done[par], after(i))
                    act.wait_ge(v_done[par], before(i))
                    ins = act.copy(xnT[:, par, :], pT[par])
                    if ctxT is not None:
                        ins = act.copy(kvT[:, par, :], ctxT[:, ds((i * 2 + par) * T, T)])
                    ins.then_inc(xnT_made[par], 1)

                def copy_chunk(i, more):
                    for par in range(2):
                        act.wait_ge(v_done[par], after(i))
                        act.copy(by_batch(vaug)[:, :, ds(i, 1), :, par, 0:DH].rearrange("p k c h d -> p k (c h) d"),
                                 pV[par].rearrange("p k (h d) -> p k h d", d=DH)).then_inc(v_made[par], 1)
                        if more:
                            copy_xnT(i + 1, par)
                        act.wait_ge(r_made[par], after(i))
                        act.copy(parts[:, ds(i, 1), 0, :, par], r[:, par].unsqueeze(1)).then_inc(part0_made[par], 1)
                    for par in range(2):
                        act.wait_ge(d1_made[par], after(i))
                        act.copy(parts[:, ds(i, 1), 1, :, par], d1[:, par].unsqueeze(1)).then_inc(part1_made[par], 1)

                if ctxT is not None:
                    act.wait_ge(sem("ctx_in"), 16)
                for par in range(2):
                    copy_xnT(0, par)
                chunks(act, copy_chunk)

            @block.tensor
            def _(pe):
                pe.wait_ge(w_in, 48)
                def transpose_xn(i, par):
                    pe.wait_ge(xn_made[par], after(i))
                    pe.wait_ge(xnT_made[par], before(i))
                    for kt in range(2):
                        ins = pe.transpose(pT[par][:, kt * P:(kt + 1) * P], xn[:, par, kt, :], ident[:])
                    ins.then_inc(xT_done[par], 1)

                def project_chunk(i, more):
                    for par in range(2):
                        pe.wait_ge(xnT_made[par], after(i))
                        pe.wait_ge(r_made[par], before(i))
                        src = (xnT, kvT)
                        for s in range(2):
                            ins = pe.matmul(pA[par][:, s, :], w[:, 2 * s, :], src[s][:, par, :], start=True, stop=True)
                            if not topk:
                                ins = pe.matmul(pB[par][:, s, :], w[:, 2 * s + 1, :], src[s][:, par, :], start=True, stop=True)
                        ins.then_inc(qk_done[par], 1)
                        pe.wait_ge(v_made[par], before(i))
                        for kt in range(2):
                            ins = pe.matmul(pV[par][:, kt, :], kvT[:, par, kt * P:(kt + 1) * P], w[:, 4, :], start=True, stop=True)
                        ins.then_inc(v_done[par], 1)
                        if more:
                            transpose_xn(i + 1, par)

                for par in range(2):
                    transpose_xn(0, par)
                chunks(pe, project_chunk)

        sem.clear()


def attend_heads(nc, stage, X, consts, tensors, topk, attentions_before):
    ident, ones = consts["ident"], consts["ones"]
    qs, ks, vaug, w, bias, bo, parts = tensors
    with ExitStack() as ctx:
        def sb(name, shape, dt=F32):
            return ctx.enter_context(nc.sbuf_tensor(f"{stage}_{name}", shape, dt))

        def bank(name):
            return ctx.enter_context(nc.psum_tensor(f"{stage}_{name}", [P, 2, T], F32))

        sem = Sems(nc, ctx, stage + "a")
        m8 = sb("m8", [P, SLOTS, 2, 4, 8]) if topk else None
        nmax = sb("nmax", [P, SLOTS, 2])
        prob = sb("prob", [P, SLOTS, 2, T])
        rest = sb("rest", [P, SLOTS, 2, T]) if topk else None
        prest = sb("prest", [P, 2, 2, T]) if topk else None
        SETS = 1 if topk else 2
        probT = [sb(f"probT{c}", [P, SLOTS, 2, T]) for c in range(SETS)]
        vslot = sb("vslot", [P, 2, SLOTS, COLS])
        oT = sb("oT", [P, T])
        oall = parts[:, 0:BPAIRS // 2].rearrange("p c t s a n -> p (c t s a n)").bitcast(F32)[:, 0:UNITS * 2 * (DH + 1)]\
            .rearrange("p (u q d) -> p u q d", q=2, d=DH + 1)
        rsum = sb("rsum", [P, TAIL, 2, H])
        on = prob[:, 0:TAIL, :, 0:P].rearrange("p j q (h d) -> p j q h d", d=DH)
        onT = probT[0][:, 0:TAIL, 0, :]
        pS = [bank(f"pS{i}") for i in range(SLOTS)]
        banksPT = [bank(f"pPT{i}") for i in range(3)]
        pPT, last_use = [banksPT[i] for i in (0, 1, 2, 1)], (4, 2, 4, 2)
        bankO = bank("pO")
        pO = bankO[:, 0, :]
        pQ = bankO[:, 1, :].rearrange("p (q c) -> p q c", q=2)
        pOT = [t[:, 0, :] for t in pS]
        pY = [t[:, :, 0:P] for t in banksPT + [bankO]]

        s_done, nmax_made, exp_done, p_made, t_done, probT_made, topk_done = (
            [sem(f"{n}{j}") for j in range(SLOTS)]
            for n in ("s_done", "nmax_made", "exp_done", "p_made", "t_done", "probT_made", "topk_done"))
        v_placed, pv_done, o_lifted, o_turned, o_kept = sem("v_placed"), sem("pv_done"), sem("o_lifted"), sem("o_turned"), sem("o_kept")
        norm_done, oT_done, onT_made, y_done, x_done = (
            [sem(f"{n}{j}") for j in range(TAIL)] for n in ("norm_done", "oT_done", "onT_made", "y_done", "x_done"))
        credited = (s_done + nmax_made + exp_done + p_made + t_done + probT_made + topk_done
                    + [v_placed, pv_done, o_lifted, o_turned, o_kept] + norm_done + oT_done + onT_made + y_done + x_done)
        dve_evacuates = () if topk else (0, 2)

        def near(i, j, c):
            return i + j // SLOTS, j % SLOTS, (c + j // SLOTS) % SETS

        def set_free(i):
            return before(i) if SETS == 1 else i

        def keep(i, copy):
            copy(oall[:, ds(i * SLOTS, SLOTS), :, :].rearrange("p a q d -> p q a d"),
                 pQ.rearrange("p q (a d) -> p q a d", a=SLOTS)[:, :, :, 0:DH + 1]).then_inc(o_kept, 1)

        def rounds(eng, step, finish, pause=None):
            for j in range(SLOTS):
                step(0, j, 0, True, False)

            def middle(k):
                for c in (1, 0):
                    for j in range(SLOTS):
                        step(k * 2 + (1 if c else 2), j, c % SETS, False, False)

            if pause:
                with eng.Fori(0, ROUNDS // 4 - 1) as k:
                    middle(k)
                pause()
            with eng.Fori(ROUNDS // 4 - 1 if pause else 0, ROUNDS // 2 - 1) as k:
                middle(k)
            for j in range(SLOTS):
                step(ROUNDS - 1, j, 1 % SETS, False, True)
            finish(ROUNDS - 1, 1 % SETS)

        half = 16 * 2 * len(TERMS) * BPAIRS // 2 * (attentions_before + 1)

        with nc.Block() as block:
            @block.sync
            def _(sp):
                for i in range(BPAIRS // 2, BPAIRS):
                    for part in range(3):
                        stack_part(sp, i, part, tensors, consts["stacked"][1])
                sp.wait_ge(consts["stacked"][1], half)

            @block.gpsimd
            def _(pool):
                for s in credited:
                    pool.sem_inc(s, 1)
                pool.memset(vslot[:], 0.0).then_inc(sem("vslot_cleared"), 1)
                pool.wait_ge(sem("vslot_cleared"), 1)
                with pool.Fori(0, ROUNDS) as i:
                    for j in range(SLOTS):
                        if topk:
                            pool.wait_ge(topk_done[j], after(i))
                            pool.wait_ge(exp_done[j], before(i))
                            pool.sem_inc(sem("waited_pool"), 1)
                            pool.tensor_scalar(nmax[:, j, :], m8[:, j, :, 0, 0], -1.0, 0.0, ALU.mult, ALU.add)\
                                .then_inc(nmax_made[j], 1)
                            pool.wait_ge(exp_done[j], after(i))
                            pool.tensor_tensor(prob[:, j], prob[:, j], prest[:, j % 2], ALU.subtract).then_inc(p_made[j], 1)
                        if j == 1:
                            pool.wait_ge(pv_done, before(i))
                            ins = pool.tensor_copy(vslot[:, :, :, 0:DH + 1], vaug[:, :, ds(i * SLOTS, SLOTS), :])
                            ins.then_inc(v_placed, 1)

            @block.vector
            def _(v):
                chain = sem("topk_chain")

                def largest(i, j, c):
                    v.wait_ge(s_done[j], after(i))
                    v.wait_ge(exp_done[j], before(i))
                    v.sem_inc(sem("waited_dve"), 1)
                    n = 0
                    for rnd in range(TOPK // 8):
                        src = pS[j] if rnd == 0 else rest[:, j]
                        for qt in range(2):
                            if rnd:
                                v.wait_ge(chain, n - 1)
                            v.max(m8[:, j, qt, rnd, :], src[:, qt, :]).then_inc(chain, 1)
                            n += 1
                        for qt in range(2):
                            v.wait_ge(chain, n - 1)
                            ins = v.match_replace(rest[:, j, qt, :], m8[:, j, qt, rnd, :], src[:, qt, :], LOW)
                            if n < 4 * TOPK // 8 - 1:
                                ins.then_inc(chain, 1)
                            else:
                                ins.then_inc(topk_done[j], 1)
                            n += 1
                    v.wait_ge(chain, 4 * TOPK // 8 - 1)
                    v.sem_clear(chain)

                def maxima(i, j, c):
                    v.wait_ge(s_done[j], after(i))
                    v.wait_ge(exp_done[j], before(i))
                    v.tensor_reduce(nmax[:, j, :], pS[j][:], AX_X, ALU.max, negate=True).then_inc(nmax_made[j], 1)

                def evacuate(i, j, c):
                    if j in dve_evacuates:
                        v.wait_ge(t_done[j], after(i))
                        v.wait_ge(pv_done, set_free(i))
                        v.tensor_copy(probT[c][:, j], pPT[j][:]).then_inc(probT_made[j], 1)

                search = largest if topk else maxima

                def step(i, j, c, first, last):
                    if not last or j + 2 < SLOTS:
                        search(*near(i, j + 2, c))
                    if not first or j > 0:
                        evacuate(*near(i, j - 1, c))
                    if not first and j == 3:
                        keep_round(i - 1)

                def keep_round(i):
                    if not topk:
                        v.wait_ge(o_turned, after(i))
                        keep(i, v.tensor_copy)

                def finish(i, c):
                    evacuate(i, SLOTS - 1, c)
                    keep_round(i)

                search(0, 0, 0)
                search(0, 1, 0)
                rounds(v, step, finish)
                v.wait_ge(o_kept, after(ROUNDS - 1))
                tail = sem("tail_chain")
                with v.Fori(0, B // TAIL) as i:
                    for j in range(TAIL):
                        units = oall[:, ds(i * (TAIL * H) + j // 2 * 2 * H + j % 2, H, step=2), :, :].rearrange("p h q d -> p q h d")
                        v.wait_ge(oT_done[j], before(i))
                        v.reciprocal(rsum[:, j], units[:, :, :, DH]).then_inc(tail, 1)
                        v.wait_ge(tail, 1)
                        v.sem_clear(tail)
                        v.tensor_tensor(on[:, j], units[:, :, :, 0:DH],
                                        rsum[:, j].unsqueeze(3).broadcast_to([P, 2, H, DH]), ALU.mult).then_inc(norm_done[j], 1)
                    for j in range(TAIL):
                        tiles = X[:, ds(i * (2 * TAIL) + j * 2, 2), :]
                        v.wait_ge(y_done[j], after(i))
                        v.tensor_tensor(tiles, tiles, pY[j], ALU.add).then_inc(x_done[j], 1)

            @block.scalar
            def _(act):
                def exponentials(i, j, c):
                    act.wait_ge(nmax_made[j], after(i))
                    act.wait_ge(t_done[j], before(i))
                    if topk:
                        li, lj, _ = near(i, j - 2, c)
                        act.wait_ge(p_made[lj], after(li))
                        for qt in range(2):
                            act.activation(prest[:, j % 2, qt, :], rest[:, j, qt, :], ACT.Exp, bias=nmax[:, j, qt:qt + 1])
                    for qt in range(2):
                        ins = act.activation(prob[:, j, qt, :], pS[j][:, qt, :], ACT.Exp, bias=nmax[:, j, qt:qt + 1])
                    ins.then_inc(exp_done[j], 1)

                def evacuate(i, j, c):
                    if j not in dve_evacuates:
                        act.wait_ge(t_done[j], after(i))
                        act.wait_ge(pv_done, set_free(i))
                        act.copy(probT[c][:, j], pPT[j][:]).then_inc(probT_made[j], 1)

                def lift(i):
                    act.wait_ge(pv_done, after(i))
                    act.wait_ge(o_turned, before(i))
                    act.copy(oT[:], pO).then_inc(o_lifted, 1)

                def keep_round(i):
                    if topk:
                        act.wait_ge(o_turned, after(i))
                        keep(i, act.copy)

                def step(i, j, c, first, last):
                    if not last or j + 1 < SLOTS:
                        exponentials(*near(i, j + 1, c))
                    if not first and j == 2:
                        lift(i - 1)
                    if not first or j > 0:
                        evacuate(*near(i, j - 1, c))
                    if not first and j == 3:
                        keep_round(i - 1)

                def finish(i, c):
                    evacuate(i, SLOTS - 1, c)
                    lift(i)
                    keep_round(i)

                exponentials(0, 0, 0)
                rounds(act, step, finish)
                with act.Fori(0, B // TAIL) as i:
                    for j in range(TAIL):
                        act.wait_ge(oT_done[j], after(i))
                        act.wait_ge(y_done[j], before(i))
                        act.activation(onT[:, j], pOT[j], ACT.Identity, bias=bias[:, 4:5]).then_inc(onT_made[j], 1)

            @block.tensor
            def _(pe):
                def scores(i, j, c):
                    pe.wait_ge(exp_done[j], before(i))
                    unit = ds(i * SLOTS + j, 1)
                    for qt in range(2):
                        ins = pe.matmul(pS[j][:, qt, :], qs[0:KROWS, unit, qt * P:(qt + 1) * P],
                                        ks[0:KROWS, unit, :], start=True, stop=True)
                    ins.then_inc(s_done[j], 1)

                def transposes(i, j, c):
                    pe.wait_ge((p_made if topk else exp_done)[j], after(i))
                    li, lj, _ = near(i, j - last_use[j], c)
                    pe.wait_ge(probT_made[lj], after(li))
                    for kt in range(2):
                        for qt in range(2):
                            ins = pe.transpose(pPT[j][:, kt, qt * P:(qt + 1) * P], prob[:, j, qt, kt * P:(kt + 1) * P], ident[:])
                    ins.then_inc(t_done[j], 1)

                def products(i, c):
                    pe.wait_ge(o_kept, before(i))
                    pe.wait_ge(v_placed, after(i))
                    for j in range(SLOTS):
                        pe.wait_ge(probT_made[j], after(i))
                    for kt in range(2):
                        for j in range(SLOTS):
                            ins = pe.matmul(pO[j * COLS:(j + 1) * COLS, :], vslot[:, kt, j, :], probT[c][:, j, kt, :],
                                            start=(kt == 0), stop=(kt == 1), skip_group_check=True)
                    ins.then_inc(pv_done, 1)

                def turn(i):
                    pe.wait_ge(o_lifted, after(i))
                    for qt in range(2):
                        ins = pe.transpose(pQ[:, qt, :], oT[:, qt * P:(qt + 1) * P], ident[:])
                    ins.then_inc(o_turned, 1)

                def step(i, j, c, first, last):
                    if not last or j + 3 < SLOTS:
                        scores(*near(i, j + 3, c))
                    if not first and j == 3:
                        turn(i - 1)
                    transposes(i, j, c)
                    if not first and j == 0:
                        products(i - 1, (c + 1) % SETS)

                def finish(i, c):
                    products(i, c)
                    turn(i)

                def second_half():
                    pe.wait_ge(consts["stacked"][1], half)

                pe.wait_ge(consts["zeroed"], consts["zeroed_by"])
                pe.wait_ge(consts["stacked"][0], half)
                for j in range(3):
                    scores(0, j, 0)
                rounds(pe, step, finish, second_half)
                with pe.Fori(0, B // TAIL) as i:
                    for j in range(TAIL):
                        pe.wait_ge(norm_done[j], after(i))
                        pe.wait_ge(onT_made[j], before(i))
                        for qt in range(2):
                            ins = pe.transpose(pOT[j][:, qt * P:(qt + 1) * P],
                                               on[:, j, qt].rearrange("p h d -> p (h d)"), ident[:])
                        ins.then_inc(oT_done[j], 1)
                    for j in range(TAIL):
                        pe.wait_ge(onT_made[j], after(i))
                        pe.wait_ge(x_done[j], before(i))
                        for qt in range(2):
                            pe.matmul(pY[j][:, qt, :], onT[:, j, qt * P:(qt + 1) * P], w[:, 5, :], start=True, stop=False)
                            ins = pe.matmul(pY[j][:, qt, :], ones[0:1, :], bo[:], start=False, stop=True)
                        ins.then_inc(y_done[j], 1)

        sem.clear()


def head_attention(nc, stage, X, ctx_dram, consts, drams, topk, attentions_before):
    with ExitStack() as ctx:
        def sb(name, shape, dt=F32):
            return ctx.enter_context(nc.sbuf_tensor(f"{stage}_{name}", shape, dt))

        tensors = (
            consts["qs"],
            consts["ks"],
            sb("vaug", [P, 2, UNITS, DH + 1]),
            sb("w", [P, 6, P]),
            sb("bias", [P, 5]),
            sb("bo", [1, P]),
            sb("parts", [P, BPAIRS, 3, 2, 2, T], BF16),
        )
        prepare_heads(nc, stage, X, ctx_dram, consts, tensors, drams, topk)
        attend_heads(nc, stage, X, consts, tensors, topk, attentions_before)


DEPTH = 7
TREES = 8
NODES = 2 ** (DEPTH + 1) - 1
WIDTH = TREES * NODES
BROWS = 120


def level(d):
    return slice(TREES * (2 ** d - 1), TREES * (2 ** (d + 1) - 1))


CHUNKS = [slice(0, level(5).stop), level(6), slice(level(7).start, level(7).start + 512),
          slice(level(7).start + 512, WIDTH)]
NCHUNK = -(-WIDTH // P)


def tree_ffn(nc, stage, X, consts, drams):
    ident = consts["ident"]
    win_dram, bin_dram, wout_dram = drams
    with ExitStack() as ctx:
        def sb(name, shape, dt=F32):
            return ctx.enter_context(nc.sbuf_tensor(f"{stage}_{name}", shape, dt))

        def bank(name):
            return ctx.enter_context(nc.psum_tensor(f"{stage}_{name}", [P, 512], F32))

        sem = Sems(nc, ctx, stage)
        stats = sb("stats", [P, TILES, 6])
        mean = sb("mean", [P, TILES])
        rstd = sb("rstd", [P, TILES])
        lntmp = sb("lntmp", [P, 4, TILES])
        win = sb("win", [P, WIDTH])
        wout = sb("wout", [P, NCHUNK, P])
        b3 = consts["qs"][0:3].rearrange("p u n -> p (u n)")[:, 0:WIDTH]
        ones3 = sb("ones3", [3, P], BF16)
        xn = sb("xn", [P, 2, P])
        xnT = sb("xnT", [P, 2, P])
        acts = sb("acts", [P, 2, WIDTH])
        path = sb("path", [P, 2, WIDTH], BF16)
        actsT = sb("actsT", [P, 2, NCHUNK, P])
        bspread = sb("bspread", [BROWS, WIDTH // BROWS])
        bparts = sb("bparts", [BROWS, 3, WIDTH // BROWS], BF16)
        pL = [bank(f"pL{c}") for c in range(4)]
        pX = bank("pX")
        pT = [bank(f"pT{c}") for c in range(2)]
        pY = bank("pY")

        def pair(name):
            return [sem(f"{name}{i}") for i in range(2)]

        xn_made, xT_done, xnT_made, y_done, x_done = (pair(n) for n in ("xn_made", "xT_done", "xnT_made", "y_done", "x_done"))
        logits, silu_made, decided, masked, aT_done, aT_made = (
            [pair(f"{n}{c}_") for c in range(4)] for n in ("logits", "silu", "decided", "masked", "aT_done", "aT_made"))
        credited = xn_made + xT_done + xnT_made + y_done + x_done + sum(
            logits + silu_made + decided[:2] + masked + aT_done + aT_made, [])

        def tiles(eng, step, finish):
            step(0, 0, None, 1)
            step(0, 1, 0, 0)
            with eng.Fori(1, TILES // 2) as i:
                step(i, 0, i - 1, 1)
                step(i, 1, i, 0)
            finish(TILES // 2 - 1, 1)

        def chunk_groups(g):
            return range(4 * g, 4 * g + 4)

        def rows(k):
            return min(P, WIDTH - k * P)

        with nc.Block() as block:
            @block.sync
            def _(sp):
                sp.dma_start(win[:], win_dram).then_inc(sem("w_in"), 16)
                sp.dma_start(bspread[:], bin_dram.rearrange("a (p n) -> (a p) n", p=BROWS)).then_inc(sem("b_in"), 16)
                full = (NCHUNK - 1) * P
                sp.dma_start(wout[:, 0:NCHUNK - 1, :], wout_dram[0:full, :].rearrange("(k p) n -> p k n", p=P)).then_inc(sem("w_in"), 16)
                sp.dma_start(wout[0:WIDTH - full, NCHUNK - 1, :], wout_dram[full:WIDTH, :]).then_inc(sem("w_in"), 16)
                sp.wait_ge(sem("b_split"), 4)
                for i in range(3):
                    sp.dma_start(b3[i:i + 1, :].rearrange("a (p n) -> a p n", p=BROWS), bparts[:, i, :]).then_inc(sem("b3_in"), 16)
                sp.wait_ge(sem("b3_in"), 48)

            @block.gpsimd
            def _(pool):
                for s in credited:
                    pool.sem_inc(s, 1)
                pool.memset(ones3[:], 1.0).then_inc(sem("ones3_made"), 1)
                pool.memset(path[:, :, level(0)], 1.0).then_inc(sem("root_made"), 1)
                split = sem("b_split")
                pool.wait_ge(sem("b_in"), 16)
                pool.tensor_copy(bparts[:, 0, :], bspread[:]).then_inc(split, 1)
                pool.wait_ge(split, 1)
                pool.tensor_tensor(bspread[:], bspread[:], bparts[:, 0, :], ALU.subtract).then_inc(split, 1)
                pool.wait_ge(split, 2)
                pool.tensor_copy(bparts[:, 1, :], bspread[:]).then_inc(split, 1)
                pool.wait_ge(split, 3)
                pool.tensor_tensor(bparts[:, 2, :], bspread[:], bparts[:, 1, :], ALU.subtract).then_inc(split, 1)

            @block.vector
            def _(v):
                layernorm_stats(v, sem, X, stats, mean, rstd, lntmp)
                chain = sem("path_chain")

                def start(i, par):
                    v.wait_ge(xT_done[par], before(i))
                    v.tensor_scalar(xn[:, par], X[:, ds(i * 2 + par, 1), :], mean[:, ds(i * 2 + par, 1)],
                                    rstd[:, ds(i * 2 + par, 1)], ALU.subtract, ALU.mult).then_inc(xn_made[par], 1)

                def end(i, par):
                    n = 0
                    for d in range(DEPTH):
                        lv, up = level(d), level(d + 1)
                        mid = up.start + TREES * 2 ** d
                        c = 0 if d < DEPTH - 1 else 1
                        if d in (0, DEPTH - 1):
                            v.wait_ge(silu_made[c][par], after(i))
                        if n:
                            v.wait_ge(chain, n)
                        off = CHUNKS[c].start
                        ins = v.scalar_tensor_tensor(path[:, par, mid:up.stop], pL[c][:, lv.start - off:lv.stop - off], 0.0,
                                                     path[:, par, lv], ALU.is_gt, ALU.mult).then_inc(chain, 1)
                        n += 1
                        v.wait_ge(chain, n)
                        v.tensor_tensor(path[:, par, up.start:mid], path[:, par, lv], path[:, par, mid:up.stop],
                                        ALU.subtract).then_inc(chain, 1)
                        n += 1
                        if d >= DEPTH - 2:
                            v.wait_ge(chain, n)
                            v.sem_inc(decided[c][par], 1)
                    v.sem_clear(chain)
                    for c in range(4):
                        v.wait_ge(silu_made[c][par], after(i))
                        v.tensor_tensor(acts[:, par, CHUNKS[c]], acts[:, par, CHUNKS[c]], path[:, par, CHUNKS[c]],
                                        ALU.mult).then_inc(masked[c][par], 1)

                def add(i, par):
                    v.wait_ge(y_done[par], after(i))
                    v.tensor_tensor(X[:, ds(i * 2 + par, 1), :], X[:, ds(i * 2 + par, 1), :], pY[:, 0:P].unsqueeze(1),
                                    ALU.add).then_inc(x_done[par], 1)

                def step(i, par, before_i, before_par):
                    start(i, par)
                    if before_i is not None:
                        end(before_i, before_par)
                    if not (isinstance(i, int) and i == 0):
                        add(i - 1, par)

                def finish(i, par):
                    end(i, par)
                    add(i, 0)
                    add(i, 1)

                v.wait_ge(sem("root_made"), 1)
                tiles(v, step, finish)

            @block.scalar
            def _(act):
                def start(i, par):
                    act.wait_ge(xT_done[par], after(i))
                    act.wait_ge(logits[3][par], before(i))
                    act.copy(xnT[:, par], pX[:, 0:P]).then_inc(xnT_made[par], 1)
                    for c in range(4):
                        act.wait_ge(logits[c][par], after(i))
                        if c == 0:
                            act.wait_ge(aT_done[3][par], before(i))
                        size = CHUNKS[c].stop - CHUNKS[c].start
                        act.activation(acts[:, par, CHUNKS[c]], pL[c][:, 0:size], ACT.Silu).then_inc(silu_made[c][par], 1)

                def end(i, par):
                    for g in range(4):
                        act.wait_ge(aT_done[g][par], after(i))
                        if g == 0:
                            act.wait_ge(y_done[par], before(i))
                        for k in chunk_groups(g)[-1:]:
                            n = rows(k)
                        if n == P:
                            ins = act.copy(actsT[:, par, 4 * g:4 * g + 4, :].rearrange("p k n -> p (k n)"), pT[g % 2][:])
                        else:
                            act.copy(actsT[:, par, 4 * g:4 * g + 3, :].rearrange("p k n -> p (k n)"), pT[g % 2][:, 0:3 * P])
                            ins = act.copy(actsT[0:n, par, 4 * g + 3, :], pT[g % 2][0:n, 3 * P:4 * P])
                        ins.then_inc(aT_made[g][par], 1)

                def step(i, par, before_i, before_par):
                    start(i, par)
                    if before_i is not None:
                        end(before_i, before_par)

                tiles(act, step, end)

            @block.tensor
            def _(pe):
                pe.wait_ge(sem("w_in"), 48)
                pe.wait_ge(sem("b3_in"), 48)
                pe.wait_ge(sem("ones3_made"), 1)

                def start(i, par, before_i, before_par):
                    pe.wait_ge(xn_made[par], after(i))
                    if before_i is not None:
                        pe.wait_ge(xnT_made[before_par], after(before_i))
                    pe.transpose(pX[:, 0:P], xn[:, par], ident[:]).then_inc(xT_done[par], 1)
                    pe.wait_ge(xnT_made[par], after(i))
                    for c in range(4):
                        size = CHUNKS[c].stop - CHUNKS[c].start
                        if before_i is not None:
                            pe.wait_ge((decided[c] if c < 2 else silu_made[c])[before_par], after(before_i))
                        pe.matmul(pL[c][:, 0:size], xnT[:, par], win[:, CHUNKS[c]], start=True, stop=False)
                        pe.matmul(pL[c][:, 0:size], ones3[:], b3[:, CHUNKS[c]], start=False, stop=True).then_inc(logits[c][par], 1)

                def end(i, par):
                    for g in range(4):
                        for c in range(4):
                            if CHUNKS[c].start < 512 * (g + 1) and CHUNKS[c].stop > 512 * g:
                                pe.wait_ge(masked[c][par], after(i))
                        if g >= 2:
                            pe.wait_ge(aT_made[g - 2][par], after(i))
                        for k in chunk_groups(g):
                            n = rows(k)
                            ins = pe.transpose(pT[g % 2][0:n, (k % 4) * P:(k % 4 + 1) * P], acts[:, par, k * P:k * P + n], ident[:])
                        ins.then_inc(aT_done[g][par], 1)
                    pe.wait_ge(x_done[1 - par], after(i - 1) if par == 0 else after(i))
                    for g in range(4):
                        pe.wait_ge(aT_made[g][par], after(i))
                        for k in chunk_groups(g):
                            n = rows(k)
                            ins = pe.matmul(pY[:, 0:P], actsT[0:n, par, k, :], wout[0:n, k, :], start=(k == 0), stop=(k == NCHUNK - 1))
                    ins.then_inc(y_done[par], 1)

                def step(i, par, before_i, before_par):
                    start(i, par, before_i, before_par)
                    if before_i is not None:
                        end(before_i, before_par)

                tiles(pe, step, end)

        sem.clear()


def entangled_attention(nc, stage, X, ctx_dram, consts, drams):
    ident, ones = consts["ident"], consts["ones"]
    w_dram, b_dram, bvrow_dram = drams
    with ExitStack() as ctx:
        def sb(name, shape, dt=F32):
            return ctx.enter_context(nc.sbuf_tensor(f"{stage}_{name}", shape, dt))

        def bank(name):
            return ctx.enter_context(nc.psum_tensor(f"{stage}_{name}", [P, 2, T], F32))

        sem = Sems(nc, ctx, stage)
        stats = sb("stats", [P, TILES, 6])
        mean = sb("mean", [P, TILES])
        rstd = sb("rstd", [P, TILES])
        lntmp = sb("lntmp", [P, 4, TILES])
        w = sb("w", [P, 5, P])
        bias = sb("bias", [P, 4])
        bvrow = sb("bvrow", [1, P])
        xn = sb("xn", [P, 2, 2, P])
        xnT = sb("xnT", [P, 2, T])
        kvT = sb("kvT", [P, 2, T])
        ctxT = sb("ctxT", [P, B * T])
        qkT = sb("qkT", [P, 2, 2, T])
        vT = sb("vT", [P, 2, T])
        vaug = sb("vaug", [P, 2, 2, P + 1])
        entT = sb("entT", [P, 2, T])
        nmax = sb("nmax", [P, 2, 2])
        prob = sb("prob", [P, 2, 2, T])
        probT = sb("probT", [P, 2, 2, T])
        rsum = sb("rsum", [P, 2, 2])
        pX, pQK, pVT, pV, pE, pS, pPT, pO = (bank(n) for n in ("pX", "pQK", "pVT", "pV", "pE", "pS", "pPT", "pO"))

        def pair(name):
            return [sem(f"{name}{i}") for i in range(2)]

        names = ("xn_made", "xT_done", "xnT_made", "qk_done", "qk_made", "vT_done", "vT_made", "v_done", "v_made",
                 "e_done", "e_made", "s_done", "nmax_made", "exp_done", "t_done", "probT_made", "o_done", "x_done")
        made = {n: pair(n) for n in names}
        (xn_made, xT_done, xnT_made, qk_done, qk_made, vT_done, vT_made, v_done, v_made, e_done, e_made, s_done,
         nmax_made, exp_done, t_done, probT_made, o_done, x_done) = (made[n] for n in names)

        def batches(eng, parts):
            def step(i, par):
                for part, shift in parts:
                    at = i + (par + shift) // 2
                    if not isinstance(at, int) or 0 <= at < B // 2:
                        part(at, (par + shift) % 2)

            for n in range(-2, 2):
                step(n // 2, n % 2)
            with eng.Fori(1, B // 2 - 1) as i:
                step(i, 0)
                step(i, 1)
            for n in range(B - 2, B + 2):
                step(n // 2, n % 2)

        with nc.Block() as block:
            @block.sync
            def _(sp):
                sp.dma_start(w[:], w_dram).then_inc(sem("w_in"), 16)
                sp.dma_start(bias[:], b_dram).then_inc(sem("w_in"), 16)
                sp.dma_start(bvrow[:], bvrow_dram).then_inc(sem("w_in"), 16)
                sp.dma_start(ctxT[:], ctx_dram).then_inc(sem("ctx_in"), 16)

            @block.gpsimd
            def _(pool):
                for s in sum(made.values(), []):
                    pool.sem_inc(s, 1)
                pool.memset(vaug[:, :, :, P:P + 1], 1.0).then_inc(sem("ones_made"), 1)

            @block.vector
            def _(v):
                layernorm_stats(v, sem, X, stats, mean, rstd, lntmp)
                v.wait_ge(sem("w_in"), 48)

                chain = sem("out_chain")

                def normalise(i, par):
                    v.wait_ge(xT_done[par], before(i))
                    for kt in range(2):
                        tile = i * 4 + par * 2 + kt
                        ins = v.tensor_scalar(xn[:, par, kt, :], X[:, ds(tile, 1), :], mean[:, ds(tile, 1)],
                                              rstd[:, ds(tile, 1)], ALU.subtract, ALU.mult)
                    ins.then_inc(xn_made[par], 1)

                def add_bias(i, par):
                    v.wait_ge(qk_done[par], after(i))
                    v.wait_ge(e_done[par], before(i))
                    v.tensor_scalar(qkT[:, par, 0, :], pQK[:, 0, :], bias[:, 0:1], None, ALU.add)
                    v.tensor_scalar(qkT[:, par, 1, :], pQK[:, 1, :], bias[:, 1:2], None, ALU.add).then_inc(qk_made[par], 1)
                    v.wait_ge(vT_done[par], after(i))
                    v.wait_ge(s_done[par], before(i))
                    v.tensor_scalar(vT[:, par, :], pVT[:, 0, :], bias[:, 2:3], float(P) ** -0.5, ALU.add, ALU.mult)\
                        .then_inc(vT_made[par], 1)

                def maxima(i, par):
                    v.wait_ge(s_done[par], after(i))
                    v.wait_ge(exp_done[par], before(i))
                    v.tensor_reduce(nmax[:, par, :], pS[:], AX_X, ALU.max, negate=True).then_inc(nmax_made[par], 1)

                def evacuate(i, par):
                    v.wait_ge(t_done[par], after(i))
                    v.wait_ge(o_done[par], before(i))
                    v.tensor_copy(probT[:, par], pPT[:]).then_inc(probT_made[par], 1)

                def add(i, par):
                    v.wait_ge(o_done[par], after(i))
                    v.reciprocal(rsum[:, par, :], pO[:, :, P]).then_inc(chain, 1)
                    v.wait_ge(chain, 1)
                    v.sem_clear(chain)
                    for qt in range(2):
                        tile = X[:, ds(i * 4 + par * 2 + qt, 1), :]
                        ins = v.scalar_tensor_tensor(tile, pO[:, qt, 0:P].unsqueeze(1), rsum[:, par, qt:qt + 1], tile, ALU.mult, ALU.add)
                    ins.then_inc(x_done[par], 1)

                batches(v, ((add_bias, 0), (add, -2), (maxima, -1), (normalise, 2), (evacuate, -1)))

            @block.scalar
            def _(act):
                def lift_xn(i, par):
                    act.wait_ge(xT_done[par], after(i))
                    act.wait_ge(v_done[par], before(i))
                    act.copy(xnT[:, par, :], pX[:, 0, :])
                    act.copy(kvT[:, par, :], ctxT[:, ds((i * 2 + par) * T, T)]).then_inc(xnT_made[par], 1)

                def place_v(i, par):
                    act.wait_ge(v_done[par], after(i))
                    act.wait_ge(o_done[par], before(i))
                    act.copy(vaug[:, par, :, 0:P], pV[:, :, 0:P]).then_inc(v_made[par], 1)

                def entangle(i, par):
                    act.wait_ge(e_done[par], after(i))
                    act.wait_ge(s_done[par], before(i))
                    act.activation(entT[:, par, :], pE[:, 0, :], ACT.Tanh, bias=bias[:, 3:4]).then_inc(e_made[par], 1)

                def exponentials(i, par):
                    act.wait_ge(nmax_made[par], after(i))
                    act.wait_ge(t_done[par], before(i))
                    for qt in range(2):
                        ins = act.activation(prob[:, par, qt, :], pS[:, qt, :], ACT.Exp, bias=nmax[:, par, qt:qt + 1])
                    ins.then_inc(exp_done[par], 1)

                act.wait_ge(sem("w_in"), 48)
                act.wait_ge(sem("ctx_in"), 16)
                batches(act, ((place_v, 0), (exponentials, -1), (lift_xn, 1), (entangle, 0)))

            @block.tensor
            def _(pe):
                pe.wait_ge(sem("w_in"), 48)
                pe.wait_ge(sem("ones_made"), 1)

                def one_before(i, par):
                    return i + (par - 1) // 2, 1 - par

                def transpose_xn(i, par):
                    li, lp = one_before(i, par)
                    pe.wait_ge(xn_made[par], after(i))
                    pe.wait_ge(xnT_made[lp], after(li))
                    for kt in range(2):
                        ins = pe.transpose(pX[:, 0, kt * P:(kt + 1) * P], xn[:, par, kt, :], ident[:])
                    ins.then_inc(xT_done[par], 1)

                def project(i, par):
                    li, lp = one_before(i, par)
                    pe.wait_ge(xnT_made[par], after(i))
                    pe.wait_ge(qk_made[lp], after(li))
                    pe.wait_ge(vT_made[lp], after(li))
                    pe.wait_ge(v_made[lp], after(li))
                    pe.matmul(pQK[:, 0, :], w[:, 0, :], xnT[:, par, :], start=True, stop=True)
                    pe.matmul(pQK[:, 1, :], w[:, 1, :], kvT[:, par, :], start=True, stop=True).then_inc(qk_done[par], 1)
                    pe.matmul(pVT[:, 0, :], w[:, 2, :], kvT[:, par, :], start=True, stop=True).then_inc(vT_done[par], 1)
                    for kt in range(2):
                        pe.matmul(pV[:, kt, 0:P], kvT[:, par, kt * P:(kt + 1) * P], w[:, 2, :], start=True, stop=False)
                        ins = pe.matmul(pV[:, kt, 0:P], ones[0:1, :], bvrow[:], start=False, stop=True)
                    ins.then_inc(v_done[par], 1)

                def entangle(i, par):
                    li, lp = one_before(i, par)
                    pe.wait_ge(qk_made[par], after(i))
                    pe.wait_ge(e_made[lp], after(li))
                    pe.matmul(pE[:, 0, :], w[:, 3, :], qkT[:, par, 0, :], start=True, stop=False)
                    pe.matmul(pE[:, 0, :], w[:, 4, :], qkT[:, par, 1, :], start=False, stop=True).then_inc(e_done[par], 1)

                def scores(i, par):
                    li, lp = one_before(i, par)
                    pe.wait_ge(e_made[par], after(i))
                    pe.wait_ge(vT_made[par], after(i))
                    pe.wait_ge(exp_done[lp], after(li))
                    for qt in range(2):
                        ins = pe.matmul(pS[:, qt, :], entT[:, par, qt * P:(qt + 1) * P], vT[:, par, :], start=True, stop=True)
                    ins.then_inc(s_done[par], 1)

                def transposes(i, par):
                    li, lp = one_before(i, par)
                    pe.wait_ge(exp_done[par], after(i))
                    pe.wait_ge(probT_made[lp], after(li))
                    for kt in range(2):
                        for qt in range(2):
                            ins = pe.transpose(pPT[:, kt, qt * P:(qt + 1) * P], prob[:, par, qt, kt * P:(kt + 1) * P], ident[:])
                    ins.then_inc(t_done[par], 1)

                def products(i, par):
                    li, lp = one_before(i, par)
                    pe.wait_ge(probT_made[par], after(i))
                    pe.wait_ge(v_made[par], after(i))
                    pe.wait_ge(x_done[lp], after(li))
                    for qt in range(2):
                        for kt in range(2):
                            ins = pe.matmul(pO[:, qt, 0:P + 1], probT[:, par, kt, qt * P:(qt + 1) * P], vaug[:, par, kt, :],
                                            start=(kt == 0), stop=(kt == 1))
                    ins.then_inc(o_done[par], 1)

                batches(pe, ((project, 0), (products, -2), (scores, -1), (transpose_xn, 1), (entangle, 0), (transposes, -1)))

        sem.clear()


NH = 8
HW = 64
K = T // 8
MASKED = -1e30


def route_tokens(nc, stage, X, consts, shared, drams, loads, loaded):
    ident = consts["ident"]
    xn_all, xnT_all, slots = shared
    with ExitStack() as ctx:
        def sb(name, shape, dt=F32):
            return ctx.enter_context(nc.sbuf_tensor(f"{stage}r_{name}", shape, dt))

        def bank(name):
            return ctx.enter_context(nc.psum_tensor(f"{stage}r_{name}", [P, 2, T], F32))

        sem = Sems(nc, ctx, stage + "r")
        ROWS = NH * B
        stats = sb("stats", [P, TILES, 6])
        mean = sb("mean", [P, TILES])
        rstd = sb("rstd", [P, TILES])
        lntmp = sb("lntmp", [P, 4, TILES])
        router = sb("router", [P, NH])
        xn = sb("xn", [P, 2, 2, P])
        scores8 = sb("scores8", [NH, B, T])
        scores = sb("scores", [ROWS, T])
        rest = sb("rest", [ROWS, T])
        taken = sb("taken", [ROWS, T])
        onesr = sb("onesr", [ROWS, T])
        slotgate = sb("slotgate", [ROWS, 2, T])
        m8 = sb("m8", [ROWS, 4, 8])
        pX = [bank(f"pX{i}") for i in range(2)]
        pR = [bank(f"pR{i}") for i in range(2)]
        pT = bank("pT")

        def pair(name):
            return [sem(f"{name}{i}") for i in range(2)]

        xn_made, xT_done, xnT_made, r_done, r_made = (pair(n) for n in ("xn_made", "xT_done", "xnT_made", "r_done", "r_made"))

        with nc.Block() as block:
            @block.sync
            def _(sp):
                sp.dma_start(router[:], drams["router"]).then_inc(sem("w_in"), 16)
                for name, (tensor, dram) in loads.items():
                    sp.dma_start(tensor[:], dram).then_inc(loaded[name.split("_")[0]], 16)
                for par in range(2):
                    sp.wait_ge(r_made[par], after(B // 2 - 1))
                sp.dma_start(scores[:], scores8[:].rearrange("n b t -> n (b t)")).then_inc(sem("scores_in"), 16)
                sp.wait_ge(sem("scores_in"), 16)

            @block.gpsimd
            def _(pool):
                for s in xn_made + xT_done + xnT_made + r_done + r_made + [sem("kept0"), sem("kept1")]:
                    pool.sem_inc(s, 1)
                pool.memset(onesr[:], 1.0).then_inc(sem("ones_made"), 1)
                with pool.Fori(0, B // 2) as i:
                    for par in range(2):
                        pool.wait_ge(xn_made[par], after(i))
                        pool.tensor_copy(xn_all[:, ds(i * 4 + par * 2, 2), :], xn[:, par]).then_inc(sem(f"kept{par}"), 1)

            @block.vector
            def _(v):
                layernorm_stats(v, sem, X, stats, mean, rstd, lntmp)
                with v.Fori(0, B // 2) as i:
                    for par in range(2):
                        v.wait_ge(xT_done[par], before(i))
                        v.wait_ge(sem(f"kept{par}"), before(i))
                        for kt in range(2):
                            tile = i * 4 + par * 2 + kt
                            ins = v.tensor_scalar(xn[:, par, kt, :], X[:, ds(tile, 1), :], mean[:, ds(tile, 1)],
                                                  rstd[:, ds(tile, 1)], ALU.subtract, ALU.mult)
                        ins.then_inc(xn_made[par], 1)
                chain = sem("topk_chain")
                n = [0]

                def step(ins):
                    n[0] += 1
                    ins.then_inc(chain, 1)
                    v.wait_ge(chain, n[0])

                v.wait_ge(sem("scores_in"), 16)
                src = scores
                for rnd in range(K // 8):
                    step(v.max(m8[:, rnd, :], src[:]))
                    step(v.match_replace(rest[:], m8[:, rnd, :], src[:], LOW))
                    src = rest
                step(v.tensor_scalar(taken[:], rest[:], LOW, None, ALU.is_equal))
                v.wait_ge(sem("ones_made"), 1)
                step(v.tensor_tensor_scan(slotgate[:, 0, :], onesr[:], taken[:], 0.0, ALU.mult, ALU.add))
                v.tensor_tensor(slotgate[:, 0, :], slotgate[:, 0, :], taken[:], ALU.mult).then_inc(sem("slots_made"), 1)
                v.wait_ge(sem("tanh_made"), 1)
                v.tensor_scalar(slotgate[:, 1, :], scores[:], 0.5, 0.5, ALU.mult, ALU.add).then_inc(sem("slots_made"), 1)
                v.wait_ge(sem("slots_transposed"), 1)
                v.tensor_copy(slots[:], pT[:].rearrange("p a (k r) -> p (a k r)", k=4)[:, 0:4 * ROWS].rearrange("p (k r) -> p k r", r=ROWS))

            @block.scalar
            def _(act):
                with act.Fori(0, B // 2) as i:
                    for par in range(2):
                        act.wait_ge(xT_done[par], after(i))
                        act.copy(xnT_all[:, ds((i * 2 + par) * T, T)], pX[par][:, 0, :]).then_inc(xnT_made[par], 1)
                    for par in range(2):
                        act.wait_ge(r_done[par], after(i))
                        act.copy(scores8[:, ds(i * 2 + par, 1), :], pR[par][0:NH, 0, :].unsqueeze(1)).then_inc(r_made[par], 1)
                act.wait_ge(sem("slots_made"), 1)
                act.activation(scores[:], scores[:], ACT.Tanh, scale=0.5).then_inc(sem("tanh_made"), 1)

            @block.tensor
            def _(pe):
                pe.wait_ge(sem("w_in"), 16)
                with pe.Fori(0, B // 2) as i:
                    for par in range(2):
                        pe.wait_ge(xn_made[par], after(i))
                        pe.wait_ge(xnT_made[par], before(i))
                        for kt in range(2):
                            ins = pe.transpose(pX[par][:, 0, kt * P:(kt + 1) * P], xn[:, par, kt, :], ident[:])
                        ins.then_inc(xT_done[par], 1)
                    for par in range(2):
                        pe.wait_ge(xnT_made[par], after(i))
                        pe.wait_ge(r_made[par], before(i))
                        pe.matmul(pR[par][0:NH, 0, :], router[:], xnT_all[:, ds((i * 2 + par) * T, T)], start=True, stop=True)\
                            .then_inc(r_done[par], 1)
                pe.wait_ge(sem("slots_made"), 2)
                flat = pT[:].rearrange("p a t -> p (a t)")
                for a in range(2):
                    for kt in range(2):
                        at = (a * 2 + kt) * ROWS
                        ins = pe.transpose(flat[:, at:at + ROWS], slotgate[:, a, kt * P:(kt + 1) * P], ident[0:ROWS, 0:ROWS])
                ins.then_inc(sem("slots_transposed"), 1)

        sem.clear()


def dense_heads(nc, stage, X, consts, shared, loads, loaded):
    ident = consts["ident"]
    _, xnT_all, _ = shared
    HP = NH // 2
    with ExitStack() as ctx:
        def sb(name, shape, dt=F32):
            return ctx.enter_context(nc.sbuf_tensor(f"{stage}d_{name}", shape, dt))

        def bank(name, shape=(P, 2, T)):
            return ctx.enter_context(nc.psum_tensor(f"{stage}d_{name}", list(shape), F32))

        sem = Sems(nc, ctx, stage + "d")
        w, wo, rope = (loads[f"dense_{n}"][0] for n in ("w", "wo", "rope"))
        identb = sb("identb", [P, P], BF16)
        causal = sb("causal", [P, P], BF16)
        xb = sb("xb", [P, T])
        r = sb("r", [P, 2, 2, T])
        r2 = sb("r2", [P, 2, 2, T])
        vv = sb("vv", [P, 2, 2, P])
        nmax = sb("nmax", [P, 2, 2, 2])
        prob = sb("prob", [P, 2, 2, 2, T])
        probT = sb("probT", [P, 2, 3, P])
        sums = sb("sums", [P, 2, 2, 2])
        rsum = sb("rsum", [P, 2, 2, 2])
        oT = sb("oT", [P, 2, HP, P])
        pA, pC, bankV, pPT0, pPT1, pO = (bank(n) for n in ("pA", "pC", "pV", "pPT0", "pPT1", "pO"))
        pV, pY = bankV[:, :, 0:P], bankV[:, :, P:2 * P]
        pS = bank("pS", (P, 2, 2, T))

        def pair(name):
            return [sem(f"{name}{i}") for i in range(2)]

        names = ("qk_done", "r2_made", "r_made", "v_done", "v_made", "s_done", "nmax_made", "exp_done", "rsum_made",
                 "p_made", "t0_done", "t1_done", "probT0_made", "probT1_made", "o_done", "oT_made")
        made = {n: pair(n) for n in names}
        (qk_done, r2_made, r_made, v_done, v_made, s_done, nmax_made, exp_done, rsum_made, p_made, t0_done, t1_done,
         probT0_made, probT1_made, o_done, oT_made) = (made[n] for n in names)
        t_done, probT_made = (t0_done, t1_done), (probT0_made, probT1_made)
        batch_names = ("xb_made", "y_done", "x_done")
        bmade = {n: sem(n) for n in batch_names}
        xb_made, y_done, x_done = (bmade[n] for n in batch_names)
        BLOCKS = ((0, 0), (0, 1), (1, 1))

        def near(b, hp):
            b, hp = b + hp // HP, hp % HP
            return b, hp, b * 2 + hp // 2, hp % 2

        def two_ahead(b, hp):
            return not isinstance(b, int) or b * HP + hp + 2 < B * HP

        def units(eng, step, finish):
            for hp in range(HP):
                step(0, hp, hp == 0, False)
            with eng.Fori(1, B - 1) as b:
                for hp in range(HP):
                    step(b, hp, False, False)
            for hp in range(HP):
                step(B - 1, hp, False, hp == HP - 1)
            finish(B)

        def follows(b):
            return not (isinstance(b, int) and b == 0)

        pPT = [t[:].rearrange("p a t -> p (a t)")[:, 0:3 * P].rearrange("p (k q) -> p k q", k=3) for t in (pPT0, pPT1)]

        with nc.Block() as block:
            @block.gpsimd
            def _(pool):
                for s in sum(made.values(), []) + list(bmade.values()):
                    pool.sem_inc(s, 1)
                c = sem("mask_made")
                pool.memset(causal[:], 0.0).then_inc(c, 1)
                pool.tensor_copy(identb[:], ident[:]).then_inc(c, 1)
                pool.wait_ge(c, 2)
                pool.affine_select(out=causal[:], in_=causal[:], compare_op=ALU.is_ge, fill=MASKED, base=0,
                                   pattern=[[-1, P]], channel_multiplier=1).then_inc(c, 1)

                def place_xb(b):
                    pool.wait_ge(v_done[1], b * 2 + 1)
                    pool.tensor_copy(xb[:], xnT_all[:, ds(b * T, T)]).then_inc(xb_made, 1)

                def scale(b, hp, i, par):
                    pool.wait_ge(rsum_made[par], after(i))
                    for qt in range(2):
                        n = (qt + 1) * P
                        ins = pool.tensor_tensor(prob[:, par, :, qt, 0:n], prob[:, par, :, qt, 0:n],
                                                 rsum[:, par, :, qt].unsqueeze(2).broadcast_to([P, 2, n]), ALU.mult)
                    ins.then_inc(p_made[par], 1)

                def batch(b, more):
                    for hp in range(HP):
                        if more and hp == HP - 1:
                            place_xb(b + 1)
                        scale(*near(b, hp))

                place_xb(0)
                with pool.Fori(0, B - 1) as b:
                    batch(b, True)
                batch(B - 1, False)

            @block.vector
            def _(v):
                v.wait_ge(loaded, 48)
                chain = sem("rope_chain")

                def tables(b, hp, i, par):
                    v.wait_ge(qk_done[par], after(i))
                    v.wait_ge(s_done[par], before(i))
                    v.tensor_tensor(r[:, par], pA[:], rope[:, 0:2, :], ALU.mult).then_inc(chain, 1)
                    v.tensor_tensor(r2[:, par], pC[:], rope[:, 2:4, :], ALU.mult).then_inc(r2_made[par], 1)
                    v.wait_ge(chain, 1)
                    v.sem_clear(chain)
                    v.wait_ge(r2_made[par], after(i))
                    v.tensor_tensor(r[:, par], r[:, par], r2[:, par], ALU.add).then_inc(r_made[par], 1)

                def maxima(b, hp, i, par):
                    v.wait_ge(s_done[par], after(i))
                    v.wait_ge(exp_done[par], before(i))
                    v.tensor_reduce(nmax[:, par, 0, :], pS[:, :, 0, 0:P], AX_X, ALU.max, negate=True)
                    v.tensor_reduce(nmax[:, par, 1, :], pS[:, :, 1, :], AX_X, ALU.max, negate=True).then_inc(nmax_made[par], 1)

                def evacuate(b, hp, i, par):
                    _, _, li, lp = near(b, hp - 1)
                    v.wait_ge(t_done[1][par], after(i))
                    v.wait_ge(o_done[lp], after(li))
                    v.tensor_copy(probT[:, 1], pPT[1]).then_inc(probT_made[1][par], 1)

                def invert(b, hp, i, par):
                    v.wait_ge(exp_done[par], after(i))
                    v.wait_ge(p_made[par], before(i))
                    v.reciprocal(rsum[:, par], sums[:, par]).then_inc(rsum_made[par], 1)

                def add(b):
                    v.wait_ge(y_done, after(b))
                    v.tensor_tensor(X[:, ds(b * 2, 2), :], X[:, ds(b * 2, 2), :], pY, ALU.add).then_inc(x_done, 1)

                def step(b, hp, first, last):
                    if follows(b) and hp == 2:
                        add(b - 1)
                    maxima(*near(b, hp))
                    if not first:
                        evacuate(*near(b, hp - 1))
                    invert(*near(b, hp))
                    if two_ahead(b, hp):
                        tables(*near(b, hp + 2))

                def finish(b):
                    evacuate(*near(b, -1))
                    add(b - 1)

                tables(*near(0, 0))
                tables(*near(0, 1))
                units(v, step, finish)

            @block.scalar
            def _(act):
                def place_v(b, hp, i, par):
                    act.wait_ge(v_done[par], after(i))
                    act.wait_ge(o_done[par], before(i))
                    act.copy(vv[:, par], pV).then_inc(v_made[par], 1)

                def exponentials(b, hp, i, par):
                    act.wait_ge(nmax_made[par], after(i))
                    act.wait_ge(t_done[1][par], before(i))
                    act.wait_ge(rsum_made[par], before(i))
                    for x in range(2):
                        for qt in range(2):
                            n = (qt + 1) * P
                            ins = act.activation(prob[:, par, x, qt, 0:n], pS[:, x, qt, 0:n], ACT.Exp,
                                                 bias=nmax[:, par, qt, x:x + 1], accum_out=sums[:, par, x, qt:qt + 1])
                    ins.then_inc(exp_done[par], 1)

                def evacuate(b, hp, i, par):
                    _, _, li, lp = near(b, hp - 1)
                    act.wait_ge(t_done[0][par], after(i))
                    act.wait_ge(o_done[lp], after(li))
                    act.copy(probT[:, 0], pPT[0]).then_inc(probT_made[0][par], 1)

                def place_o(b, hp, i, par):
                    act.wait_ge(o_done[par], after(i))
                    act.wait_ge(y_done, b + 1)
                    act.copy(oT[:, :, hp, :], pO[:, 0, :].rearrange("p (a q) -> p a q", a=2)).then_inc(oT_made[par], 1)

                def step(b, hp, first, last):
                    if not first:
                        evacuate(*near(b, hp - 1))
                    exponentials(*near(b, hp))
                    if not last:
                        place_v(*near(b, hp + 1))
                    if not first:
                        place_o(*near(b, hp - 1))

                def finish(b):
                    evacuate(*near(b, -1))
                    place_o(*near(b, -1))

                place_v(*near(0, 0))
                units(act, step, finish)

            @block.tensor
            def _(pe):
                pe.wait_ge(loaded, 48)
                pe.wait_ge(sem("mask_made"), 3)

                def project_qk(b, hp, i, par):
                    _, _, li, lp = near(b, hp - 1)
                    pe.wait_ge(r2_made[lp], after(li))
                    for s in range(2):
                        pe.matmul(pA[:, s, :], w[:, 2 * s, hp, :], xnT_all[:, ds(b * T, T)], start=True, stop=True)
                        ins = pe.matmul(pC[:, s, :], w[:, 2 * s + 1, hp, :], xnT_all[:, ds(b * T, T)], start=True, stop=True)
                    ins.then_inc(qk_done[par], 1)

                def project_v(b, hp, i, par):
                    _, _, li, lp = near(b, hp - 1)
                    if hp == 0:
                        pe.wait_ge(xb_made, after(b))
                    pe.wait_ge(v_made[lp], after(li))
                    if hp == 3:
                        pe.wait_ge(x_done, b + 1)
                    for kt in range(2):
                        ins = pe.matmul(pV[:, kt, :], xb[:, kt * P:(kt + 1) * P], w[:, 4, hp, :], start=True, stop=True)
                    ins.then_inc(v_done[par], 1)

                def scores(b, hp, i, par):
                    _, _, li, lp = near(b, hp - 1)
                    pe.wait_ge(r_made[par], after(i))
                    pe.wait_ge(exp_done[lp], after(li))
                    for qt in range(2):
                        for kt in range(qt + 1):
                            for x in range(2):
                                rows = slice(x * HW, (x + 1) * HW)
                                pe.matmul(pS[:, x, qt, kt * P:(kt + 1) * P], r[rows, par, 0, qt * P:(qt + 1) * P],
                                          r[rows, par, 1, kt * P:(kt + 1) * P], start=True, stop=(kt < qt))
                        for x in range(2):
                            ins = pe.matmul(pS[:, x, qt, qt * P:(qt + 1) * P], identb[:], causal[:], start=False, stop=True)
                    ins.then_inc(s_done[par], 1)

                def transposes(b, hp, i, par, x):
                    _, _, li, lp = near(b, hp - 1)
                    pe.wait_ge(p_made[par], after(i))
                    pe.wait_ge(probT_made[x][lp], after(li))
                    for j, (kt, qt) in enumerate(BLOCKS):
                        ins = pe.transpose(pPT[x][:, j, :], prob[:, par, x, qt, kt * P:(kt + 1) * P], ident[:])
                    ins.then_inc(t_done[x][par], 1)

                def products(b, hp, i, par):
                    _, _, li, lp = near(b, hp - 1)
                    pe.wait_ge(v_made[par], after(i))
                    pe.wait_ge(oT_made[lp], after(li))
                    pe.wait_ge(probT_made[0][par], after(i))
                    pe.wait_ge(probT_made[1][par], after(i))
                    for j, (kt, qt) in enumerate(BLOCKS):
                        for x in range(2):
                            ins = pe.matmul(pO[x * HW:(x + 1) * HW, 0, qt * P:(qt + 1) * P], vv[:, par, kt, x * HW:(x + 1) * HW],
                                            probT[:, x, j, :], start=(kt == 0), stop=(kt == qt), skip_group_check=True)
                    ins.then_inc(o_done[par], 1)

                def project_out(b, last=False):
                    pe.wait_ge(oT_made[1], b * 2 + 3)
                    if last:
                        pe.wait_ge(v_made[1], after(b * 2 + 1))
                    else:
                        pe.wait_ge(v_made[0], after((b + 1) * 2 + 1))
                    for qt in range(2):
                        for hp in range(HP):
                            ins = pe.matmul(pY[:, qt, :], oT[:, qt, hp, :], wo[:, hp, :], start=(hp == 0), stop=(hp == HP - 1))
                    ins.then_inc(y_done, 1)

                def step(b, hp, first, last):
                    if follows(b) and hp == 2:
                        project_out(b - 1)
                    scores(*near(b, hp))
                    if not first:
                        transposes(*near(b, hp - 1), 0)
                    if not first:
                        transposes(*near(b, hp - 1), 1)
                    if two_ahead(b, hp):
                        project_qk(*near(b, hp + 2))
                    if not last:
                        project_v(*near(b, hp + 1))
                    if not first:
                        products(*near(b, hp - 1))

                def finish(b):
                    transposes(*near(b, -1), 0)
                    transposes(*near(b, -1), 1)
                    products(*near(b, -1))
                    project_out(b - 1, last=True)

                project_qk(*near(0, 0))
                project_qk(*near(0, 1))
                project_v(*near(0, 0))
                units(pe, step, finish)

        sem.clear()


def sparse_heads(nc, stage, X, consts, shared, loads, loaded):
    ident = consts["ident"]
    xn_all, _, slots = shared
    with ExitStack() as ctx:
        def sb(name, shape, dt=F32):
            return ctx.enter_context(nc.sbuf_tensor(f"{stage}m_{name}", shape, dt))

        def bank(name):
            return ctx.enter_context(nc.psum_tensor(f"{stage}m_{name}", [P, 2, T], F32))

        sem = Sems(nc, ctx, stage + "m")
        w, wo, rope = (loads[f"mosa_{n}"][0] for n in ("w", "wo", "rope"))
        slot_no = sb("slot_no", [P, K])
        identb = sb("identb", [P, P], BF16)
        mask = sb("mask", [P, P], BF16)
        xs = sb("xs", [P, 2, P])
        pick = sb("pick", [P, 2, NH, K])
        gated = sb("gated", [P, 2, NH, K])
        xgT = sb("xgT", [P, NH * K])
        tg = sb("tg", [P, 2, 2, HW])
        r = sb("r", [P, 2, 2, HW])
        r2 = sb("r2", [P, 2, 2, HW])
        rT = sb("rT", [HW, 2, NH * K])
        vaug = sb("vaug", [P, 2, HW + 1])
        nmax = sb("nmax", [P, 2])
        prob = sb("prob", [P, 2, P])
        probT = sb("probT", [P, 2, P])
        rsum = sb("rsum", [P, 2])
        av = sb("av", [P, 2, HW])
        avT = sb("avT", [HW, 2, P])
        z = sb("z", [P, 2, P])
        gT = sb("gT", [P, 2, T])
        pG, pR, pS, pT, pO, pY = (bank(n) for n in ("pG", "pR", "pS", "pT", "pO", "pY"))
        pP = ctx.enter_context(nc.psum_tensor(f"{stage}m_pP", [P, 2, 2 * T], F32))
        projected = pP[:, :, 0:4 * HW].rearrange("p g (s w d) -> p g s w d", s=2, w=2)
        names = ("xs_made", "pick_made", "gated_made", "xg_done", "xg_made", "tg_done", "tg_made", "p_done", "r_made", "v_made", "rT_done", "rT_made",
                 "s_done", "nmax_made", "exp_done", "t_done", "probT_made", "o_done", "av_made", "avT_done", "avT_made",
                 "z_done", "z_made", "gT_done", "gT_made", "y_done", "x_done")
        made = {n: sem(n) for n in names}

        by_head = slots[:].rearrange("p k (n b) -> p k n b", b=B)

        def batches(eng, step):
            with eng.Fori(0, B - 1) as b:
                step(b, True)
            step(B - 1, False)

        with nc.Block() as block:
            @block.gpsimd
            def _(pool):
                for s in made.values():
                    pool.sem_inc(s, 1)
                c = sem("mask_made")
                pool.memset(mask[:], 0.0).then_inc(c, 1)
                pool.memset(vaug[:, :, HW:HW + 1], 1.0).then_inc(c, 1)
                pool.tensor_copy(identb[:], ident[:]).then_inc(c, 1)
                pool.iota(slot_no[:], pattern=[[1, K]], base=1, channel_multiplier=0,
                          allow_small_or_imprecise_dtypes=True).then_inc(c, 1)
                pool.wait_ge(c, 4)
                pool.affine_select(out=mask[:], in_=mask[:], compare_op=ALU.is_ge, fill=MASKED, base=0,
                                   pattern=[[-1, P]], channel_multiplier=1).then_inc(c, 1)
                pool.wait_ge(c, 5)
                pool.affine_select(out=mask[:].rearrange("p (h k) -> p h k", k=K), in_=mask[:].rearrange("p (h k) -> p h k", k=K),
                                   compare_op=ALU.is_ge, fill=MASKED, base=K - 1,
                                   pattern=[[K, P // K], [0, K]], channel_multiplier=-1).then_inc(c, 1)
                with pool.Fori(0, B) as b:
                    pool.wait_ge(made["xg_done"], before(b))
                    pool.tensor_copy(xs[:], xn_all[:, ds(b * 2, 2), :]).then_inc(made["xs_made"], 1)
                    pool.wait_ge(made["gT_done"], before(b))
                    pool.wait_ge(made["pick_made"], after(b))
                    pool.tensor_tensor(gated[:], pick[:], by_head[:, 2:4, :, ds(b, 1)].broadcast_to([P, 2, NH, K]), ALU.mult)\
                        .then_inc(made["gated_made"], 1)

            @block.vector
            def _(v):
                v.wait_ge(loaded, 48)
                v.wait_ge(sem("mask_made"), 6)
                chain = sem("rope_chain")
                ochain = sem("out_chain")

                def mark(b):
                    v.wait_ge(made["tg_done"], before(b))
                    v.wait_ge(made["xg_done"], before(b))
                    v.wait_ge(made["gated_made"], before(b))
                    v.tensor_tensor(pick[:], by_head[:, 0:2, :, ds(b, 1)].broadcast_to([P, 2, NH, K]),
                                    slot_no[:].unsqueeze(1).unsqueeze(1).broadcast_to([P, 2, NH, K]), ALU.is_equal)\
                        .then_inc(made["pick_made"], 1)

                def lift_tables(b):
                    v.wait_ge(made["tg_done"], after(b))
                    v.wait_ge(made["r_made"], before(b))
                    v.tensor_copy(tg[:].rearrange("p g a d -> p g (a d)"), pR[:, :, 0:2 * HW]).then_inc(made["tg_made"], 1)

                def rotate(b):
                    v.wait_ge(made["p_done"], after(b))
                    v.wait_ge(made["o_done"], before(b))
                    v.wait_ge(made["rT_done"], before(b))
                    v.wait_ge(made["tg_made"], after(b))
                    v.tensor_copy(vaug[:, :, 0:HW], pP[:, :, 4 * HW:5 * HW]).then_inc(made["v_made"], 1)
                    v.tensor_tensor(r[:], projected[:, :, :, 0, :], tg[:, :, 0:1, :].broadcast_to([P, 2, 2, HW]), ALU.mult).then_inc(chain, 1)
                    v.tensor_tensor(r2[:], projected[:, :, :, 1, :], tg[:, :, 1:2, :].broadcast_to([P, 2, 2, HW]), ALU.mult).then_inc(chain, 1)
                    v.wait_ge(chain, 2)
                    v.sem_clear(chain)
                    v.tensor_tensor(r[:], r[:], r2[:], ALU.add).then_inc(made["r_made"], 1)

                def step(b, more):
                    v.wait_ge(made["s_done"], after(b))
                    v.tensor_reduce(nmax[:], pS[:, :, 0:P], AX_X, ALU.max, negate=True).then_inc(made["nmax_made"], 1)
                    if more:
                        mark(b + 1)
                    v.wait_ge(made["t_done"], after(b))
                    v.tensor_copy(probT[:], pT[:, :, 0:P]).then_inc(made["probT_made"], 1)
                    v.wait_ge(made["o_done"], after(b))
                    v.reciprocal(rsum[:], pO[:, :, HW]).then_inc(ochain, 1)
                    v.wait_ge(ochain, 1)
                    v.sem_clear(ochain)
                    v.tensor_tensor(av[:], pO[:, :, 0:HW], rsum[:].unsqueeze(2).broadcast_to([P, 2, HW]), ALU.mult).then_inc(made["av_made"], 1)
                    if more:
                        lift_tables(b + 1)
                    v.wait_ge(made["avT_done"], after(b))
                    v.tensor_copy(avT[:], pT[0:HW, :, 0:P]).then_inc(made["avT_made"], 1)
                    if more:
                        rotate(b + 1)
                    v.wait_ge(made["y_done"], after(b))
                    v.tensor_tensor(X[:, ds(b * 2, 2), :], X[:, ds(b * 2, 2), :], pY[:, :, 0:P], ALU.add).then_inc(made["x_done"], 1)

                mark(0)
                lift_tables(0)
                rotate(0)
                batches(v, step)

            @block.scalar
            def _(act):
                def lift_gathered(b):
                    act.wait_ge(made["xg_done"], after(b))
                    act.wait_ge(made["p_done"], before(b))
                    act.copy(xgT[:], pG[:, 0, :]).then_inc(made["xg_made"], 1)

                def lift_rotated(b):
                    act.wait_ge(made["rT_done"], after(b))
                    act.wait_ge(made["s_done"], before(b))
                    act.activation(rT[:, 0, :], pR[0:HW, 0, :], ACT.Identity, scale=HW ** -0.5)
                    act.activation(rT[:, 1, :], pR[0:HW, 1, :], ACT.Identity).then_inc(made["rT_made"], 1)

                def lift_gated(b):
                    act.wait_ge(made["gT_done"], after(b))
                    act.wait_ge(made["y_done"], before(b))
                    act.copy(gT[:], pY[:]).then_inc(made["gT_made"], 1)

                def step(b, more):
                    act.wait_ge(made["nmax_made"], after(b))
                    for g in range(2):
                        ins = act.activation(prob[:, g, :], pS[:, g, 0:P], ACT.Exp, bias=nmax[:, g:g + 1])
                    ins.then_inc(made["exp_done"], 1)
                    if more:
                        lift_gathered(b + 1)
                    act.wait_ge(made["z_done"], after(b))
                    act.wait_ge(made["y_done"], before(b))
                    act.copy(z[:], pG[:, :, 0:P]).then_inc(made["z_made"], 1)
                    if more:
                        lift_rotated(b + 1)
                        lift_gated(b + 1)

                lift_gathered(0)
                lift_rotated(0)
                lift_gated(0)
                batches(act, step)

            @block.tensor
            def _(pe):
                pe.wait_ge(loaded, 48)
                pe.wait_ge(sem("mask_made"), 6)

                def gather_tokens(b):
                    pe.wait_ge(made["xs_made"], after(b))
                    pe.wait_ge(made["pick_made"], after(b))
                    pe.wait_ge(made["z_made"], b)
                    for kt in range(2):
                        ins = pe.matmul(pG[:, 0, :], xs[:, kt, :], pick[:, kt], start=(kt == 0), stop=(kt == 1))
                    ins.then_inc(made["xg_done"], 1)

                def gather_tables(b):
                    pe.wait_ge(made["rT_made"], before(b))
                    for g in range(2):
                        for kt in range(2):
                            ins = pe.matmul(pR[:, g, 0:2 * HW], pick[:, kt, g * 4:(g + 1) * 4].rearrange("p n k -> p (n k)"),
                                            rope[:, kt, :], start=(kt == 0), stop=(kt == 1))
                    ins.then_inc(made["tg_done"], 1)

                def transpose_gated(b):
                    pe.wait_ge(made["gated_made"], after(b))
                    pe.wait_ge(made["x_done"], before(b))
                    for g in range(2):
                        for kt in range(2):
                            ins = pe.transpose(pY[:, g, kt * P:(kt + 1) * P],
                                               gated[:, kt, g * 4:(g + 1) * 4].rearrange("p n k -> p (n k)"), ident[:])
                    ins.then_inc(made["gT_done"], 1)

                def project(b):
                    pe.wait_ge(made["xg_made"], after(b))
                    pe.wait_ge(made["r_made"], before(b))
                    pe.wait_ge(made["v_made"], before(b))
                    for n in range(NH):
                        rows = slice(n % 4 * K, n % 4 * K + K)
                        ins = pe.matmul(pP[rows, n // 4, 0:5 * HW], xgT[:, n * K:(n + 1) * K], w[:, n].rearrange("p a d -> p (a d)"),
                                        start=True, stop=True, skip_group_check=True)
                    ins.then_inc(made["p_done"], 1)

                def transpose_rotated(b):
                    pe.wait_ge(made["r_made"], after(b))
                    pe.wait_ge(made["tg_made"], after(b))
                    pe.sem_inc(sem("waited_pe"), 1)
                    for a in range(2):
                        for g in range(2):
                            ins = pe.transpose(pR[0:HW, a, g * P:(g + 1) * P], r[:, g, a, :], ident[:])
                    ins.then_inc(made["rT_done"], 1)

                def step(b, more):
                    pe.wait_ge(made["rT_made"], after(b))
                    pe.wait_ge(made["exp_done"], before(b))
                    for g in range(2):
                        cols = slice(g * P, (g + 1) * P)
                        pe.matmul(pS[:, g, 0:P], rT[:, 0, cols], rT[:, 1, cols], start=True, stop=False)
                        ins = pe.matmul(pS[:, g, 0:P], identb[:], mask[:], start=False, stop=True)
                    ins.then_inc(made["s_done"], 1)
                    pe.wait_ge(made["exp_done"], after(b))
                    pe.wait_ge(made["avT_made"], before(b))
                    for g in range(2):
                        ins = pe.transpose(pT[:, g, 0:P], prob[:, g, :], ident[:])
                    ins.then_inc(made["t_done"], 1)
                    if more:
                        gather_tokens(b + 1)
                        gather_tables(b + 1)
                    pe.wait_ge(made["probT_made"], after(b))
                    pe.wait_ge(made["v_made"], after(b))
                    pe.wait_ge(made["av_made"], before(b))
                    for g in range(2):
                        ins = pe.matmul(pO[:, g, 0:HW + 1], probT[:, g, :], vaug[:, g, :], start=True, stop=True)
                    ins.then_inc(made["o_done"], 1)
                    if more:
                        project(b + 1)
                    pe.wait_ge(made["av_made"], after(b))
                    pe.sem_inc(sem("waited_pe"), 1)
                    for g in range(2):
                        ins = pe.transpose(pT[0:HW, g, 0:P], av[:, g, :], ident[:])
                    ins.then_inc(made["avT_done"], 1)
                    pe.wait_ge(made["avT_made"], after(b))
                    pe.sem_inc(sem("waited_pe"), 1)
                    for n in range(NH):
                        rows = slice(n % 4 * K, n % 4 * K + K)
                        ins = pe.matmul(pG[rows, n // 4, 0:P], avT[:, n // 4, rows], wo[:, n, :], start=True, stop=True,
                                        skip_group_check=True)
                    ins.then_inc(made["z_done"], 1)
                    pe.wait_ge(made["z_made"], after(b))
                    pe.wait_ge(made["gT_made"], after(b))
                    for qt in range(2):
                        for g in range(2):
                            ins = pe.matmul(pY[:, qt, 0:P], gT[:, g, qt * P:(qt + 1) * P], z[:, g, :], start=(g == 0), stop=(g == 1))
                    ins.then_inc(made["y_done"], 1)
                    if more:
                        transpose_rotated(b + 1)
                        transpose_gated(b + 1)

                gather_tokens(0)
                gather_tables(0)
                project(0)
                transpose_rotated(0)
                transpose_gated(0)
                batches(pe, step)

        sem.clear()


def mixed_attention(nc, stage, X, consts, drams):
    with ExitStack() as ctx:
        shared = (
            ctx.enter_context(nc.sbuf_tensor("xn_all", [P, TILES, P], F32)),
            ctx.enter_context(nc.sbuf_tensor("xnT_all", [P, B * T], F32)),
            ctx.enter_context(nc.sbuf_tensor("slots", [P, 4, NH * B], F32)),
        )
        loads = {name: (ctx.enter_context(nc.sbuf_tensor(f"{stage}_{name}", shape, F32)), drams[name]) for name, shape in (
            ("dense_w", [P, 5, NH // 2, P]),
            ("dense_wo", [P, NH // 2, P]),
            ("dense_rope", [P, 4, T]),
            ("mosa_w", [P, NH, 5, HW]),
            ("mosa_wo", [HW, NH, P]),
            ("mosa_rope", [P, 2, 2 * HW]),
        )}
        loaded = {kind: ctx.enter_context(nc.semaphore(f"{stage}_{kind}_loaded")) for kind in ("dense", "mosa")}
        route_tokens(nc, stage, X, consts, shared, drams, loads, loaded)
        dense_heads(nc, stage, X, consts, shared, loads, loaded["dense"])
        sparse_heads(nc, stage, X, consts, shared, loads, loaded["mosa"])


def build(nc, ins, out, stages=(1, 2, 3, 4, 5, 6)):
    with ExitStack() as ctx:
        def sb(name, shape, dt=F32):
            return ctx.enter_context(nc.sbuf_tensor(name, shape, dt))

        X = sb("X", [P, TILES, P])
        ident = sb("ident", [P, P])
        ones = sb("ones", [P, P])
        stack_ctx = ExitStack()
        qs = stack_ctx.enter_context(nc.sbuf_tensor("qs", [P, UNITS, T], BF16))
        ks = stack_ctx.enter_context(nc.sbuf_tensor("ks", [P, UNITS, T], BF16))
        zeros_ctx = ExitStack()
        zeros = zeros_ctx.enter_context(nc.sbuf_tensor("zeros", [P, H * T // 2], BF16))
        loaded, made, zeroed, *stacked = (ctx.enter_context(nc.semaphore(n)) for n in (
            "loaded", "consts_made", "zeroed", "stacked_half0", "stacked_half1"))
        consts = {"ident": ident, "ones": ones, "qs": qs, "ks": ks, "zeroed": zeroed, "zeroed_by": 16 * 2, "stacked": stacked}
        with nc.Block() as block:
            @block.sync
            def _(sp):
                sp.dma_start(X[:], ins["x"].rearrange("(t p) d -> p t d", p=P)).then_inc(loaded, 16)
                sp.wait_ge(made, 1)
                for stack in (qs, ks):
                    zero_rows = zeros[DH * len(TERMS):KROWS, :].unsqueeze(1).broadcast_to([KROWS - DH * len(TERMS), 2 * B, H * T // 2])
                    sp.dma_start(stack[DH * len(TERMS):KROWS, 0:UNITS, :].rearrange("p (b h) n -> p b (h n)", h=H // 2),
                                 zero_rows).then_inc(zeroed, 16)
                sp.wait_ge(loaded, 16)
                if 1 not in stages:
                    sp.wait_ge(zeroed, consts["zeroed_by"])

            @block.gpsimd
            def _(pool):
                pool.memset(zeros[:].bitcast(F32), 0.0).then_inc(made, 1)
                pool.memset(ident[:], 0.0).then_inc(made, 1)
                pool.memset(ones[:], 1.0).then_inc(made, 1)
                pool.wait_ge(made, 3)
                pool.affine_select(out=ident[:], in_=ident[:], compare_op=ALU.not_equal, fill=1.0, base=0,
                                   pattern=[[-1, P]], channel_multiplier=1).then_inc(made, 1)

        if 1 in stages:
            head_attention(nc, "s1", X, None, consts, (ins["w1"], None, None, ins["rope1"]), False, 0)
        zeros_ctx.close()
        if 2 in stages:
            head_attention(nc, "s2", X, ins["ctxT"], consts, (ins["w2"], ins["b2"], ins["bo2"], ins["rope2"]), False,
                           sum(n in stages for n in (1,)))
        if 3 in stages:
            tree_ffn(nc, "s3", X, consts, (ins["win"], ins["bin"], ins["wout"]))
        if 4 in stages:
            head_attention(nc, "s4", X, None, consts, (ins["w4"], ins["b4"], ins["bo4"], None), True,
                           sum(n in stages for n in (1, 2)))
        stack_ctx.close()
        if 5 in stages:
            entangled_attention(nc, "s5", X, ins["ctxT"], consts, (ins["w5"], ins["b5"], ins["bv5"]))
        if 6 in stages:
            mixed_attention(nc, "s6", X, consts, {k: ins[k] for k in (
                "router", "dense_w", "dense_wo", "dense_rope", "mosa_w", "mosa_wo", "mosa_rope")})

        stored = ctx.enter_context(nc.semaphore("stored"))
        with nc.Block() as block:
            @block.sync
            def _(sp):
                sp.dma_start(out.rearrange("(t p) d -> p t d", p=P), X[:]).then_inc(stored, 16)
                sp.wait_ge(stored, 16)


def swap_pairs(w):
    return w.reshape(w.shape[0], -1, 2)[:, :, ::-1].reshape(w.shape)


def swap_halves(w, d):
    return w.reshape(w.shape[0], -1, 2, d // 2)[:, :, ::-1].reshape(w.shape)


def by_width(w):
    return w.reshape(w.shape[:-1] + (H, DH)).swapaxes(-1, -2).reshape(w.shape)


def rope_tables(angles, signs):
    cos = np.cos(angles).astype(np.float32)
    sin = (np.sin(angles) * signs).astype(np.float32)
    scale = np.float32(DH ** -0.5)
    return by_width(np.stack([cos * scale, cos, sin * scale, sin], axis=0)).transpose(2, 0, 1)


def lay_out(x):
    f = np.float32
    a = {k: np.asarray(v) for k, v in x.items()}
    o = {"x": a["x"].reshape(B * T, P), "ctxT": a["ctx_1024"].reshape(B * T, P).T}
    pos = np.arange(T, dtype=f)[:, None]
    f1 = np.exp(-np.float32(np.log(10000.0)) * np.arange(0, DH, 2, dtype=f) / DH).astype(f)
    ang1 = np.tile(np.repeat((pos * f1).astype(f), 2, axis=1), (1, H))
    o["rope1"] = rope_tables(ang1, np.tile([-1, 1], P // 2).astype(f))
    f2 = (1.0 / 10000.0 ** (np.arange(0, DH, 2, dtype=f) / DH)).astype(f)
    ang2 = np.tile((pos * np.concatenate([f2, f2])).astype(f), (1, H))
    o["rope2"] = rope_tables(ang2, np.tile(np.repeat([-1, 1], DH // 2), H).astype(f))

    def weights(q, k, v, out, swap):
        return np.stack([by_width(q.T), by_width(swap(q.T)), by_width(k.T), by_width(swap(k.T)), v.T, out.T], axis=1)

    def rows(q, k, v, swap):
        return np.stack([by_width(q), by_width(swap(q[None])[0]), by_width(k), by_width(swap(k[None])[0]), v], axis=1)

    def per_head(w):
        return np.repeat(w.reshape((4, DH) + w.shape[1:]), 4, axis=0).reshape((P,) + w.shape[1:])

    halves = lambda w: swap_halves(w, DH)
    o["w1"] = weights(a["L0_attn_W_q"], a["L0_attn_W_k"], a["L0_attn_W_v"], a["L0_attn_W_o"], swap_pairs)
    o["w2"] = weights(a["L0_xattn_Wq"], per_head(a["L0_xattn_Wk"]), per_head(a["L0_xattn_Wv"]), a["L0_xattn_Wo"], halves)
    o["b2"] = rows(a["L0_xattn_bq"], per_head(a["L0_xattn_bk"]), per_head(a["L0_xattn_bv"]), halves)
    o["bo2"] = a["L0_xattn_bo"][None]
    node = [2 ** d - 1 + sum(((pos >> k) & 1) << (d - 1 - k) for k in range(d)) for d in range(DEPTH + 1) for pos in range(2 ** d)]
    order = (np.arange(TREES)[None, :] * NODES + np.array(node)[:, None]).reshape(-1)
    o["win"] = a["L0_ffn_W_in"][order].T
    o["bin"] = a["L0_ffn_b_in"][order][None]
    o["wout"] = a["L0_ffn_W_out"][:, order].T
    o["w4"] = weights(a["L1_attn_Wq"], a["L1_attn_Wk"], a["L1_attn_Wv"], a["L1_attn_Wo"], halves)
    o["b4"] = rows(a["L1_attn_bq"], a["L1_attn_bk"], a["L1_attn_bv"], halves)
    o["bo4"] = a["L1_attn_bo"][None]
    we = a["L1_xattn_We"]
    o["w5"] = np.stack([a["L1_xattn_Wq"].T, a["L1_xattn_Wk"].T, a["L1_xattn_Wv"].T, we[:, :P].T, we[:, P:].T], axis=1)
    o["b5"] = np.stack([a["L1_xattn_bq"], a["L1_xattn_bk"], a["L1_xattn_bv"], a["L1_xattn_be"]], axis=1)
    o["bv5"] = a["L1_xattn_bv"][None]

    ROT = 32

    def swap_rot(w):
        return np.concatenate([w[..., ROT // 2:ROT], w[..., :ROT // 2], w[..., ROT:]], axis=-1)

    inv = (np.float32(10000.0) ** (-np.arange(ROT // 2, dtype=f) / np.float32(ROT // 2))).astype(f)
    ang = (pos * inv).astype(f)
    cos = np.concatenate([np.cos(ang), np.cos(ang), np.ones((T, HW - ROT), f)], axis=1).astype(f)
    sin = np.concatenate([-np.sin(ang), np.sin(ang), np.zeros((T, HW - ROT), f)], axis=1).astype(f)
    o["router"] = a["L1_ffn_mosa_router_w"]
    d = a["L1_ffn_dense_wqkv"]
    q, k, v = d[..., :HW], d[..., HW:2 * HW], d[..., 2 * HW:]
    o["dense_w"] = np.stack([q, swap_rot(q), k, swap_rot(k), v], axis=1).reshape(P, 5, NH // 2, P)
    o["dense_wo"] = a["L1_ffn_dense_wo"].reshape(NH // 2, P, P).transpose(1, 0, 2)
    eighth = np.float32(HW ** -0.5)
    o["dense_rope"] = np.tile(np.stack([cos * eighth, cos, sin * eighth, sin]).transpose(2, 0, 1), (2, 1, 1))
    m = a["L1_ffn_mosa_wqkv"]
    q, k, v = m[..., :HW], m[..., HW:2 * HW], m[..., 2 * HW:]
    o["mosa_w"] = np.stack([q, swap_rot(q), k, swap_rot(k), v], axis=2)
    o["mosa_wo"] = a["L1_ffn_mosa_wo"].reshape(NH, HW, P).transpose(1, 0, 2)
    o["mosa_rope"] = np.concatenate([cos, sin], axis=1).reshape(2, P, 2 * HW).transpose(1, 0, 2)
    return {k: np.ascontiguousarray(v) for k, v in o.items()}


def kernel(**inputs):
    import concourse.bacc as bacc
    from concourse.bass_utils import run_bass_kernel_spmd

    arrays = lay_out(inputs)
    nc = bacc.Bacc("TRN2", target_bir_lowering=False, num_devices=1)
    ins = {k: nc.dram_tensor(f"in_{k}", v.shape, mybir.dt.from_np(v.dtype), kind="ExternalInput").ap()
           for k, v in arrays.items()}
    out = nc.dram_tensor("out_0", (B * T, P), F32, kind="ExternalOutput").ap()
    build(nc, ins, out)
    r = run_bass_kernel_spmd(nc, [{f"in_{k}": v for k, v in arrays.items()}], core_ids=[0])
    return r.results[0]["out_0"].reshape(B, T, P)
```
